# Optimizing a Trainium2 kernel written in Bass

```python
import numpy as np
import jax
import jax.numpy as jnp

def _softmax(x, axis=-1):
    return jax.nn.softmax(x, axis=axis)

def _gelu(x):
    return jax.nn.gelu(x, approximate=True)

def _silu(x):
    return jax.nn.silu(x)

def _sigmoid(x):
    return jax.nn.sigmoid(x)

def _layernorm(x, axis=-1, eps=1e-05):
    m = jnp.mean(x, axis=axis, keepdims=True)
    v = jnp.var(x, axis=axis, keepdims=True)
    return (x - m) / jnp.sqrt(v + eps)

def _scatter_add(tgt, idx, src, axis=0):
    return tgt.at[idx].add(src)

def _segment_sum(src, seg, n):
    return jax.ops.segment_sum(src, seg, n)
kernel_name = 'mk_xattn_ffn_d4_seqx_r8_befb22'

def setup_inputs(seed: int=0):
    np.random.seed(seed)
    _w = jnp.asarray

    def _rec_inputs():
        import jax
        import jax.numpy as jnp
        _rk = jax.random.key(seed)
        x = -0.0003929 + 0.9999 * jax.random.normal(jax.random.fold_in(_rk, 1), (32, 128, 128), jnp.float32)
        _lenS = 128 - jax.random.randint(jax.random.fold_in(_rk, 7), (32,), 0, max(1, 128 // 4) + 1, jnp.int32)
        _lenS2 = 77 - jax.random.randint(jax.random.fold_in(_rk, 8), (32,), 0, max(1, 77 // 4) + 1, jnp.int32)
        _ctx_768P = jax.random.normal(jax.random.fold_in(_rk, 11), (32, 16, 96), jnp.float32)
        _ctx_768c = jax.random.dirichlet(jax.random.fold_in(_rk, 511), 0.3 * jnp.ones((16,), jnp.float32), (32, 77))
        _ctx_768t = jnp.einsum('bsk,bkd->bsd', _ctx_768c, _ctx_768P)
        _ctx_768t = _ctx_768t * jax.lax.rsqrt(jnp.mean(jnp.square(_ctx_768t)) + 1e-12) * 0.953939
        ctx_768 = 2.09791e-05 + 1.00001 * (_ctx_768t + 0.3 * jax.random.normal(jax.random.fold_in(_rk, 611), (32, 77, 96), jnp.float32))
        _validS = jnp.arange(128)[None, :] < _lenS[:, None]
        _validS2 = jnp.arange(77)[None, :] < _lenS2[:, None]
        _causal = jnp.tril(jnp.ones((128, 128), dtype=bool))
        mask_BxS2_bk0 = jnp.logical_not(jnp.broadcast_to(_validS2[:, :], (32, 77)))
        return (x, ctx_768, mask_BxS2_bk0)
    x, ctx_768, mask_BxS2_bk0 = _rec_inputs()

    def _L0_xattn_setup():
        import jax, jax.numpy as jnp
        import numpy as np
        HEADS = 8
        DIM_HEAD = 64
        QUERY_DIM = 128
        CONTEXT_DIM = 96
        INNER = HEADS * DIM_HEAD
        key = jax.random.key(seed)
        ks = jax.random.split(key, 7)
        B, Sq, Skv = (4, 512, 128)
        x = jax.random.normal(ks[0], (B, Sq, QUERY_DIM), dtype=jnp.float32)
        context = jax.random.normal(ks[1], (B, Skv, CONTEXT_DIM), dtype=jnp.float32)
        Wq = jax.random.normal(ks[2], (QUERY_DIM, INNER), dtype=jnp.float32) * QUERY_DIM ** (-0.5)
        Wk = jax.random.normal(ks[3], (CONTEXT_DIM, INNER), dtype=jnp.float32) * CONTEXT_DIM ** (-0.5)
        Wv = jax.random.normal(ks[4], (CONTEXT_DIM, INNER), dtype=jnp.float32) * CONTEXT_DIM ** (-0.5)
        Wo = jax.random.normal(ks[5], (INNER, QUERY_DIM), dtype=jnp.float32) * INNER ** (-0.5)
        bo = jax.random.normal(ks[6], (QUERY_DIM,), dtype=jnp.float32) * 0.01
        return {'x': x, 'context': context, 'Wq': Wq, 'Wk': Wk, 'Wv': Wv, 'Wo': Wo, 'bo': bo}
    _L0_xattn_all = _L0_xattn_setup()
    _L0_xattn_in = {k: v for k, v in _L0_xattn_all.items() if k in ('Wq', 'Wk', 'Wv', 'Wo', 'bo')}
    del _L0_xattn_all

    def _L0_ffn_setup():
        import jax, jax.numpy as jnp
        import numpy as np
        E = 8
        K = 2
        CAP_FACTOR = 1.0
        key = jax.random.key(seed)
        k0, k1, k2, k3 = jax.random.split(key, 4)
        B, S, M, H = (4, 256, 128, 512)
        x = jax.random.normal(k0, (B, S, M), jnp.float32)
        wg = jax.random.normal(k1, (M, E), jnp.float32) * 0.02
        w1 = jax.random.normal(k2, (E, M, H), jnp.float32) * 0.02
        b1 = jnp.zeros((E, H), jnp.float32)
        w2 = jax.random.normal(k3, (E, H, M), jnp.float32) * 0.02
        b2 = jnp.zeros((E, M), jnp.float32)
        return {'x': x, 'wg': wg, 'w1': w1, 'b1': b1, 'w2': w2, 'b2': b2}
    _L0_ffn_all = _L0_ffn_setup()
    _L0_ffn_in = {k: v for k, v in _L0_ffn_all.items() if k in ('wg', 'w1', 'b1', 'w2', 'b2')}
    del _L0_ffn_all

    def _L1_xattn_setup():
        import jax, jax.numpy as jnp
        import numpy as np
        HEADS = 16
        DIM_HEAD = 64
        SCALE = DIM_HEAD ** (-0.5)
        QUERY_DIM = 128
        CONTEXT_DIM = 96
        INNER_DIM = HEADS * DIM_HEAD
        key = jax.random.key(seed)
        ks = jax.random.split(key, 7)
        B, Nq, Nk = (8, 512, 77)
        x = jax.random.normal(ks[0], (B, Nq, QUERY_DIM), dtype=jnp.float32)
        context = jax.random.normal(ks[1], (B, Nk, CONTEXT_DIM), dtype=jnp.float32)
        Wq = jax.random.normal(ks[2], (QUERY_DIM, INNER_DIM), dtype=jnp.float32) * QUERY_DIM ** (-0.5)
        Wk = jax.random.normal(ks[3], (CONTEXT_DIM, INNER_DIM), dtype=jnp.float32) * CONTEXT_DIM ** (-0.5)
        Wv = jax.random.normal(ks[4], (CONTEXT_DIM, INNER_DIM), dtype=jnp.float32) * CONTEXT_DIM ** (-0.5)
        Wo = jax.random.normal(ks[5], (INNER_DIM, QUERY_DIM), dtype=jnp.float32) * INNER_DIM ** (-0.5)
        bo = jnp.zeros((QUERY_DIM,), dtype=jnp.float32)
        return {'x': x, 'context': context, 'Wq': Wq, 'Wk': Wk, 'Wv': Wv, 'Wo': Wo, 'bo': bo}
    _L1_xattn_all = _L1_xattn_setup()
    _L1_xattn_in = {k: v for k, v in _L1_xattn_all.items() if k in ('Wq', 'Wk', 'Wv', 'Wo', 'bo')}
    del _L1_xattn_all

    def _L1_ffn_setup():
        import jax, jax.numpy as jnp
        import numpy as np
        D, H, E, K = (128, 128, 8, 2)

        def _moe(x, router_w, w_in, b_in, w_out, b_out):
            B, S, Dm = x.shape
            T = B * S
            x2 = x.reshape(T, Dm)
            logits = x2 @ router_w
            probs = jax.nn.softmax(logits, axis=-1)
            top_p, top_e = jax.lax.top_k(probs, K)
            flat_e = top_e.reshape(-1)
            flat_p = top_p.reshape(-1)
            tok = jnp.repeat(jnp.arange(T), K)
            order = jnp.argsort(flat_e)
            se, sp, st = (flat_e[order], flat_p[order], tok[order])
            xd = x2[st]
            N = xd.shape[0]
            h = jnp.zeros((N, H), x.dtype)
            for e in range(E):
                m = (se == e)[:, None]
                h = h + jnp.where(m, jax.nn.gelu(xd @ w_in[e] + b_in[e]), 0.0)
            y = jnp.zeros((N, Dm), x.dtype)
            for e in range(E):
                m = (se == e)[:, None]
                y = y + jnp.where(m, h @ w_out[e] + b_out[e], 0.0)
            y = y * sp[:, None]
            out = jnp.zeros((T, Dm), x.dtype).at[st].add(y)
            return out.reshape(B, S, Dm)
        key = jax.random.key(seed)
        ks = jax.random.split(key, 5)
        s = lambda k, shape, scale: jax.random.normal(k, shape, dtype=jnp.float32) * scale
        return {'input_batch': s(ks[0], (2, 64, D), 1.0), 'router_w': s(ks[1], (D, E), D ** (-0.5)), 'w_in': s(ks[2], (E, D, H), D ** (-0.5)), 'b_in': jnp.zeros((E, H), jnp.float32), 'w_out': s(ks[3], (E, H, D), H ** (-0.5)), 'b_out': jnp.zeros((E, D), jnp.float32)}
    _L1_ffn_all = _L1_ffn_setup()
    _L1_ffn_in = {k: v for k, v in _L1_ffn_all.items() if k in ('router_w', 'w_in', 'b_in', 'w_out', 'b_out')}
    del _L1_ffn_all

    def _L2_xattn_setup():
        import jax, jax.numpy as jnp
        import numpy as np
        IMG_DIM, TXT_DIM, HID = (128, 96, 128)
        B, LQ, LK = (8, 256, 256)
        key = jax.random.key(seed)
        ks = jax.random.split(key, 8)
        s_img = 1.0 / np.sqrt(IMG_DIM)
        s_txt = 1.0 / np.sqrt(TXT_DIM)
        return {'image_features': jax.random.normal(ks[0], (B, LQ, IMG_DIM), jnp.float32), 'text_features': jax.random.normal(ks[1], (B, LK, TXT_DIM), jnp.float32), 'Wq': jax.random.uniform(ks[2], (IMG_DIM, HID), jnp.float32, -s_img, s_img), 'bq': jax.random.uniform(ks[3], (HID,), jnp.float32, -s_img, s_img), 'Wk': jax.random.uniform(ks[4], (TXT_DIM, HID), jnp.float32, -s_txt, s_txt), 'bk': jax.random.uniform(ks[5], (HID,), jnp.float32, -s_txt, s_txt), 'Wv': jax.random.uniform(ks[6], (TXT_DIM, HID), jnp.float32, -s_txt, s_txt), 'bv': jax.random.uniform(ks[7], (HID,), jnp.float32, -s_txt, s_txt)}
    _L2_xattn_all = _L2_xattn_setup()
    _L2_xattn_in = {k: v for k, v in _L2_xattn_all.items() if k in ('Wq', 'bq', 'Wk', 'bk', 'Wv', 'bv')}
    del _L2_xattn_all

    def _L2_ffn_setup():
        import jax, jax.numpy as jnp
        import numpy as np
        B, S, DIM, FFN, E = (4, 256, 128, 512, 8)
        key = jax.random.key(seed)
        k0, k1, k2, k3 = jax.random.split(key, 4)
        scale = 0.02
        return {'hidden_states': jax.random.normal(k0, (B, S, DIM), jnp.float32), 'router_w': jax.random.normal(k1, (DIM, E), jnp.float32) * scale, 'router_b': jnp.zeros((E,), jnp.float32), 'w1': jax.random.normal(k2, (E, DIM, 2 * FFN), jnp.float32) * scale, 'w2': jax.random.normal(k3, (E, FFN, DIM), jnp.float32) * scale}
    _L2_ffn_all = _L2_ffn_setup()
    _L2_ffn_in = {k: v for k, v in _L2_ffn_all.items() if k in ('router_w', 'router_b', 'w1', 'w2')}
    del _L2_ffn_all

    def _L3_xattn_setup():
        import jax, jax.numpy as jnp
        import numpy as np
        DIM_IN, DIM_LAT, DIM_HEAD = (96, 128, 64)
        INNER = max(DIM_LAT, DIM_IN)
        HEADS = INNER // DIM_HEAD
        SCALE = DIM_HEAD ** (-0.5)
        RMS_EPS = 1e-08
        LN_EPS = 1e-05

        def layernorm(x, g, b):
            mu = jnp.mean(x, axis=-1, keepdims=True)
            var = jnp.mean((x - mu) ** 2, axis=-1, keepdims=True)
            return (x - mu) * jax.lax.rsqrt(var + LN_EPS) * g + b

        def rmsnorm(x, gamma):
            norm = jnp.sqrt(jnp.sum(x * x, axis=-1, keepdims=True)) * x.shape[-1] ** (-0.5)
            return x / jnp.maximum(norm, RMS_EPS) * gamma
        key = jax.random.key(seed)
        ks = jax.random.split(key, 12)
        b, n, m = (4, 512, 64)
        x = jax.random.normal(ks[0], (b, n, DIM_IN), jnp.float32)
        latents = jax.random.normal(ks[1], (b, m, DIM_LAT), jnp.float32)
        mask = jax.random.randint(ks[2], (b, n), 0, 2).astype(bool)
        s = lambda k, sh, fan: jax.random.normal(k, sh, jnp.float32) * fan ** (-0.5)
        return {'x': x, 'latents': latents, 'mask': mask, 'ln_x_g': jnp.ones((DIM_IN,), jnp.float32), 'ln_x_b': jnp.zeros((DIM_IN,), jnp.float32), 'ln_l_g': jnp.ones((DIM_LAT,), jnp.float32), 'ln_l_b': jnp.zeros((DIM_LAT,), jnp.float32), 'qn_g': jnp.ones((DIM_HEAD,), jnp.float32), 'kn_g': jnp.ones((DIM_HEAD,), jnp.float32), 'Wq': s(ks[3], (INNER, DIM_LAT), DIM_LAT), 'Wkv': s(ks[4], (2 * INNER, DIM_IN), DIM_IN), 'Wlkv': s(ks[5], (2 * INNER, DIM_LAT), DIM_LAT), 'Wo': s(ks[6], (DIM_LAT, INNER), INNER), 'bo': jnp.zeros((DIM_LAT,), jnp.float32)}
    _L3_xattn_all = _L3_xattn_setup()
    _L3_xattn_in = {k: v for k, v in _L3_xattn_all.items() if k in ('ln_x_g', 'ln_x_b', 'ln_l_g', 'ln_l_b', 'qn_g', 'kn_g', 'Wq', 'Wkv', 'Wlkv', 'Wo', 'bo')}
    del _L3_xattn_all

    def _L3_ffn_setup():
        import jax, jax.numpy as jnp
        import numpy as np
        DIM = 128
        HIDDEN = 384
        SCALE = 1.0 / 127.0

        def _dequant(w_int, dtype):
            return w_int.astype(dtype) * jnp.asarray(SCALE, dtype)
        key = jax.random.key(seed)
        k_x, k_g, k_u, k_d = jax.random.split(key, 4)
        x = jax.random.normal(k_x, (4, 256, DIM), dtype=jnp.float32)
        w_gate = jax.random.randint(k_g, (HIDDEN, DIM), -127, 128, dtype=jnp.int32)
        w_up = jax.random.randint(k_u, (HIDDEN, DIM), -127, 128, dtype=jnp.int32)
        w_down = jax.random.randint(k_d, (DIM, HIDDEN), -127, 128, dtype=jnp.int32)
        return {'x': x, 'w_gate': w_gate, 'w_up': w_up, 'w_down': w_down}
    _L3_ffn_all = _L3_ffn_setup()
    _L3_ffn_in = {k: v for k, v in _L3_ffn_all.items() if k in ('w_gate', 'w_up', 'w_down')}
    del _L3_ffn_all
    return {'x': x, 'ctx_768': ctx_768, 'mask_BxS2_bk0': mask_BxS2_bk0, 'L0_xattn_Wq': _L0_xattn_in['Wq'], 'L0_xattn_Wk': _L0_xattn_in['Wk'], 'L0_xattn_Wv': _L0_xattn_in['Wv'], 'L0_xattn_Wo': _L0_xattn_in['Wo'], 'L0_xattn_bo': _L0_xattn_in['bo'], 'L0_ffn_wg': _L0_ffn_in['wg'], 'L0_ffn_w1': _L0_ffn_in['w1'], 'L0_ffn_b1': _L0_ffn_in['b1'], 'L0_ffn_w2': _L0_ffn_in['w2'], 'L0_ffn_b2': _L0_ffn_in['b2'], 'L1_xattn_Wq': _L1_xattn_in['Wq'], 'L1_xattn_Wk': _L1_xattn_in['Wk'], 'L1_xattn_Wv': _L1_xattn_in['Wv'], 'L1_xattn_Wo': _L1_xattn_in['Wo'], 'L1_xattn_bo': _L1_xattn_in['bo'], 'L1_ffn_router_w': _L1_ffn_in['router_w'], 'L1_ffn_w_in': _L1_ffn_in['w_in'], 'L1_ffn_b_in': _L1_ffn_in['b_in'], 'L1_ffn_w_out': _L1_ffn_in['w_out'], 'L1_ffn_b_out': _L1_ffn_in['b_out'], 'L2_xattn_Wq': _L2_xattn_in['Wq'], 'L2_xattn_bq': _L2_xattn_in['bq'], 'L2_xattn_Wk': _L2_xattn_in['Wk'], 'L2_xattn_bk': _L2_xattn_in['bk'], 'L2_xattn_Wv': _L2_xattn_in['Wv'], 'L2_xattn_bv': _L2_xattn_in['bv'], 'L2_ffn_router_w': _L2_ffn_in['router_w'], 'L2_ffn_router_b': _L2_ffn_in['router_b'], 'L2_ffn_w1': _L2_ffn_in['w1'], 'L2_ffn_w2': _L2_ffn_in['w2'], 'L3_xattn_ln_x_g': _L3_xattn_in['ln_x_g'], 'L3_xattn_ln_x_b': _L3_xattn_in['ln_x_b'], 'L3_xattn_ln_l_g': _L3_xattn_in['ln_l_g'], 'L3_xattn_ln_l_b': _L3_xattn_in['ln_l_b'], 'L3_xattn_qn_g': _L3_xattn_in['qn_g'], 'L3_xattn_kn_g': _L3_xattn_in['kn_g'], 'L3_xattn_Wq': _L3_xattn_in['Wq'], 'L3_xattn_Wkv': _L3_xattn_in['Wkv'], 'L3_xattn_Wlkv': _L3_xattn_in['Wlkv'], 'L3_xattn_Wo': _L3_xattn_in['Wo'], 'L3_xattn_bo': _L3_xattn_in['bo'], 'L3_ffn_w_gate': _L3_ffn_in['w_gate'], 'L3_ffn_w_up': _L3_ffn_in['w_up'], 'L3_ffn_w_down': _L3_ffn_in['w_down']}

def reference(x, ctx_768, mask_BxS2_bk0, L0_xattn_Wq, L0_xattn_Wk, L0_xattn_Wv, L0_xattn_Wo, L0_xattn_bo, L0_ffn_wg, L0_ffn_w1, L0_ffn_b1, L0_ffn_w2, L0_ffn_b2, L1_xattn_Wq, L1_xattn_Wk, L1_xattn_Wv, L1_xattn_Wo, L1_xattn_bo, L1_ffn_router_w, L1_ffn_w_in, L1_ffn_b_in, L1_ffn_w_out, L1_ffn_b_out, L2_xattn_Wq, L2_xattn_bq, L2_xattn_Wk, L2_xattn_bk, L2_xattn_Wv, L2_xattn_bv, L2_ffn_router_w, L2_ffn_router_b, L2_ffn_w1, L2_ffn_w2, L3_xattn_ln_x_g, L3_xattn_ln_x_b, L3_xattn_ln_l_g, L3_xattn_ln_l_b, L3_xattn_qn_g, L3_xattn_kn_g, L3_xattn_Wq, L3_xattn_Wkv, L3_xattn_Wlkv, L3_xattn_Wo, L3_xattn_bo, L3_ffn_w_gate, L3_ffn_w_up, L3_ffn_w_down):
    import jax
    import jax.numpy as jnp

    def _L0_xattn_ref(x, context, Wq, Wk, Wv, Wo, bo):
        import jax, jax.numpy as jnp
        import numpy as np
        HEADS = 8
        DIM_HEAD = 64
        QUERY_DIM = 128
        CONTEXT_DIM = 96
        INNER = HEADS * DIM_HEAD
        B, Sq, _ = x.shape
        h, d = (HEADS, DIM_HEAD)
        scale = d ** (-0.5)
        q = (x @ Wq).reshape(B, Sq, h, d).transpose(0, 2, 1, 3)
        k = (context @ Wk).reshape(B, -1, h, d).transpose(0, 2, 1, 3)
        v = (context @ Wv).reshape(B, -1, h, d).transpose(0, 2, 1, 3)
        scores = jnp.einsum('bhid,bhjd->bhij', q, k) * scale
        attn = jax.nn.softmax(scores, axis=-1)
        out = jnp.einsum('bhij,bhjd->bhid', attn, v)
        out = out.transpose(0, 2, 1, 3).reshape(B, Sq, h * d)
        return out @ Wo + bo

    def _L0_ffn_ref(x, wg, w1, b1, w2, b2):
        import jax, jax.numpy as jnp
        import numpy as np
        E = 8
        K = 2
        CAP_FACTOR = 1.0
        B, S, M = x.shape
        N = B * S
        capacity = int(CAP_FACTOR * K * N // E)
        xt = x.reshape(N, M)
        logits = xt @ wg
        scores = jax.nn.softmax(logits, axis=-1)
        topv, topi = jax.lax.top_k(scores, K)
        topv = topv / jnp.sum(topv, axis=-1, keepdims=True)
        masks = jax.nn.one_hot(topi.T, E, dtype=jnp.int32)
        flat = masks.reshape(K * N, E)
        locs = jnp.cumsum(flat, axis=0) - 1
        pos = jnp.sum(locs * flat, axis=-1).reshape(K, N).T
        valid = pos < capacity
        gate = topv * valid.astype(topv.dtype)
        pos_c = jnp.where(valid, pos, 0)
        xk = xt[:, None, :] * valid[..., None].astype(xt.dtype)
        disp = jnp.zeros((E, capacity, M), xt.dtype)
        disp = disp.at[topi, pos_c].add(xk)
        h = jax.nn.relu(jnp.einsum('ecm,emh->ech', disp, w1) + b1[:, None, :])
        y = jnp.einsum('ech,ehm->ecm', h, w2) + b2[:, None, :]
        out = jnp.sum(gate[..., None] * y[topi, pos_c], axis=1)
        return out.reshape(B, S, M)

    def _L1_xattn_ref(x, context, Wq, Wk, Wv, Wo, bo):
        import jax, jax.numpy as jnp
        import numpy as np
        HEADS = 16
        DIM_HEAD = 64
        SCALE = DIM_HEAD ** (-0.5)
        QUERY_DIM = 128
        CONTEXT_DIM = 96
        INNER_DIM = HEADS * DIM_HEAD
        B, Nq, _ = x.shape
        Nk = context.shape[1]
        q = x @ Wq
        k = context @ Wk
        v = context @ Wv
        q = q.reshape(B, Nq, HEADS, DIM_HEAD).transpose(0, 2, 1, 3)
        k = k.reshape(B, Nk, HEADS, DIM_HEAD).transpose(0, 2, 1, 3)
        v = v.reshape(B, Nk, HEADS, DIM_HEAD).transpose(0, 2, 1, 3)
        sim = jnp.einsum('bhid,bhjd->bhij', q, k) * SCALE
        attn = jax.nn.softmax(sim, axis=-1)
        out = jnp.einsum('bhij,bhjd->bhid', attn, v)
        out = out.transpose(0, 2, 1, 3).reshape(B, Nq, INNER_DIM)
        return out @ Wo + bo

    def _L1_ffn_ref(input_batch, router_w, w_in, b_in, w_out, b_out):
        import jax, jax.numpy as jnp
        import numpy as np
        D, H, E, K = (128, 128, 8, 2)

        def _moe(x, router_w, w_in, b_in, w_out, b_out):
            B, S, Dm = x.shape
            T = B * S
            x2 = x.reshape(T, Dm)
            logits = x2 @ router_w
            probs = jax.nn.softmax(logits, axis=-1)
            top_p, top_e = jax.lax.top_k(probs, K)
            flat_e = top_e.reshape(-1)
            flat_p = top_p.reshape(-1)
            tok = jnp.repeat(jnp.arange(T), K)
            order = jnp.argsort(flat_e)
            se, sp, st = (flat_e[order], flat_p[order], tok[order])
            xd = x2[st]
            N = xd.shape[0]
            h = jnp.zeros((N, H), x.dtype)
            for e in range(E):
                m = (se == e)[:, None]
                h = h + jnp.where(m, jax.nn.gelu(xd @ w_in[e] + b_in[e]), 0.0)
            y = jnp.zeros((N, Dm), x.dtype)
            for e in range(E):
                m = (se == e)[:, None]
                y = y + jnp.where(m, h @ w_out[e] + b_out[e], 0.0)
            y = y * sp[:, None]
            out = jnp.zeros((T, Dm), x.dtype).at[st].add(y)
            return out.reshape(B, S, Dm)
        return _moe(input_batch, router_w, w_in, b_in, w_out, b_out)

    def _L2_xattn_ref(image_features, text_features, Wq, bq, Wk, bk, Wv, bv):
        import jax, jax.numpy as jnp
        import numpy as np
        IMG_DIM, TXT_DIM, HID = (128, 96, 128)
        B, LQ, LK = (8, 256, 256)
        query = jnp.einsum('bqi,ih->bqh', image_features, Wq) + bq
        key = jnp.einsum('bkt,th->bkh', text_features, Wk) + bk
        value = jnp.einsum('bkt,th->bkh', text_features, Wv) + bv
        scale = 1.0 / jnp.sqrt(jnp.asarray(HID, query.dtype))
        scores = jnp.einsum('bqh,bkh->bqk', query, key) * scale
        weights = jax.nn.softmax(scores, axis=-1)
        attended = jnp.einsum('bqk,bkh->bqh', weights, value)
        return attended

    def _L2_ffn_ref(hidden_states, router_w, router_b, w1, w2):
        import jax, jax.numpy as jnp
        import numpy as np
        B, S, DIM, FFN, E = (4, 256, 128, 512, 8)
        b, s, d = hidden_states.shape
        x = hidden_states.reshape(-1, d)
        logits = x @ router_w + router_b
        route = jax.nn.softmax(logits, axis=1)
        max_prob = jnp.max(route, axis=1, keepdims=True)
        max_ind = jnp.argmax(route, axis=1)
        out = jnp.zeros_like(x)
        num_experts = w1.shape[0]
        for e in range(num_experts):
            h = x @ w1[e]
            a, g = jnp.split(h, 2, axis=1)
            y = jax.nn.silu(a) * g @ w2[e]
            out = jnp.where((max_ind == e)[:, None], y, out)
        out = out * max_prob
        return out.reshape(b, s, d)

    def _L3_xattn_ref(x, latents, mask, ln_x_g, ln_x_b, ln_l_g, ln_l_b, qn_g, kn_g, Wq, Wkv, Wlkv, Wo, bo):
        import jax, jax.numpy as jnp
        import numpy as np
        DIM_IN, DIM_LAT, DIM_HEAD = (96, 128, 64)
        INNER = max(DIM_LAT, DIM_IN)
        HEADS = INNER // DIM_HEAD
        SCALE = DIM_HEAD ** (-0.5)
        RMS_EPS = 1e-08
        LN_EPS = 1e-05

        def layernorm(x, g, b):
            mu = jnp.mean(x, axis=-1, keepdims=True)
            var = jnp.mean((x - mu) ** 2, axis=-1, keepdims=True)
            return (x - mu) * jax.lax.rsqrt(var + LN_EPS) * g + b

        def rmsnorm(x, gamma):
            norm = jnp.sqrt(jnp.sum(x * x, axis=-1, keepdims=True)) * x.shape[-1] ** (-0.5)
            return x / jnp.maximum(norm, RMS_EPS) * gamma
        b, n, _ = x.shape
        m = latents.shape[1]
        xn = layernorm(x, ln_x_g, ln_x_b)
        ln = layernorm(latents, ln_l_g, ln_l_b)
        q = ln @ Wq.T
        kv = jnp.concatenate([xn @ Wkv.T, ln @ Wlkv.T], axis=1)
        k, v = (kv[..., :INNER], kv[..., INNER:])
        split_heads = lambda t: t.reshape(t.shape[0], t.shape[1], HEADS, DIM_HEAD).transpose(0, 2, 1, 3)
        q, k, v = (split_heads(q), split_heads(k), split_heads(v))
        qn = rmsnorm(q, qn_g) * SCALE
        kn = rmsnorm(k, kn_g)
        attn = jnp.einsum('bhid,bhjd->bhij', qn, kn)
        full_mask = jnp.pad(mask, ((0, 0), (0, m)), constant_values=True)
        attn = jnp.where(full_mask[:, None, None, :], attn, -jnp.finfo(attn.dtype).max)
        attn = jax.nn.softmax(attn, axis=-1)
        out = jnp.einsum('bhij,bhjd->bhid', attn, v)
        out = out.transpose(0, 2, 1, 3).reshape(b, m, INNER)
        return out @ Wo.T + bo

    def _L3_ffn_ref(x, w_gate, w_up, w_down):
        import jax, jax.numpy as jnp
        import numpy as np
        DIM = 128
        HIDDEN = 384
        SCALE = 1.0 / 127.0

        def _dequant(w_int, dtype):
            return w_int.astype(dtype) * jnp.asarray(SCALE, dtype)
        wg = _dequant(w_gate, x.dtype)
        wu = _dequant(w_up, x.dtype)
        wd = _dequant(w_down, x.dtype)
        gate = jnp.einsum('bsd,hd->bsh', x, wg)
        up = jnp.einsum('bsd,hd->bsh', x, wu)
        h = jax.nn.silu(gate) * up
        return jnp.einsum('bsh,dh->bsd', h, wd)
    x = x + _L0_xattn_ref(_layernorm(x, axis=-1), ctx_768, L0_xattn_Wq, L0_xattn_Wk, L0_xattn_Wv, L0_xattn_Wo, L0_xattn_bo)
    x = x + _L0_ffn_ref(_layernorm(x, axis=-1), L0_ffn_wg, L0_ffn_w1, L0_ffn_b1, L0_ffn_w2, L0_ffn_b2)
    x = x + _L1_xattn_ref(_layernorm(x, axis=-1), ctx_768, L1_xattn_Wq, L1_xattn_Wk, L1_xattn_Wv, L1_xattn_Wo, L1_xattn_bo)
    x = x + _L1_ffn_ref(_layernorm(x, axis=-1), L1_ffn_router_w, L1_ffn_w_in, L1_ffn_b_in, L1_ffn_w_out, L1_ffn_b_out)
    x = x + _L2_xattn_ref(_layernorm(x, axis=-1), ctx_768, L2_xattn_Wq, L2_xattn_bq, L2_xattn_Wk, L2_xattn_bk, L2_xattn_Wv, L2_xattn_bv)
    x = x + _L2_ffn_ref(_layernorm(x, axis=-1), L2_ffn_router_w, L2_ffn_router_b, L2_ffn_w1, L2_ffn_w2)
    x = x + _L3_xattn_ref(ctx_768, _layernorm(x, axis=-1), mask_BxS2_bk0, L3_xattn_ln_x_g, L3_xattn_ln_x_b, L3_xattn_ln_l_g, L3_xattn_ln_l_b, L3_xattn_qn_g, L3_xattn_kn_g, L3_xattn_Wq, L3_xattn_Wkv, L3_xattn_Wlkv, L3_xattn_Wo, L3_xattn_bo)
    x = x + _L3_ffn_ref(_layernorm(x, axis=-1), L3_ffn_w_gate, L3_ffn_w_up, L3_ffn_w_down)
    return x

_drawn_inputs = setup_inputs


def setup_inputs(seed=0):
    import zlib

    import numpy as np

    out = dict(_drawn_inputs(seed))
    spreads = {'L0_ffn_b1': (0.0, 0.1),
     'L0_ffn_b2': (0.0, 0.1),
     'L1_xattn_bo': (0.0, 0.1),
     'L1_ffn_b_in': (0.0, 0.267),
     'L1_ffn_b_out': (0.0, 0.1),
     'L2_ffn_router_b': (0.0, 0.8),
     'L3_xattn_ln_x_g': (1.0, 0.597),
     'L3_xattn_ln_x_b': (0.0, 1.14),
     'L3_xattn_ln_l_g': (1.0, 0.2),
     'L3_xattn_ln_l_b': (0.0, 0.268),
     'L3_xattn_qn_g': (1.0, 0.6),
     'L3_xattn_kn_g': (1.0, 0.6),
     'L3_xattn_bo': (0.0, 0.1)}
    factors = {'L2_xattn_bq': 8.0,
     'L2_xattn_bk': 64.0,
     'L2_ffn_router_w': 8.0,
     'L2_ffn_w1': 8.0,
     'L2_ffn_w2': 8.0}
    for name, (base, spread) in spreads.items():
        noise = np.random.default_rng([zlib.crc32(name.encode()), seed]).standard_normal(out[name].shape)
        drawn = base * np.exp(spread * noise) if base else spread * noise
        out[name] = jnp.asarray(drawn.astype(out[name].dtype))
    for name, factor in factors.items():
        out[name] = (out[name] * factor).astype(out[name].dtype)
    return out
```

```python
from contextlib import ExitStack

import concourse.bass as bass
from concourse import mybir

F32 = mybir.dt.float32
I32 = mybir.dt.int32
U8 = mybir.dt.uint8
ALU = mybir.AluOpType
ACT = mybir.ActivationFunctionType
AX = mybir.AxisListType
ds = bass.ds

P = 128
NB = 32
D = 128
S2 = 77
DC = 96
HD = 64
NE = 8
G = 4
NG = NB // G
CAP = 2 * NB * P // NE
EPS = 1e-5
RMS_EPS = 1e-8
FLT_MAX = 3.4028234663852886e38
BANK = 512
ENGINES = 4


def at_least(eng, sem, value):
    if isinstance(value, int) and value <= 0:
        return
    eng.wait_ge(sem, value)


def within(n, low, high):
    return not isinstance(n, int) or low <= n < high


def steps(eng, step, total, head, tail):
    for n in range(head):
        step(n, n % 2)
    with eng.Fori(head // 2, (total - tail) // 2) as i:
        for u in (0, 1):
            step(i * 2 + u, u)
    for n in range(total - tail, total):
        step(n, n % 2)


class Stage:

    def __init__(self, sem):
        self.bn = sem("bn")
        self.mv = sem("mv")
        self.ve = sem("ve")
        self.rstd = sem("rstd")
        self.xn = sem("xn")
        self.bn2 = sem("bn2")
        self.mv2 = sem("mv2")
        self.ve2 = sem("ve2")
        self.rstd2 = sem("rstd2")
        self.xn2 = sem("xn2")
        self.xt_ps = sem("xt_ps")
        self.xt_sb = sem("xt_sb")
        self.xall = sem("xall")
        self.ctx = sem("ctx")
        self.fold_ps = sem("fold_ps")
        self.fold_sb = sem("fold_sb")
        self.q_ps = sem("q_ps")
        self.q_sb = sem("q_sb")
        self.k_ps = sem("k_ps")
        self.k_sb = sem("k_sb")
        self.v_ps = sem("v_ps")
        self.v_sb = sem("v_sb")
        self.t_ps = sem("t_ps")
        self.t_sb = sem("t_sb")
        self.qkv_ps = sem("qkv_ps")
        self.sq = sem("sq")
        self.ss = sem("ss")
        self.sr = sem("sr")
        self.sr2 = sem("sr2")
        self.qk = sem("qk")
        self.qkt_ps = sem("qkt_ps")
        self.qt_sb = sem("qt_sb")
        self.kt_ps = sem("kt_ps")
        self.kt_sb = sem("kt_sb")
        self.s_ps = sem("s_ps")
        self.m1 = sem("m1")
        self.m2 = sem("m2")
        self.m3 = sem("m3")
        self.m4 = sem("m4")
        self.top = sem("top")
        self.shift = sem("shift")
        self.ex = sem("ex")
        self.tot = sem("tot")
        self.rec = sem("rec")
        self.probs = sem("probs")
        self.pt_ps = sem("pt_ps")
        self.pt_sb = sem("pt_sb")
        self.o_ps = sem("o_ps")
        self.o_sb = sem("o_sb")
        self.mask = sem("mask")
        self.l_ps = sem("l_ps")
        self.lg = sem("lg")
        self.gate_step = sem("gate_step")
        self.cnt_ps = sem("cnt_ps")
        self.gb = sem("gb")
        self.gt_ps = sem("gt_ps")
        self.gt_sb = sem("gt_sb")
        self.bb_ps = sem("bb_ps")
        self.bb = sem("bb")
        self.w0 = sem("w0")
        self.w1 = sem("w1")
        self.up_ps = sem("up_ps")
        self.act = sem("act")
        self.h = sem("h")
        self.y_ps = sem("y_ps")
        self.added = sem("added")
        self.x = sem("x")


class Loads:

    def __init__(self, sem):
        self.x = sem("x")
        self.attn0 = sem("attn0")
        self.attn1 = sem("attn1")
        self.l2 = sem("l2")
        self.ffn0 = sem("ffn0")
        self.ffn1 = sem("ffn1")
        self.ffn2 = sem("ffn2")
        self.ffn3 = sem("ffn3")
        self.l3 = sem("l3")
        self.ctxn = sem("ctxn")
        self.out = sem("out")


class Constants:

    def __init__(self, sem):
        self.zero = sem("zero")
        self.order = sem("order")
        self.ready = sem("ready")
        self.bias = sem("bias")


def build(nc, t, out):
    with ExitStack() as ctx:
        def sb(name, shape, dt=F32):
            return ctx.enter_context(nc.sbuf_tensor("sb_" + name, shape, dt))

        X = sb("X", [P, NB, D])
        ctxT = sb("ctxT", [DC, NB * S2])
        ident = sb("ident", [P, P])
        raw = sb("raw", [P, 10752])
        work = sb("work", [P, 5600])
        score = sb("score", [P, 2, 16 * S2])
        foldT = sb("foldT", [DC, 16 * P])
        foldV = sb("foldV", [DC, 16 * D])
        ctx_b = sb("ctx_b", [DC, 2, G * S2])
        xn = sb("xn", [P, G, D])
        xnT = sb("xnT", [P, 2, G * P])
        bnst = sb("bnst", [P, 2, G, 6])
        mv = sb("mv", [P, 2, G, 2])
        ve = sb("ve", [P, 2, G])
        rstd = sb("rstd", [P, 2, G])
        mhalf = sb("mhalf", [P, 16])
        epss = sb("epss", [P, G])
        top = sb("top", [P, 16])
        tot = sb("tot", [P, 16])
        rec = sb("rec", [P, 16])
        obias = sb("obias", [P, 3, D])
        xall = sb("xall", [P, NB * P])
        hid = sb("hid", [P, 2, 4, BANK])
        w1 = sb("w1", [P, 2, 1024])
        w2 = sb("w2", [P, 2, 4, D])
        b1 = sb("b1", [P, 2, 4])
        silu = sb("silu", [P, 2, BANK])
        b2 = sb("b2", [NE, 2, D])
        gates = sb("gates", [P, NB, NE])
        gb = sb("gb", [P, G * NE])
        gT = sb("gT", [NE, G * P])
        wr = sb("wr", [P, 3, NE])
        rb = sb("rb", [P, NE])
        lg = sb("lg", [P, NB, NE])
        ga = sb("ga", [P, NB, NE])
        gc = sb("gc", [P, NB, NE])
        pick = sb("pick", [P, NE, 2, NB])
        pref = sb("pref", [P, NE * 2 * NB])
        first = sb("first", [P, NE * 2 * NB])
        gtop = sb("gtop", [P, 2, NB])
        gtmp = sb("gtmp", [P, NB])
        order = sb("order", [P, NE])
        upper = sb("upper", [P, P])
        ones = sb("ones", [P, P])
        l2w = sb("l2w", [P, 3, D])
        l2b = sb("l2b", [P, 2])
        qkn = sb("qkn", [P, 2, G * P])
        l3g = sb("l3g", [P, 8])
        l3w = sb("l3w", [P, 384 + 256 + 128])
        sq = sb("sq", [P, 512])
        ss = sb("ss", [P, 8])
        sr = sb("sr", [P, 8])
        sr2 = sb("sr2", [P, 8])
        mask8 = sb("mask8", [P, NB * S2], U8)

        bank = [ctx.enter_context(nc.psum_tensor(f"bank{i}", [P, BANK], F32)) for i in range(8)]

        def sems(kind, prefix):
            return kind(lambda n: ctx.enter_context(nc.semaphore(f"{prefix}_{n}")))

        stage = [sems(Stage, "even"), sems(Stage, "odd")]
        passed = ctx.enter_context(nc.semaphore("passed"))
        phase_done = ctx.enter_context(nc.semaphore("phase_done"))
        loads = sems(Loads, "load")
        const = sems(Constants, "const")

        def phase_start(eng, k):
            if k > 0:
                eng.wait_ge(phase_done, ENGINES * k)

        def clear_last_phase(pool, k):
            if k > 0:
                old = stage[(k - 1) % 2]
                pool.sem_clear(range(old.bn.num, old.x.num + 1))

        def phase_end(eng):
            eng.drain().then_inc(phase_done, 1)

        def tile(n):
            return X[:, ds(n, 1), :].rearrange("p a d -> p (a d)")


        def hold(dve, sem, value):
            dve.wait_ge(sem, value)
            dve.sem_inc(passed, 1)

        def ln_stats(dve, s, n, u, g):
            for i in range(g):
                dve.bn_stats(bnst[:, u, i, :], tile(n * g + i)).then_inc(s.bn, 1)
            hold(dve, s.bn, (n + 1) * g)
            for i in range(g):
                dve.bn_aggr(mv[:, u, i, :], bnst[:, u, i, :]).then_inc(s.mv, 1)

        def ln_rstd(pool, s, n, u, g):
            pool.wait_ge(s.mv, (n + 1) * g)
            pool.tensor_tensor(ve[:, u, 0:g], mv[:, u, 0:g, 1], epss[:, 0:g], ALU.add).then_inc(s.ve, 1)
            pool.wait_ge(s.ve, n + 1)
            pool.tensor_tensor(rstd[:, u, 0:g], ve[:, u, 0:g], mhalf[:, 0:g], ALU.pow).then_inc(s.rstd, 1)

        def ln_apply(dve, s, n, u, g, transposed):
            dve.wait_ge(s.rstd, n + 1)
            at_least(dve, transposed, n)
            for i in range(g):
                ins = dve.tensor_scalar(xn[:, i, :], tile(n * g + i), mv[:, u, i, 0:1],
                                        rstd[:, u, i:i + 1], ALU.subtract, ALU.mult)
            ins.then_inc(s.xn, 1)

        class Attention:
            def __init__(self, layer, phase, heads):
                self.layer, self.phase, self.heads = layer, phase, heads
                self.chunks = heads // 4
                self.load = (loads.attn0, loads.attn1)[layer]
                o = 0 if layer else 7168
                self.wqT = raw[0:HD, o:o + heads * D].rearrange("p (h d) -> p h d", h=heads)
                self.woh = raw[HD:P, o:o + heads * D].rearrange("p (h d) -> p h d", h=heads)
                o += heads * D
                self.wkT = raw[0:HD, o:o + heads * DC].rearrange("p (h d) -> p h d", h=heads)
                self.wvT = raw[HD:P, o:o + heads * DC].rearrange("p (h d) -> p h d", h=heads)
                self.bias = obias[:, layer, :]
                self.s = stage[phase % 2]

        keys = work[:, 0:1232]
        vals = work[0:S2, 1232:3280]
        probsT = work[0:S2, 3280:5328]
        RING = (4, 5, 6)

        def ring(a, kind, c):
            return bank[RING[(kind * a.chunks + c) % 3]]

        def ring_free(pe, a, n, kind, c):
            s, k = a.s, kind * a.chunks + c - 3
            back = 0
            if k < 0:
                k, back = k + 3 * a.chunks, 1
            was, c0 = k // a.chunks, k % a.chunks
            if was == 0 and not within(n, 0, NB):
                return at_least(pe, s.pt_sb, (n - 1) * a.chunks)
            done = (s.t_sb, s.v_sb, s.pt_sb)[was]
            at_least(pe, done, (n - back - (1 if was else 0)) * a.chunks + c0 + 1)

        def attn_fold_pe(pe, a):
            s = a.s
            pe.wait_ge(a.load, 16 * 4)
            pe.wait_ge(const.ready, 3)
            for j in range(2 * a.chunks):
                if j >= 3:
                    pe.wait_ge(s.fold_sb, j - 2)
                for i in range(4):
                    h = 4 * (j % a.chunks) + i
                    lhs, rhs = (a.wkT, a.wqT) if j < a.chunks else (a.wvT, a.woh)
                    ins = pe.matmul(bank[RING[j % 3]][0:DC, i * D:(i + 1) * D], lhs[:, h, :], rhs[:, h, :],
                                    start=True, stop=True)
                ins.then_inc(s.fold_ps, 1)
            pe.wait_ge(s.fold_sb, 2 * a.chunks)

        def attn_fold_act(act, a):
            for j in range(2 * a.chunks):
                act.wait_ge(a.s.fold_ps, j + 1)
                c = j % a.chunks
                dst = foldT if j < a.chunks else foldV
                nc.scalar.copy(dst[:, c * BANK:(c + 1) * BANK], bank[RING[j % 3]][0:DC, :]).then_inc(a.s.fold_sb, 1)

        def attn_pe(pe, a):
            s, C, W = a.s, a.chunks, 4 * S2
            phase_start(pe, a.phase)
            attn_fold_pe(pe, a)

            def step(n, u):
                if within(n, 0, NB):
                    pe.wait_ge(s.xn, n + 1)
                    at_least(pe, s.shift, (n - 1) * C + 1)
                    pe.transpose(bank[0][:, 384:512], xn[:, 0, :], ident[:, :]).then_inc(s.xt_ps, 1)
                    pe.wait_ge(s.ctx, n + 1)
                    for c in range(C):
                        ring_free(pe, a, n, 0, c)
                        for i in range(4):
                            h = 4 * c + i
                            ins = pe.matmul(ring(a, 0, c)[:, i * S2:(i + 1) * S2], foldT[:, h * P:(h + 1) * P],
                                            ctx_b[:, u, 0:S2], start=True, stop=True)
                        ins.then_inc(s.t_ps, 1)
                if within(n, 1, NB + 1):
                    for c in range(C):
                        ring_free(pe, a, n, 1, c)
                        pe.matmul(ring(a, 1, c)[0:S2, :], ctx_b[:, 1 - u, 0:S2], foldV[:, c * BANK:(c + 1) * BANK],
                                  start=True, stop=True).then_inc(s.v_ps, 1)
                    pe.wait_ge(s.probs, n)
                    for c in range(C):
                        ring_free(pe, a, n, 2, c)
                        for i in range(4):
                            h = 4 * c + i
                            ins = pe.transpose(ring(a, 2, c)[0:S2, i * P:(i + 1) * P],
                                               score[:, 1 - u, h * S2:(h + 1) * S2], ident[:, :])
                        ins.then_inc(s.pt_ps, 1)
                if within(n, 0, NB):
                    pe.wait_ge(s.xt_sb, n + 1)
                    for c in range(C):
                        pe.wait_ge(s.t_sb, n * C + c + 1)
                        at_least(pe, s.shift, (n - 1) * C + c + 1)
                        pe.matmul(bank[c][:, 0:W], xnT[:, 0, 0:P], keys[:, c * W:(c + 1) * W],
                                  start=True, stop=True).then_inc(s.s_ps, 1)
                if within(n, 1, NB + 1):
                    pe.wait_ge(s.v_sb, n * C)
                    pe.wait_ge(s.pt_sb, n * C)
                    at_least(pe, s.added, n - 1)
                    for h in range(a.heads):
                        ins = pe.matmul(bank[7][:, 0:D], probsT[:, h * P:(h + 1) * P], vals[:, h * D:(h + 1) * D],
                                        start=(h == 0), stop=(h == a.heads - 1))
                    ins.then_inc(s.y_ps, 1)

            steps(pe, step, NB + 1, 2, 3)
            phase_end(pe)

        def attn_act(act, a):
            s, C, W = a.s, a.chunks, 4 * S2
            phase_start(act, a.phase)
            attn_fold_act(act, a)

            def step(n, u):
                if within(n, 0, NB):
                    act.wait_ge(s.xt_ps, n + 1)
                    at_least(act, s.s_ps, n * C)
                    nc.scalar.copy(xnT[:, 0, 0:P], bank[0][:, 384:512]).then_inc(s.xt_sb, 1)
                    for c in range(C):
                        act.wait_ge(s.t_ps, n * C + c + 1)
                        nc.scalar.copy(keys[:, c * W:(c + 1) * W], ring(a, 0, c)[:, 0:W]).then_inc(s.t_sb, 1)
                if within(n, 1, NB + 1):
                    at_least(act, s.y_ps, n - 1)
                    for c in range(C):
                        act.wait_ge(s.pt_ps, (n - 1) * C + c + 1)
                        nc.scalar.copy(probsT[:, c * BANK:(c + 1) * BANK], ring(a, 2, c)[0:S2, :]).then_inc(s.pt_sb, 1)
                if within(n, 0, NB):
                    for c in range(C):
                        act.wait_ge(s.shift, n * C + c + 1)
                        e = score[:, u, c * W:(c + 1) * W]
                        nc.scalar.activation(e, e, ACT.Exp, scale=HD ** -0.5).then_inc(s.ex, 1)

            steps(act, step, NB + 1, 2, 3)
            phase_end(act)

        def attn_pool(pool, a):
            s, C = a.s, a.chunks
            phase_start(pool, a.phase)
            clear_last_phase(pool, a.phase)

            def fetch(n, u):
                at_least(pool, s.v_ps, (n - 1) * C)
                pool.tensor_copy(ctx_b[:, u, 0:S2], ctxT[:, ds(n * S2, S2)]).then_inc(s.ctx, 1)

            pool.wait_ge(loads.x, 32)
            fetch(0, 0)
            ln_rstd(pool, s, 0, 0, 1)

            def step(n, u):
                if within(n, 0, NB - 1):
                    ln_rstd(pool, s, n + 1, 1 - u, 1)
                    fetch(n + 1, 1 - u)

            steps(pool, step, NB + 1, 2, 3)
            phase_end(pool)

        def attn_dve(dve, a):
            s, C, H, W = a.s, a.chunks, a.heads, 4 * S2
            phase_start(dve, a.phase)
            dve.wait_ge(loads.x, 32)
            ln_stats(dve, s, 0, 0, 1)
            ln_apply(dve, s, 0, 0, 1, s.xt_ps)

            def heads_of(ap):
                return ap.rearrange("p (h j) -> p h j", j=S2)

            def step(n, u):
                if within(n, 1, NB + 1):
                    at_least(dve, s.y_ps, n - 1)
                    for c in range(C):
                        dve.wait_ge(s.v_ps, (n - 1) * C + c + 1)
                        dve.tensor_copy(vals[:, c * BANK:(c + 1) * BANK], ring(a, 1, c)[0:S2, :]).then_inc(s.v_sb, 1)
                if within(n, 0, NB - 1):
                    ln_stats(dve, s, n + 1, 1 - u, 1)
                if within(n, 0, NB):
                    at_least(dve, s.pt_ps, (n - 1) * C)
                    for c in range(C):
                        dve.wait_ge(s.s_ps, n * C + c + 1)
                        dve.reduce_max(top[:, 4 * c:4 * c + 4], heads_of(bank[c][:, 0:W]), AX.X).then_inc(s.top, 1)
                        dve.wait_ge(s.top, n * C + c + 1)
                        dve.tensor_tensor(heads_of(score[:, u, c * W:(c + 1) * W]), heads_of(bank[c][:, 0:W]),
                                          top[:, 4 * c:4 * c + 4].unsqueeze(2).to_broadcast([P, 4, S2]),
                                          ALU.subtract).then_inc(s.shift, 1)
                if within(n, 0, NB - 1):
                    ln_apply(dve, s, n + 1, 1 - u, 1, s.xt_ps)
                if within(n, 0, NB):
                    for c in range(C):
                        e = heads_of(score[:, u, c * W:(c + 1) * W])
                        dve.wait_ge(s.ex, n * C + c + 1)
                        dve.reduce_sum(tot[:, 4 * c:4 * c + 4], e, AX.X).then_inc(s.tot, 1)
                    dve.wait_ge(s.tot, (n + 1) * C)
                    dve.reciprocal(rec[:, 0:H], tot[:, 0:H]).then_inc(s.rec, 1)
                    dve.wait_ge(s.rec, n + 1)
                    e = heads_of(score[:, u, 0:H * S2])
                    dve.tensor_tensor(e, e, rec[:, 0:H].unsqueeze(2).to_broadcast([P, H, S2]),
                                      ALU.mult).then_inc(s.probs, 1)
                if within(n, 1, NB + 1):
                    dve.wait_ge(s.y_ps, n)
                    x = tile(n - 1)
                    dve.tensor_tensor(x, bank[7][:, 0:D], x, ALU.add).then_inc(s.added, 1)
                    dve.wait_ge(s.added, n)
                    dve.tensor_tensor(x, x, a.bias, ALU.add).then_inc(s.x, 1)

            steps(dve, step, NB + 1, 2, 3)
            phase_end(dve)

        s2 = stage[4 % 2]
        PH2 = 4
        q2, k2 = qkn[:, 0, :], work[:, 0:G * S2]
        v2, pT2 = work[0:S2, 512:1024], work[0:S2, 1024:1536]

        def attn2_pe(pe):
            s = s2
            phase_start(pe, PH2)
            pe.wait_ge(loads.l2, 16 * 5)

            def step(n, u):
                if within(n, 0, NG):
                    pe.wait_ge(s.xn, n + 1)
                    at_least(pe, s.xt_sb, n)
                    for i in range(G):
                        ins = pe.transpose(bank[0][:, i * P:(i + 1) * P], xn[:, i, :], ident[:, :])
                    ins.then_inc(s.xt_ps, 1)
                    pe.wait_ge(s.ctx, n + 1)
                    at_least(pe, s.k_sb, n)
                    pe.matmul(bank[2][:, 0:G * S2], l2w[0:DC, 1, :], ctx_b[:, u, :], start=True, stop=True)\
                      .then_inc(s.k_ps, 1)
                    pe.wait_ge(s.xt_sb, n + 1)
                    at_least(pe, s.q_sb, n)
                    pe.matmul(bank[1][:, :], l2w[:, 0, :], xnT[:, 0, :], start=True, stop=True).then_inc(s.q_ps, 1)
                if within(n, 1, NG + 1):
                    at_least(pe, s.v_sb, n - 1)
                    for i in range(G):
                        ins = pe.matmul(bank[3][0:S2, i * D:(i + 1) * D], ctx_b[:, 1 - u, i * S2:(i + 1) * S2],
                                        l2w[0:DC, 2, :], start=True, stop=True)
                    ins.then_inc(s.v_ps, 1)
                    pe.wait_ge(s.probs, n)
                    at_least(pe, s.pt_sb, n - 1)
                    for i in range(G):
                        ins = pe.transpose(bank[5][0:S2, i * P:(i + 1) * P], score[:, 1 - u, i * S2:(i + 1) * S2],
                                           ident[:, :])
                    ins.then_inc(s.pt_ps, 1)
                if within(n, 0, NG):
                    pe.wait_ge(s.q_sb, n + 1)
                    pe.wait_ge(s.k_sb, n + 1)
                    at_least(pe, s.shift, n)
                    for i in range(G):
                        ins = pe.matmul(bank[4][:, i * S2:(i + 1) * S2], q2[:, i * P:(i + 1) * P],
                                        k2[:, i * S2:(i + 1) * S2], start=True, stop=True)
                    ins.then_inc(s.s_ps, 1)
                if within(n, 1, NG + 1):
                    pe.wait_ge(s.v_sb, n)
                    pe.wait_ge(s.pt_sb, n)
                    at_least(pe, s.added, n - 1)
                    for i in range(G):
                        ins = pe.matmul(bank[6][:, i * D:(i + 1) * D], pT2[:, i * P:(i + 1) * P],
                                        v2[:, i * D:(i + 1) * D], start=True, stop=True)
                    ins.then_inc(s.y_ps, 1)

            steps(pe, step, NG + 1, 2, 3)
            phase_end(pe)

        def attn2_act(act):
            s = s2
            phase_start(act, PH2)
            act.wait_ge(loads.l2, 16 * 5)

            def step(n, u):
                if within(n, 0, NG):
                    act.wait_ge(s.xt_ps, n + 1)
                    at_least(act, s.q_ps, n)
                    nc.scalar.copy(xnT[:, 0, :], bank[0][:, :]).then_inc(s.xt_sb, 1)
                    act.wait_ge(s.k_ps, n + 1)
                    at_least(act, s.s_ps, n)
                    nc.scalar.activation(k2, bank[2][:, 0:G * S2], ACT.Identity, bias=l2b[:, 1:2]).then_inc(s.k_sb, 1)
                    act.wait_ge(s.q_ps, n + 1)
                    nc.scalar.activation(q2, bank[1][:, :], ACT.Identity, bias=l2b[:, 0:1]).then_inc(s.q_sb, 1)
                if within(n, 1, NG + 1):
                    act.wait_ge(s.v_ps, n)
                    at_least(act, s.y_ps, n - 1)
                    nc.scalar.copy(v2, bank[3][0:S2, :]).then_inc(s.v_sb, 1)
                    act.wait_ge(s.pt_ps, n)
                    nc.scalar.copy(pT2, bank[5][0:S2, :]).then_inc(s.pt_sb, 1)
                if within(n, 0, NG):
                    act.wait_ge(s.shift, n + 1)
                    e = score[:, u, 0:G * S2]
                    nc.scalar.activation(e, e, ACT.Exp, scale=D ** -0.5).then_inc(s.ex, 1)

            steps(act, step, NG + 1, 2, 3)
            phase_end(act)

        def attn2_pool(pool):
            s = s2
            phase_start(pool, PH2)
            clear_last_phase(pool, PH2)

            def fetch(n, u):
                at_least(pool, s.v_ps, n - 1)
                pool.tensor_copy(ctx_b[:, u, :], ctxT[:, ds(n * G * S2, G * S2)]).then_inc(s.ctx, 1)

            fetch(0, 0)
            ln_rstd(pool, s, 0, 0, G)

            def step(n, u):
                if within(n, 0, NG - 1):
                    ln_rstd(pool, s, n + 1, 1 - u, G)
                    fetch(n + 1, 1 - u)

            steps(pool, step, NG + 1, 2, 3)
            phase_end(pool)

        def attn2_dve(dve):
            s = s2
            phase_start(dve, PH2)
            dve.wait_ge(loads.l2, 16 * 5)
            ln_stats(dve, s, 0, 0, G)
            ln_apply(dve, s, 0, 0, G, s.xt_ps)

            def step(n, u):
                if within(n, 0, NG - 1):
                    ln_stats(dve, s, n + 1, 1 - u, G)
                e = score[:, u, 0:G * S2].rearrange("p (h j) -> p h j", j=S2)
                if within(n, 0, NG):
                    at_least(dve, s.pt_ps, n - 1)
                    sc = bank[4][:, 0:G * S2].rearrange("p (h j) -> p h j", j=S2)
                    dve.wait_ge(s.s_ps, n + 1)
                    dve.reduce_max(top[:, 0:G], sc, AX.X).then_inc(s.top, 1)
                    dve.wait_ge(s.top, n + 1)
                    dve.tensor_tensor(e, sc, top[:, 0:G].unsqueeze(2).to_broadcast([P, G, S2]),
                                      ALU.subtract).then_inc(s.shift, 1)
                if within(n, 0, NG - 1):
                    ln_apply(dve, s, n + 1, 1 - u, G, s.xt_ps)
                if within(n, 0, NG):
                    dve.wait_ge(s.ex, n + 1)
                    dve.reduce_sum(tot[:, 0:G], e, AX.X).then_inc(s.tot, 1)
                    dve.wait_ge(s.tot, n + 1)
                    dve.reciprocal(rec[:, 0:G], tot[:, 0:G]).then_inc(s.rec, 1)
                    dve.wait_ge(s.rec, n + 1)
                    dve.tensor_tensor(e, e, rec[:, 0:G].unsqueeze(2).to_broadcast([P, G, S2]),
                                      ALU.mult).then_inc(s.probs, 1)
                if within(n, 1, NG + 1):
                    dve.wait_ge(s.y_ps, n)
                    x = X[:, ds((n - 1) * G, G), :]
                    dve.tensor_tensor(x, bank[6][:, :].rearrange("p (g d) -> p g d", g=G), x, ALU.add)\
                       .then_inc(s.added, 1)
                    dve.wait_ge(s.added, n)
                    dve.tensor_tensor(x, x, obias[:, 2, :].unsqueeze(1).to_broadcast([P, G, D]), ALU.add)\
                       .then_inc(s.x, 1)

            steps(dve, step, NG + 1, 2, 3)
            phase_end(dve)

        PH3C, PH3X = 6, 7
        kc = raw[:, 0:NB * S2]
        vc = raw[0:S2, 2560:2560 + NB * D].rearrange("p (b d) -> p b d", d=D)
        maskf = raw[:, 6656:6656 + NB * S2]
        ctxn = work[0:S2, 0:NB * DC].rearrange("p (b c) -> p b c", c=DC)
        maskb = work[:, NB * DC:NB * DC + NB * S2]
        wkv, wl, wo3 = l3w[0:DC, 384:640], l3w[:, 0:384], l3w[:, 640:768]
        s3c = stage[6 % 2]

        def ctx3_pe(pe):
            s = s3c
            phase_start(pe, PH3C)
            pe.wait_ge(loads.l3, 16 * 9)
            with pe.Fori(0, NG) as n:
                pe.wait_ge(s.xn, n + 1)
                for i in range(G):
                    ins = pe.transpose(bank[0][0:DC, i * S2:(i + 1) * S2], xn[0:S2, i, 0:DC], ident[0:S2, 0:S2])
                ins.then_inc(s.xt_ps, 1)
                pe.wait_ge(s.xt_sb, n + 1)
                for i in range(G):
                    ins = pe.matmul(bank[1 + i // 2][0:S2, (i % 2) * 256:(i % 2) * 256 + 256],
                                    xnT[0:DC, 0, i * S2:(i + 1) * S2], wkv, start=True, stop=True)
                ins.then_inc(s.qkv_ps, 1)
                pe.wait_ge(s.qk, n + 1)
                for i in range(G):
                    ins = pe.transpose(bank[3][:, i * S2:(i + 1) * S2], qkn[0:S2, 0, i * P:(i + 1) * P],
                                       ident[0:S2, 0:S2])
                ins.then_inc(s.kt_ps, 1)
                pe.wait_ge(s.kt_sb, n + 1)
            phase_end(pe)

        def kv_view(lo, hi, i):
            return bank[1 + i][0:S2, :].rearrange("p (b c) -> p b c", b=2)[:, :, lo:hi]

        def ctx3_act(act):
            s = s3c
            phase_start(act, PH3C)
            act.wait_ge(loads.l3, 16 * 9)
            with act.Fori(0, NG) as n:
                act.wait_ge(s.xt_ps, n + 1)
                nc.scalar.activation(xnT[0:DC, 0, 0:G * S2], bank[0][0:DC, 0:G * S2], ACT.Identity,
                                     bias=l3g[0:DC, 1:2], scale=l3g[0:DC, 0:1]).then_inc(s.xt_sb, 1)
                act.wait_ge(s.qkv_ps, n + 1)
                for i in range(2):
                    nc.scalar.activation(sq[0:S2, i * 256:(i + 1) * 256].rearrange("p (b c) -> p b c", b=2),
                                         kv_view(0, 128, i), ACT.Square).then_inc(s.sq, 1)
                for i in range(2):
                    nc.scalar.copy(vc[:, ds(n * G + 2 * i, 2), :], kv_view(128, 256, i)).then_inc(s.v_sb, 1)
                act.wait_ge(s.kt_ps, n + 1)
                nc.scalar.copy(kc[:, ds(n * G * S2, G * S2)], bank[3][:, 0:G * S2]).then_inc(s.kt_sb, 1)
            phase_end(act)

        def ctx3_pool(pool):
            s = s3c
            phase_start(pool, PH3C)
            clear_last_phase(pool, PH3C)
            with pool.Fori(0, NG) as n:
                pool.wait_ge(s.mv, (n + 1) * G)
                pool.tensor_tensor(ve[0:S2, 0, :], mv[0:S2, 0, :, 1], epss[0:S2, :], ALU.add).then_inc(s.ve, 1)
                pool.wait_ge(s.ve, n + 1)
                pool.tensor_tensor(rstd[0:S2, 0, :], ve[0:S2, 0, :], mhalf[0:S2, 0:G], ALU.pow).then_inc(s.rstd, 1)
                pool.wait_ge(s.sr, n + 1)
                pool.tensor_tensor(sr2[0:S2, :], sr[0:S2, :], mhalf[0:S2, 0:8], ALU.pow).then_inc(s.sr2, 1)
            phase_end(pool)

        def ctx3_dve(dve):
            s = s3c
            phase_start(dve, PH3C)
            dve.wait_ge(loads.l3, 16 * 9)
            dve.wait_ge(loads.ctxn, 32)
            dve.tensor_copy(maskf, mask8[:, :]).then_inc(s.mask, 1)
            dve.wait_ge(s.mask, 1)
            dve.tensor_scalar(maskb, maskf, -1.0, FLT_MAX, ALU.add, ALU.mult).then_inc(s.mask, 1)
            dve.tensor_tensor(l3g[:, 5:6], l3g[:, 4:5], l3g[:, 6:7], ALU.mult).then_inc(s.mask, 1)
            with dve.Fori(0, NG) as n:
                for i in range(G):
                    dve.bn_stats(bnst[0:S2, 0, i, :], ctxn[:, ds(n * G + i, 1), :].rearrange("p a c -> p (a c)")).then_inc(s.bn, 1)
                hold(dve, s.bn, (n + 1) * G)
                for i in range(G):
                    dve.bn_aggr(mv[0:S2, 0, i, :], bnst[0:S2, 0, i, :]).then_inc(s.mv, 1)
                dve.wait_ge(s.rstd, n + 1)
                for i in range(G):
                    ins = dve.tensor_scalar(xn[0:S2, i, 0:DC], ctxn[:, ds(n * G + i, 1), :].rearrange("p a c -> p (a c)"), mv[0:S2, 0, i, 0:1],
                                            rstd[0:S2, 0, i:i + 1], ALU.subtract, ALU.mult)
                ins.then_inc(s.xn, 1)
                dve.wait_ge(s.sq, 2 * n + 2)
                dve.reduce_sum(ss[0:S2, :], sq[0:S2, :].rearrange("p (h d) -> p h d", d=HD), AX.X).then_inc(s.ss, 1)
                dve.wait_ge(s.ss, n + 1)
                dve.tensor_scalar(sr[0:S2, :], ss[0:S2, :], 1.0 / HD, RMS_EPS ** 2, ALU.mult, ALU.max)\
                   .then_inc(s.sr, 1)
                dve.wait_ge(s.sr2, n + 1)
                dve.wait_ge(s.v_sb, 2 * n + 2)
                for i in range(2):
                    ins = dve.tensor_tensor(
                        qkn[0:S2, 0, i * 256:(i + 1) * 256].rearrange("p (b h d) -> p b h d", b=2, h=2),
                        kv_view(0, 128, i).rearrange("p b (h d) -> p b h d", h=2),
                        sr2[0:S2, 4 * i:4 * i + 4].rearrange("p (b h) -> p b h", b=2).unsqueeze(3)
                        .to_broadcast([S2, 2, 2, HD]), ALU.mult)
                ins.then_inc(s.qk, 1)
            phase_end(dve)

        s3 = stage[7 % 2]
        g3, N3 = 2, NB // 2
        KL = S2 + P
        v3 = hid[:, 0, 0:2, 0:P]
        qT3, kT3 = xall[:, 0:2 * P], xall[:, 256:512]
        pT3 = xall[:, 512:1536]
        oT3 = xall[:, 1536:1536 + 2 * P]
        sc3 = xall[:, 2048:2048 + 2 * 2 * 2 * KL].rearrange("p (u t h j) -> p u t h j", u=2, t=2, h=2)
        v3 = hid[:, :, 0, 0:2 * P].rearrange("p u (t d) -> p u t d", t=2)
        xn3 = hid[:, 0, 1, 0:2 * P].rearrange("p (t d) -> p t d", t=2)
        mv3, rs3 = silu[:, 0, 0:4].rearrange("p (t k) -> p t k", t=2), silu[:, 0, 4:6]
        ve3, bn3 = silu[:, 0, 6:8], silu[:, 0, 8:20].rearrange("p (t k) -> p t k", t=2)

        def sbank(h):
            return bank[4 + h][:, 0:2 * KL].rearrange("p (t j) -> p t j", t=2)

        def attn3_pe(pe):
            s = s3
            phase_start(pe, PH3X)

            def step(n, u):
                if within(n, 0, N3):
                    pe.wait_ge(s.xn2, n + 1)
                    at_least(pe, s.xt_sb, n)
                    for i in range(g3):
                        ins = pe.transpose(bank[0][:, i * P:(i + 1) * P], xn3[:, i, :], ident[:, :])
                    ins.then_inc(s.xt_ps, 1)
                    pe.wait_ge(s.xt_sb, n + 1)
                    at_least(pe, s.qk, n)
                    at_least(pe, s.v_sb, n)
                    for i in range(g3):
                        ins = pe.matmul(bank[1 + i][:, 0:384], xnT[:, 0, i * P:(i + 1) * P], wl, start=True, stop=True)
                    ins.then_inc(s.qkv_ps, 1)
                if within(n, 1, N3 + 1):
                    pe.wait_ge(s.qk, n)
                    at_least(pe, s.kt_sb, n - 1)
                    for i in range(g3):
                        for j in range(2):
                            ins = pe.transpose(bank[3][:, (2 * j + i) * P:(2 * j + i + 1) * P],
                                               qkn[:, 1 - u, (2 * i + j) * P:(2 * i + j + 1) * P], ident[:, :])
                    ins.then_inc(s.qkt_ps, 1)
                    pe.wait_ge(s.kt_sb, n)
                    pe.wait_ge(s.ctx, n)
                    at_least(pe, s.pt_sb, 2 * (n - 1))
                    for i in range(g3):
                        for h in range(2):
                            hp = slice(h * HD, (h + 1) * HD)
                            pe.matmul(bank[4 + h][:, i * KL:i * KL + S2], qT3[hp, i * P:(i + 1) * P],
                                      kcs[hp, 1 - u, i * S2:(i + 1) * S2], start=True, stop=True)
                            ins = pe.matmul(bank[4 + h][:, i * KL + S2:(i + 1) * KL], qT3[hp, i * P:(i + 1) * P],
                                            kT3[hp, i * P:(i + 1) * P], start=True, stop=True)
                    ins.then_inc(s.s_ps, 1)
                    pe.wait_ge(s.probs, n)
                    for i in range(g3):
                        for h in range(2):
                            pr = sc3[:, 1 - u, i, h, :]
                            pe.transpose(bank[4 + i][0:S2, h * P:(h + 1) * P], pr[:, 0:S2], ident[:, :])
                            ins = pe.transpose(bank[4 + i][:, (2 + h) * P:(3 + h) * P], pr[:, S2:KL], ident[:, :])
                        ins.then_inc(s.pt_ps, 1)
                    pe.wait_ge(s.pt_sb, 2 * n)
                    pe.wait_ge(s.xall, n)
                    at_least(pe, s.added, n - 1)
                    for i in range(g3):
                        for h in range(2):
                            o = bank[7][h * HD:(h + 1) * HD, i * P:(i + 1) * P]
                            hv = slice(h * HD, (h + 1) * HD)
                            pe.matmul(o, vcs[:, 1 - u, i, hv], pT3[0:S2, (4 * i + h) * P:(4 * i + h + 1) * P],
                                      start=True, stop=False)
                            ins = pe.matmul(o, v3[:, 1 - u, i, hv], pT3[:, (4 * i + 2 + h) * P:(4 * i + 3 + h) * P],
                                            start=False, stop=True)
                    ins.then_inc(s.o_ps, 1)
                    pe.wait_ge(s.o_sb, n)
                    for i in range(g3):
                        ins = pe.matmul(bank[7][:, 256 + i * P:256 + (i + 1) * P], oT3[:, i * P:(i + 1) * P], wo3,
                                        start=True, stop=True)
                    ins.then_inc(s.y_ps, 1)

            steps(pe, step, N3 + 1, 2, 3)
            phase_end(pe)

        kcs = sb("kcs", [P, 2, g3 * S2])
        vcs = sb("vcs", [S2, 2, g3, D])

        def attn3_act(act):
            s = s3
            phase_start(act, PH3X)

            def step(n, u):
                if within(n, 0, N3):
                    act.wait_ge(s.xt_ps, n + 1)
                    at_least(act, s.qkv_ps, n)
                    nc.scalar.activation(xnT[:, 0, 0:2 * P], bank[0][:, 0:2 * P], ACT.Identity,
                                         bias=l3g[:, 3:4], scale=l3g[:, 2:3]).then_inc(s.xt_sb, 1)
                    act.wait_ge(s.qkv_ps, n + 1)
                    at_least(act, s.ss, n)
                    for i in range(g3):
                        ins = nc.scalar.activation(sq[:, i * 256:(i + 1) * 256], bank[1 + i][:, 0:256], ACT.Square)
                    ins.then_inc(s.sq, 1)
                    at_least(act, s.o_ps, n - 1)
                    for i in range(g3):
                        ins = nc.scalar.copy(v3[:, u, i, :], bank[1 + i][:, 256:384])
                    ins.then_inc(s.v_sb, 1)
                if within(n, 1, N3 + 1):
                    act.wait_ge(s.qkt_ps, n)
                    at_least(act, s.s_ps, n - 1)
                    nc.scalar.activation(qT3, bank[3][:, 0:2 * P], ACT.Copy, scale=l3g[:, 5:6]).then_inc(s.qt_sb, 1)
                    nc.scalar.copy(kT3, bank[3][:, 2 * P:4 * P]).then_inc(s.kt_sb, 1)
                    act.wait_ge(s.shift, n)
                    e = sc3[:, 1 - u, :, :, :].rearrange("p t h j -> p (t h j)")
                    nc.scalar.activation(e, e, ACT.Exp, scale=HD ** -0.5).then_inc(s.ex, 1)
                    at_least(act, s.o_ps, n - 1)
                    for i in range(g3):
                        act.wait_ge(s.pt_ps, 2 * (n - 1) + i + 1)
                        nc.scalar.copy(pT3[0:S2, 4 * i * P:(4 * i + 2) * P], bank[4 + i][0:S2, 0:2 * P])
                        nc.scalar.copy(pT3[:, (4 * i + 2) * P:(4 * i + 4) * P], bank[4 + i][:, 2 * P:4 * P])\
                            .then_inc(s.pt_sb, 1)
                    act.wait_ge(s.o_ps, n)
                    at_least(act, s.y_ps, n - 1)
                    nc.scalar.copy(oT3, bank[7][:, 0:2 * P]).then_inc(s.o_sb, 1)

            steps(act, step, N3 + 1, 2, 3)
            phase_end(act)

        def attn3_pool(pool):
            s = s3
            phase_start(pool, PH3X)
            clear_last_phase(pool, PH3X)

            def rstds(n, u):
                ln_rstd(pool, s, n, u, g3)
                pool.wait_ge(s.mv2, (n + 1) * g3)
                pool.tensor_tensor(ve3, mv3[:, :, 1], epss[:, 0:2], ALU.add).then_inc(s.ve2, 1)
                pool.wait_ge(s.ve2, n + 1)
                pool.tensor_tensor(rs3, ve3, mhalf[:, 0:2], ALU.pow).then_inc(s.rstd2, 1)

            def step(n, u):
                if within(n, 0, N3):
                    rstds(n, u)
                    at_least(pool, s.s_ps, n - 1)
                    pool.tensor_copy(kcs[:, u, :], kc[:, ds(n * g3 * S2, g3 * S2)]).then_inc(s.ctx, 1)
                    at_least(pool, s.o_ps, n - 1)
                    pool.tensor_copy(vcs[:, u, :, :], vc[:, ds(n * g3, g3), :]).then_inc(s.xall, 1)
                    pool.wait_ge(s.sr, n + 1)
                    pool.tensor_tensor(sr2[:, :], sr[:, :], mhalf[:, 0:8], ALU.pow).then_inc(s.sr2, 1)

            steps(pool, step, N3 + 1, 2, 3)
            phase_end(pool)

        def attn3_dve(dve):
            s = s3
            phase_start(dve, PH3X)

            def step(n, u):
                if within(n, 0, N3):
                    ln_stats(dve, s, n, u, g3)
                    ln_apply(dve, s, n, u, g3, s.xt_ps)
                    for i in range(g3):
                        dve.wait_ge(s.xn, n + 1)
                        dve.bn_stats(bn3[:, i, :], xn[:, i, :]).then_inc(s.bn2, 1)
                    hold(dve, s.bn2, (n + 1) * g3)
                    for i in range(g3):
                        dve.bn_aggr(mv3[:, i, :], bn3[:, i, :]).then_inc(s.mv2, 1)
                    dve.wait_ge(s.rstd2, n + 1)
                    for i in range(g3):
                        ins = dve.tensor_scalar(xn3[:, i, :], xn[:, i, :], mv3[:, i, 0:1], rs3[:, i:i + 1],
                                                ALU.subtract, ALU.mult)
                    ins.then_inc(s.xn2, 1)
                if within(n, 1, N3 + 1):
                    m0 = (n - 1) * g3 * S2
                    mf = maskf[:, ds(m0, g3 * S2)].rearrange("p (t j) -> p t j", t=2)
                    mb = maskb[:, ds(m0, g3 * S2)].rearrange("p (t j) -> p t j", t=2)
                    e = sc3[:, 1 - u, :, :, :]
                    dve.wait_ge(s.s_ps, n)
                    at_least(dve, s.pt_ps, 2 * (n - 2))
                    ctop, ltop, mx = (top[:, 4 * k:4 * k + 4].rearrange("p (t h) -> p t h", t=2) for k in range(3))
                    for h in range(2):
                        dve.tensor_tensor(e[:, :, h, 0:S2], sbank(h)[:, :, 0:S2], mf, ALU.mult).then_inc(s.m1, 1)
                        dve.reduce_max(ltop[:, :, h], sbank(h)[:, :, S2:KL], AX.X).then_inc(s.m3, 1)
                    for h in range(2):
                        dve.wait_ge(s.m1, (n - 1) * 2 + h + 1)
                        dve.tensor_tensor(e[:, :, h, 0:S2], e[:, :, h, 0:S2], mb, ALU.add).then_inc(s.m2, 1)
                    dve.wait_ge(s.m2, n * 2)
                    dve.reduce_max(ctop, e[:, :, :, 0:S2], AX.X).then_inc(s.m3, 1)
                    dve.wait_ge(s.m3, n * 3)
                    dve.tensor_tensor(mx, ctop, ltop, ALU.max).then_inc(s.m4, 1)
                    dve.wait_ge(s.m4, n)
                    for h in range(2):
                        dve.tensor_tensor(e[:, :, h, 0:S2], e[:, :, h, 0:S2],
                                          mx[:, :, h].unsqueeze(2).to_broadcast([P, 2, S2]), ALU.subtract)
                        ins = dve.tensor_tensor(e[:, :, h, S2:KL], sbank(h)[:, :, S2:KL],
                                                mx[:, :, h].unsqueeze(2).to_broadcast([P, 2, P]), ALU.subtract)
                    ins.then_inc(s.shift, 1)
                if within(n, 0, N3):
                    dve.wait_ge(s.sq, n + 1)
                    dve.reduce_sum(ss[:, :], sq[:, :].rearrange("p (h d) -> p h d", d=HD), AX.X).then_inc(s.ss, 1)
                    dve.wait_ge(s.ss, n + 1)
                    dve.tensor_scalar(sr[:, :], ss[:, :], 1.0 / HD, RMS_EPS ** 2, ALU.mult, ALU.max).then_inc(s.sr, 1)
                if within(n, 1, N3 + 1):
                    dve.wait_ge(s.ex, n)
                    et = e.rearrange("p t h j -> p (t h) j")
                    dve.reduce_sum(tot[:, 0:4], et, AX.X).then_inc(s.tot, 1)
                    dve.wait_ge(s.tot, n)
                    dve.reciprocal(rec[:, 0:4], tot[:, 0:4]).then_inc(s.rec, 1)
                    dve.wait_ge(s.rec, n)
                    dve.tensor_tensor(et, et, rec[:, 0:4].unsqueeze(2).to_broadcast([P, 4, KL]),
                                      ALU.mult).then_inc(s.probs, 1)
                if within(n, 0, N3):
                    dve.wait_ge(s.sr2, n + 1)
                    dve.wait_ge(s.v_sb, n + 1)
                    at_least(dve, s.qkt_ps, n - 1)
                    for i in range(g3):
                        ins = dve.tensor_tensor(
                            qkn[:, u, i * 256:(i + 1) * 256].rearrange("p (h d) -> p h d", d=HD),
                            bank[1 + i][:, 0:256].rearrange("p (h d) -> p h d", d=HD),
                            sr2[:, 4 * i:4 * i + 4].unsqueeze(2).to_broadcast([P, 4, HD]), ALU.mult)
                    ins.then_inc(s.qk, 1)
                if within(n, 1, N3 + 1):
                    dve.wait_ge(s.y_ps, n)
                    x = X[:, ds((n - 1) * g3, g3), :]
                    dve.tensor_tensor(x, bank[7][:, 256:512].rearrange("p (t d) -> p t d", t=2), x, ALU.add)\
                       .then_inc(s.added, 1)
                    dve.wait_ge(s.added, n)
                    dve.tensor_tensor(x, x, l3bo[:, :].unsqueeze(1).to_broadcast([P, g3, D]), ALU.add)\
                       .then_inc(s.x, 1)

            steps(dve, step, N3 + 1, 2, 3)
            phase_end(dve)

        l3bo = sb("l3bo", [P, D])

        class Ffn:
            def __init__(self, layer, phase, experts, chunks, func, gated, ranks, router, biased):
                self.layer, self.phase, self.experts, self.chunks = layer, phase, experts, chunks
                self.func, self.gated, self.ranks, self.router, self.biased = func, gated, ranks, router, biased
                self.slots = {(4, False): 4, (1, False): 2, (4, True): 2, (3, True): 3}[chunks, gated]
                self.load = (loads.ffn0, loads.ffn1, loads.ffn2, loads.ffn3)[layer]
                self.s = stage[phase % 2]

        def chunk_at(f, g, c):
            return (g * f.chunks + c) % f.slots

        def up_bank(f, slot, half=0):
            return bank[2 * slot + half] if f.gated else bank[slot]

        def over_experts(eng, f, body):
            if f.experts == 1:
                body(0, 0, 0)
                return
            with eng.Fori(0, f.experts // 2) as i:
                for p in (0, 1):
                    body(i * 2 + p, p, i)

        def ffn_sp(sp, f, w1_of, w2_of, b1_of):
            s = f.s
            phase_start(sp, f.phase)

            def load(e, p, wait):
                if wait is not None:
                    sp.wait_ge(s.y_ps, wait)
                n = f.chunks * P * (2 if f.gated else 1)
                sp.dma_start(w1[:, p, 0:n], w1_of(e)).then_inc((s.w0, s.w1)[p], 16)
                sp.dma_start(w2[:, p, 0:f.chunks, :], w2_of(e)).then_inc((s.w0, s.w1)[p], 16)
                sp.dma_start(b1[:, p, 0:f.chunks], b1_of(e)).then_inc((s.w0, s.w1)[p], 16)

            load(0, 0, None)
            load(1, 1, None)
            with sp.Fori(1, f.experts // 2) as i:
                for p in (0, 1):
                    load(i * 2 + p, p, (i * 2 + p - 1) * NG + 2)

        def ffn_pe(pe, f):
            s, C, R = f.s, f.chunks, f.slots
            phase_start(pe, f.phase)
            pe.wait_ge(f.load, 16 * 2)

            def front(n, u):
                pe.wait_ge(s.xn, n + 1)
                at_least(pe, s.xt_sb, n)
                for i in range(G):
                    ins = pe.transpose(bank[0][:, i * P:(i + 1) * P], xn[:, i, :], ident[:, :])
                ins.then_inc(s.xt_ps, 1)
                if f.ranks:
                    pe.wait_ge(s.xt_sb, n + 1)
                    at_least(pe, s.lg, n - 1)
                    for i in range(G):
                        ins = pe.matmul(bank[1 + u][:, i * NE:(i + 1) * NE], xnT[:, u, i * P:(i + 1) * P],
                                        wr[:, f.layer, :], start=True, stop=True)
                    ins.then_inc(s.l_ps, 1)

            steps(pe, front, NG, 2, 2)
            if f.layer == 0:
                pe.wait_ge(s.gate_step, 16)
                pe.wait_ge(const.ready, 3)
                rhs = pick[:, :, :, :].rearrange("p e k b -> p (e k b)")
                pe.matmul(bank[3][:, :], upper[:, :], rhs, start=True, stop=True)
                pe.matmul(bank[4][:, :], ones[:, :], rhs, start=True, stop=True).then_inc(s.cnt_ps, 1)
            if f.biased:
                def bias(n, u):
                    pe.wait_ge(s.gb, n + 1)
                    at_least(pe, s.gt_sb, n)
                    for i in range(G):
                        ins = pe.transpose(bank[5][0:NE, i * P:(i + 1) * P], gb[:, i * NE:(i + 1) * NE], ident[:, :])
                    ins.then_inc(s.gt_ps, 1)
                    pe.wait_ge(s.gt_sb, n + 1)
                    at_least(pe, s.bb, n)
                    for i in range(G):
                        ins = pe.matmul(bank[6][:, i * D:(i + 1) * D], gT[:, i * P:(i + 1) * P], b2[:, f.layer, :],
                                        start=True, stop=True)
                    ins.then_inc(s.bb_ps, 1)

                steps(pe, bias, NG, 2, 2)
            if f.biased:
                pe.wait_ge(s.bb, NG)
            elif f.ranks:
                pe.wait_ge(s.lg, NG)
            pe.wait_ge(s.xall, NG)
            pe.sem_inc(s.y_ps, 2)

            def expert(e, p, i):
                if f.experts == 1:
                    pe.wait_ge(s.w0, 1)
                else:
                    pe.wait_ge((s.w0, s.w1)[p], i * 48 + 48)

                def step(g, u):
                    it = e * NG + g
                    if within(g, 0, NG):
                        for c in range(C):
                            slot = chunk_at(f, u, c)
                            pe.wait_ge(s.h, it * C + c + 1)
                            for half in range(2 if f.gated else 1):
                                o = (half * C + c) * P
                                ins = pe.matmul(up_bank(f, slot, half)[:, :], w1[:, p, o:o + P],
                                                xall[:, ds(g * G * P, G * P)], start=True, stop=True)
                            ins.then_inc(s.up_ps, 1)
                    if within(g, 1, NG + 1):
                        pe.wait_ge(s.h, it * C + R)
                        pe.wait_ge(s.x, it)
                        for i in range(G):
                            for c in range(C):
                                ins = pe.matmul(bank[6 + (1 - u)][:, i * D:(i + 1) * D],
                                                hid[:, 1 - u, c, i * P:(i + 1) * P], w2[:, p, c, :],
                                                start=(c == 0), stop=(c == C - 1))
                        ins.then_inc(s.y_ps, 1)

                steps(pe, step, NG + 1, 2, 1)

            over_experts(pe, f, expert)
            phase_end(pe)

        def ffn_act(act, f):
            s, C, R = f.s, f.chunks, f.slots
            phase_start(act, f.phase)

            def front(n, u):
                act.wait_ge(s.xt_ps, n + 1)
                at_least(act, s.xall, n - 1)
                if f.ranks:
                    at_least(act, s.l_ps, n - 1)
                nc.scalar.copy(xnT[:, u, :], bank[0][:, :]).then_inc(s.xt_sb, 1)

            steps(act, front, NG, 2, 2)
            if f.ranks:
                act.wait_ge(s.gate_step, 2)
                nc.scalar.activation(ga[:, :, :], gc[:, :, :], ACT.Exp).then_inc(s.ex, 1)
            if f.biased:
                def bias(n, u):
                    act.wait_ge(s.gt_ps, n + 1)
                    at_least(act, s.bb_ps, n)
                    nc.scalar.copy(gT[:, :], bank[5][0:NE, :]).then_inc(s.gt_sb, 1)

                steps(act, bias, NG, 2, 2)
            if not f.gated:
                act.sem_inc(s.h, R)

            def expert(e, p, i):
                if f.experts > 1:
                    act.wait_ge((s.w0, s.w1)[p], i * 48 + 48)

                def step(g, u):
                    it = e * NG + g
                    act.wait_ge(s.y_ps, it + 1)
                    for c in range(C):
                        src = up_bank(f, chunk_at(f, u, c))[:, :]
                        act.wait_ge(s.up_ps, it * C + c + 1)
                        if f.gated:
                            act.wait_ge(s.h, it * C + c - 1 + R)
                            nc.scalar.activation(silu[:, c % 2 if C % 2 == 0 else (u + c) % 2, :], src,
                                                 ACT.Silu).then_inc(s.act, 1)
                        elif f.biased:
                            nc.scalar.activation(hid[:, u, c, :], src, f.func, bias=b1[:, p, c:c + 1])\
                                .then_inc(s.h, 1)

                steps(act, step, NG, 2, 2)

            over_experts(act, f, expert)
            phase_end(act)

        def ffn_pool(pool, f):
            s = f.s
            phase_start(pool, f.phase)
            clear_last_phase(pool, f.phase)
            ln_rstd(pool, s, 0, 0, G)

            def front(n, u):
                if within(n, 0, NG - 1):
                    ln_rstd(pool, s, n + 1, 1 - u, G)
                pool.wait_ge(s.xt_sb, n + 1)
                pool.tensor_copy(xall[:, ds(n * G * P, G * P)], xnT[:, u, :]).then_inc(s.xall, 1)

            steps(pool, front, NG, 2, 2)
            phase_end(pool)

        def softmax_and_choice(dve, f):
            s = f.s
            done = [0]

            def link(ins):
                done[0] += 1
                ins.then_inc(s.gate_step, 1)
                dve.wait_ge(s.gate_step, done[0])

            def per_expert(ap):
                return ap.unsqueeze(2).to_broadcast([P, NB, NE])

            src = lg[:, :, :]
            dve.wait_ge(s.lg, NG)
            link(dve.reduce_max(gtmp[:, :], src, AX.X))
            link(dve.tensor_tensor(gc[:, :, :], src, per_expert(gtmp[:, :]), ALU.subtract))
            dve.wait_ge(s.ex, 1)
            link(dve.reduce_sum(gtmp[:, :], ga[:, :, :], AX.X))
            link(dve.reciprocal(gtmp[:, :], gtmp[:, :]))
            link(dve.tensor_tensor(ga[:, :, :], ga[:, :, :], per_expert(gtmp[:, :]), ALU.mult))
            for r in range(f.ranks):
                link(dve.reduce_max(gtop[:, r, :], ga[:, :, :], AX.X))
                link(dve.tensor_tensor(gc[:, :, :], ga[:, :, :], per_expert(gtop[:, r, :]), ALU.is_equal))
                link(dve.tensor_tensor(gc[:, :, :], gc[:, :, :],
                                       order[:, :].unsqueeze(1).to_broadcast([P, NB, NE]), ALU.mult))
                link(dve.reduce_max(gtmp[:, :], gc[:, :, :], AX.X))
                chosen = pick[:, :, r, :].rearrange("p e b -> p b e")
                link(dve.tensor_tensor(chosen, gc[:, :, :], per_expert(gtmp[:, :]), ALU.is_equal))
                if r + 1 < f.ranks:
                    link(dve.scalar_tensor_tensor(out=ga[:, :, :], in0=chosen, scalar=-2.0, in1=ga[:, :, :],
                                                  op0=ALU.mult, op1=ALU.add))
            if f.layer == 0:
                assert done[0] == 16
                flat = pick[:, :, :, :].rearrange("p e k b -> p (e k b)")
                link(dve.tensor_tensor(gtmp[:, :], gtop[:, 0, :], gtop[:, 1, :], ALU.add))
                link(dve.reciprocal(gtmp[:, :], gtmp[:, :]))
                link(dve.tensor_tensor(gtop[:, :, :], gtop[:, :, :],
                                       gtmp[:, :].unsqueeze(1).to_broadcast([P, 2, NB]), ALU.mult))
                dve.wait_ge(s.cnt_ps, 1)
                link(dve.tensor_tensor_scan(pref[:, :], first[:, :], bank[4][:, :], 0.0, ALU.mult, ALU.add))
                link(dve.tensor_tensor(pref[:, :], pref[:, :], bank[4][:, :], ALU.subtract))
                link(dve.tensor_tensor(pref[:, :], pref[:, :], bank[3][:, :], ALU.add))
                link(dve.tensor_scalar(pref[:, :], pref[:, :], float(CAP), None, ALU.is_le))
                link(dve.tensor_tensor(flat, flat, pref[:, :], ALU.mult))
            out_view = gates[:, :, :]
            for r in range(f.ranks):
                link(dve.tensor_tensor(pick[:, :, r, :], pick[:, :, r, :],
                                       gtop[:, r, :].unsqueeze(1).to_broadcast([P, NE, NB]), ALU.mult))
            if f.ranks == 2:
                link(dve.tensor_tensor(out_view, pick[:, :, 0, :].rearrange("p e b -> p b e"),
                                       pick[:, :, 1, :].rearrange("p e b -> p b e"), ALU.add))
            else:
                link(dve.tensor_copy(out_view, pick[:, :, 0, :].rearrange("p e b -> p b e")))

        gate_of = gates[:, :, :].rearrange("p b e -> p (b e)")

        def ffn_dve(dve, f):
            s, C, R = f.s, f.chunks, f.slots
            phase_start(dve, f.phase)
            dve.wait_ge(f.load, 16 * 2)
            ln_stats(dve, s, 0, 0, G)
            ln_apply(dve, s, 0, 0, G, s.xt_ps)
            if f.layer == 3:
                w1i, w2i = lay3.w1i, lay3.w2i
                dve.tensor_scalar(w1[:, 0, 0:768], w1i, 1.0 / 127.0, None, ALU.mult)
                dve.tensor_scalar(w2[:, 0, 0:3, :], w2i, 1.0 / 127.0, None, ALU.mult).then_inc(s.w0, 1)

            def front(n, u):
                if within(n, 0, NG - 1):
                    ln_stats(dve, s, n + 1, 1 - u, G)
                    ln_apply(dve, s, n + 1, 1 - u, G, s.xt_ps)
                if f.ranks:
                    dve.wait_ge(s.l_ps, n + 1)
                    dst = lg[:, ds(n * G, G), :]
                    src = bank[1 + u][:, 0:G * NE].rearrange("p (g e) -> p g e", g=G)
                    if f.layer == 2:
                        dve.tensor_tensor(dst, src, rb[:, :].unsqueeze(1).to_broadcast([P, G, NE]), ALU.add)\
                           .then_inc(s.lg, 1)
                    else:
                        dve.tensor_copy(dst, src).then_inc(s.lg, 1)

            steps(dve, front, NG, 2, 2)
            if f.ranks:
                softmax_and_choice(dve, f)
            if f.biased:
                def bias(n, u):
                    at_least(dve, s.gt_ps, n)
                    dve.tensor_copy(gb[:, :], gates[:, ds(n * G, G), :].rearrange("p g e -> p (g e)"))\
                       .then_inc(s.gb, 1)
                    dve.wait_ge(s.bb_ps, n + 1)
                    x = X[:, ds(n * G, G), :]
                    dve.tensor_tensor(x, bank[6][:, :].rearrange("p (g d) -> p g d", g=G), x, ALU.add)\
                       .then_inc(s.bb, 1)

                steps(dve, bias, NG, 2, 2)
                dve.wait_ge(s.bb, NG)
            dve.sem_inc(s.x, 2)
            if f.gated:
                dve.sem_inc(s.h, R)

            def expert(e, p, i):
                def step(g, u):
                    it = e * NG + g
                    if f.gated and within(g, 0, NG):
                        dve.wait_ge(s.y_ps, it + 1)
                        for c in range(C):
                            dve.wait_ge(s.act, it * C + c + 1)
                            dve.tensor_tensor(hid[:, u, c, :], up_bank(f, chunk_at(f, u, c), 1)[:, :],
                                              silu[:, c % 2 if C % 2 == 0 else (u + c) % 2, :], ALU.mult)\
                               .then_inc(s.h, 1)
                    if within(g, 1, NG + 1):
                        y = bank[6 + (1 - u)][:, :].rearrange("p (g d) -> p g d", g=G)
                        dve.wait_ge(s.y_ps, it + 2)
                        dve.wait_ge(s.x, it + 1)
                        if f.ranks:
                            for i in range(G):
                                x = tile((g - 1) * G + i)
                                gate = gate_of[:, ds(((g - 1) * G + i) * NE + e, 1)]
                                ins = dve.scalar_tensor_tensor(out=x, in0=y[:, i, :], scalar=gate, in1=x, op0=ALU.mult, op1=ALU.add)
                        else:
                            x = X[:, ds((g - 1) * G, G), :]
                            ins = dve.tensor_tensor(x, y, x, ALU.add)
                        ins.then_inc(s.x, 1)

                steps(dve, step, NG + 1, 2, 1)

            over_experts(dve, f, expert)
            phase_end(dve)

        attn = [Attention(0, 0, 8), Attention(1, 2, 16)]
        ffn = [Ffn(0, 1, NE, 4, ACT.Relu, False, 2, True, True),
               Ffn(1, 3, NE, 1, ACT.Gelu_apprx_tanh, False, 2, True, True),
               Ffn(2, 5, NE, 4, ACT.Silu, True, 1, True, False),
               Ffn(3, 8, 1, 3, ACT.Silu, True, 0, False, False)]

        class lay3:
            w1i = raw[:, 9216:9984].bitcast(I32)
            w2i = raw[:, 9984:10368].bitcast(I32).rearrange("p (c d) -> p c d", c=3)

        def row(ap, e):
            return ap[ds(e, 1)].rearrange("a p n -> (a p) n")

        def expert_w2(ap, e):
            return ap[ds(e, 1)].rearrange("a p c d -> (a p) c d")

        def small():
            sp = nc.sync
            for i in range(3):
                q = f"L{i}_"
                sp.dma_start(obias[:, i, :], t[q + "bo"].partition_broadcast(P)).then_inc(const.bias, 16)
            for i in range(2):
                sp.dma_start(wr[:, i, :], t[f"L{i}_wr"]).then_inc(ffn[i].load, 16)
                sp.dma_start(b2[:, i, :], t[f"L{i}_b2"]).then_inc(ffn[i].load, 16)
            sp.dma_start(wr[:, 2, :], t["L2_wr"]).then_inc(loads.ffn2, 16)
            sp.dma_start(rb[:, :], t["L2_rb"].partition_broadcast(P)).then_inc(loads.ffn2, 16)
            sp.dma_start(l2w[:, 0, :], t["L2_wq"]).then_inc(loads.l2, 16)
            sp.dma_start(l2w[0:DC, 1, :], t["L2_wk"]).then_inc(loads.l2, 16)
            sp.dma_start(l2w[0:DC, 2, :], t["L2_wv"]).then_inc(loads.l2, 16)
            sp.dma_start(l2b[:, 0:1], t["L2_bq"]).then_inc(loads.l2, 16)
            sp.dma_start(l2b[:, 1:2], t["L2_bk"]).then_inc(loads.l2, 16)
            for i, name in enumerate(("ln_x_g", "ln_x_b")):
                sp.dma_start(l3g[0:DC, i:i + 1], t["L3_" + name]).then_inc(loads.l3, 16)
            for i, name in enumerate(("ln_l_g", "ln_l_b", "qn_g")):
                sp.dma_start(l3g[:, 2 + i:3 + i], t["L3_" + name]).then_inc(loads.l3, 16)
            sp.dma_start(l3g[:, 6:7], t["L3_kn_g"]).then_inc(loads.l3, 16)
            sp.dma_start(l3w[:, 0:384], t["L3_wl"]).then_inc(loads.l3, 16)
            sp.dma_start(l3w[0:DC, 384:640], t["L3_wkv"]).then_inc(loads.l3, 16)
            sp.dma_start(l3w[:, 640:768], t["L3_wo"]).then_inc(loads.l3, 16)
            sp.dma_start(l3bo[:, :], t["L3_bo"].partition_broadcast(P)).then_inc(const.bias, 16)

        block = ctx.enter_context(nc.Block())

        @block.sync
        def _(sp):
            sp.dma_start(X[:, :, :], t["x"].rearrange("b s d -> s b d")).then_inc(loads.x, 16)
            sp.dma_start(ctxT[:, :], t["ctxT"]).then_inc(loads.x, 16)
            for a in attn:
                q = f"L{a.layer}_"
                sp.dma_start(a.wqT, t[q + "wqT"]).then_inc(a.load, 16)
                sp.dma_start(a.wkT, t[q + "wkT"]).then_inc(a.load, 16)
                sp.dma_start(a.wvT, t[q + "wvT"]).then_inc(a.load, 16)
                sp.dma_start(a.woh, t[q + "wo"]).then_inc(a.load, 16)
                if a.layer == 0:
                    small()
            ffn_sp(sp, ffn[0], lambda e: row(t["L0_w1"], e), lambda e: expert_w2(t["L0_w2"], e),
                   lambda e: row(t["L0_b1"], e))
            ffn_sp(sp, ffn[1], lambda e: row(t["L1_w1"], e), lambda e: expert_w2(t["L1_w2"], e),
                   lambda e: row(t["L1_b1"], e))
            phase_start(sp, ffn[2].phase)
            sp.dma_start(ctxn, t["ctx"].rearrange("b s c -> s b c")).then_inc(loads.ctxn, 16)
            sp.dma_start(mask8[:, :], t["mask"].partition_broadcast(P)).then_inc(loads.ctxn, 16)
            sp.dma_start(lay3.w1i, t["L3_w1"]).then_inc(loads.ffn3, 16)
            sp.dma_start(lay3.w2i, t["L3_w2"]).then_inc(loads.ffn3, 16)
            ffn_sp(sp, ffn[2], lambda e: row(t["L2_w1"], e), lambda e: expert_w2(t["L2_w2"], e),
                   lambda e: row(t["L0_b1"], e))
            phase_start(sp, 9)
            sp.dma_start(out.rearrange("b s d -> s b d"), X[:, :, :]).then_inc(loads.out, 16)
            sp.wait_ge(loads.out, 16)

        @block.gpsimd
        def _(pool):
            pool.memset(mhalf[:, :], -0.5).then_inc(const.zero, 1)
            pool.memset(ones[:, :], 1.0).then_inc(const.zero, 1)
            pool.memset(epss[:, :], EPS).then_inc(const.zero, 1)
            pool.memset(first[:, :], 1.0).then_inc(const.zero, 1)
            pool.memset(ident[:, :], 0.0).then_inc(const.zero, 1)
            pool.wait_ge(const.zero, 5)
            pool.affine_select(out=ident[:, :], in_=ident[:, :], compare_op=ALU.not_equal, fill=1.0, base=0,
                               pattern=[[-1, P]], channel_multiplier=1).then_inc(const.ready, 1)
            pool.affine_select(out=upper[:, :], in_=ones[:, :], compare_op=ALU.is_ge, fill=0.0, base=0,
                               pattern=[[1, P]], channel_multiplier=-1).then_inc(const.ready, 1)
            pool.memset(first[:, :].rearrange("p (e n) -> p e n", e=NE)[:, :, 0:1], 0.0).then_inc(const.ready, 1)
            for e in range(NE):
                pool.memset(order[:, e:e + 1], float(NE - e)).then_inc(const.order, 1)
            attn_pool(pool, attn[0])
            ffn_pool(pool, ffn[0])
            attn_pool(pool, attn[1])
            ffn_pool(pool, ffn[1])
            attn2_pool(pool)
            ffn_pool(pool, ffn[2])
            ctx3_pool(pool)
            attn3_pool(pool)
            ffn_pool(pool, ffn[3])

        @block.scalar
        def _(act):
            attn_act(act, attn[0])
            ffn_act(act, ffn[0])
            attn_act(act, attn[1])
            ffn_act(act, ffn[1])
            attn2_act(act)
            ffn_act(act, ffn[2])
            ctx3_act(act)
            attn3_act(act)
            ffn_act(act, ffn[3])

        @block.vector
        def _(dve):
            dve.wait_ge(const.bias, 16 * 4)
            dve.wait_ge(const.ready, 3)
            dve.wait_ge(const.order, NE)
            attn_dve(dve, attn[0])
            ffn_dve(dve, ffn[0])
            attn_dve(dve, attn[1])
            ffn_dve(dve, ffn[1])
            attn2_dve(dve)
            ffn_dve(dve, ffn[2])
            ctx3_dve(dve)
            attn3_dve(dve)
            ffn_dve(dve, ffn[3])

        @block.tensor
        def _(pe):
            attn_pe(pe, attn[0])
            ffn_pe(pe, ffn[0])
            attn_pe(pe, attn[1])
            ffn_pe(pe, ffn[1])
            attn2_pe(pe)
            ffn_pe(pe, ffn[2])
            ctx3_pe(pe)
            attn3_pe(pe)
            ffn_pe(pe, ffn[3])


_OUT = (NB, P, D)


def kernel(**inputs):
    import numpy as np
    import concourse.bacc as bacc
    from concourse.bass_utils import run_bass_kernel_spmd as run

    a = {k: np.asarray(v) for k, v in inputs.items()}

    def heads(w):
        return w.reshape(w.shape[0], -1, HD).transpose(2, 1, 0)

    def second(w):
        return w.reshape(w.shape[0], -1, P, D).transpose(0, 2, 1, 3)

    def hidden_bias(b):
        return b.reshape(b.shape[0], -1, P).transpose(0, 2, 1)

    arrays = {
        "x": a["x"], "ctx": a["ctx_768"],
        "ctxT": a["ctx_768"].transpose(2, 0, 1).reshape(DC, NB * S2),
        "mask": a["mask_BxS2_bk0"].reshape(NB * S2),
        "L0_w1": a["L0_ffn_w1"], "L0_w2": second(a["L0_ffn_w2"]), "L0_b1": hidden_bias(a["L0_ffn_b1"]),
        "L0_b2": a["L0_ffn_b2"], "L0_wr": a["L0_ffn_wg"],
        "L1_w1": a["L1_ffn_w_in"], "L1_w2": second(a["L1_ffn_w_out"]), "L1_b1": hidden_bias(a["L1_ffn_b_in"]),
        "L1_b2": a["L1_ffn_b_out"], "L1_wr": a["L1_ffn_router_w"],
        "L2_w1": a["L2_ffn_w1"], "L2_w2": second(a["L2_ffn_w2"]), "L2_wr": a["L2_ffn_router_w"],
        "L2_rb": a["L2_ffn_router_b"],
        "L2_wq": a["L2_xattn_Wq"], "L2_wk": a["L2_xattn_Wk"], "L2_wv": a["L2_xattn_Wv"],
        "L2_bq": a["L2_xattn_bq"].reshape(D, 1), "L2_bk": a["L2_xattn_bk"].reshape(D, 1),
        "L2_bo": a["L2_xattn_bv"],
        "L3_ln_x_g": a["L3_xattn_ln_x_g"].reshape(DC, 1), "L3_ln_x_b": a["L3_xattn_ln_x_b"].reshape(DC, 1),
        "L3_ln_l_g": a["L3_xattn_ln_l_g"].reshape(D, 1), "L3_ln_l_b": a["L3_xattn_ln_l_b"].reshape(D, 1),
        "L3_qn_g": np.tile(a["L3_xattn_qn_g"], 2).reshape(D, 1),
        "L3_kn_g": np.tile(a["L3_xattn_kn_g"], 2).reshape(D, 1),
        "L3_wl": np.concatenate([a["L3_xattn_Wq"], a["L3_xattn_Wlkv"]], 0).T,
        "L3_wkv": a["L3_xattn_Wkv"].T, "L3_wo": a["L3_xattn_Wo"].T, "L3_bo": a["L3_xattn_bo"],
        "L3_w1": np.concatenate([a["L3_ffn_w_gate"], a["L3_ffn_w_up"]], 0).T,
        "L3_w2": a["L3_ffn_w_down"].T.reshape(3, P, D).transpose(1, 0, 2),
    }
    for i in (0, 1):
        q = f"L{i}_xattn_"
        arrays |= {f"L{i}_wqT": heads(a[q + "Wq"]), f"L{i}_wkT": heads(a[q + "Wk"]), f"L{i}_wvT": heads(a[q + "Wv"]),
                   f"L{i}_wo": a[q + "Wo"].reshape(-1, HD, D).transpose(1, 0, 2), f"L{i}_bo": a[q + "bo"]}
    arrays = {k: np.ascontiguousarray(v) for k, v in arrays.items()}

    nc = bacc.Bacc("TRN2", target_bir_lowering=False, num_devices=1)
    t = {k: nc.dram_tensor("in_" + k, v.shape, mybir.dt.from_np(v.dtype), kind="ExternalInput").ap()
         for k, v in arrays.items()}
    out = nc.dram_tensor("out_dram", _OUT, F32, kind="ExternalOutput").ap()
    build(nc, t, out)
    return run(nc, [{"in_" + k: v for k, v in arrays.items()}], core_ids=[0]).results[0]["out_dram"]
```

```python
from contextlib import ExitStack

import concourse.bass as bass
from concourse import mybir

F32 = mybir.dt.float32
I32 = mybir.dt.int32
U8 = mybir.dt.uint8
U32 = mybir.dt.uint32
ALU = mybir.AluOpType
ACT = mybir.ActivationFunctionType
AX = mybir.AxisListType
ds = bass.ds

P = 128
NB = 32
D = 128
S2 = 77
DC = 96
HD = 64
NE = 8
G = 4
NG = NB // G
CAP = 2 * NB * P // NE
NT = NB + NE - 1
SPARE = NE * CAP
EPS = 1e-5
RMS_EPS = 1e-8
FLT_MAX = 3.4028234663852886e38
BANK = 512
ENGINES = 4


def at_least(eng, sem, value):
    if isinstance(value, int) and value <= 0:
        return
    eng.wait_ge(sem, value)


def within(n, low, high):
    return not isinstance(n, int) or low <= n < high


def steps(eng, step, total, head, tail, by=2):
    for n in range(head):
        step(n, n % by)
    with eng.Fori(head // by, (total - tail) // by) as i:
        for u in range(by):
            step(i * by + u, u)
    for n in range(total - tail, total):
        step(n, n % by)


class Stage:

    def __init__(self, sem):
        self.bn = sem("bn")
        self.mv = sem("mv")
        self.ve = sem("ve")
        self.rstd = sem("rstd")
        self.xn = sem("xn")
        self.xt_ps = sem("xt_ps")
        self.xt_sb = sem("xt_sb")
        self.xall = sem("xall")
        self.ctx = sem("ctx")
        self.fold_ps = sem("fold_ps")
        self.fold_sb = sem("fold_sb")
        self.q_ps = sem("q_ps")
        self.q_sb = sem("q_sb")
        self.k_ps = sem("k_ps")
        self.k_sb = sem("k_sb")
        self.v_ps = sem("v_ps")
        self.v_sb = sem("v_sb")
        self.t_ps = sem("t_ps")
        self.t_sb = sem("t_sb")
        self.qkv_ps = sem("qkv_ps")
        self.sq = sem("sq")
        self.ss = sem("ss")
        self.sr = sem("sr")
        self.sr2 = sem("sr2")
        self.qk = sem("qk")
        self.qkt_ps = sem("qkt_ps")
        self.qt_sb = sem("qt_sb")
        self.kt_ps = sem("kt_ps")
        self.kt_sb = sem("kt_sb")
        self.s_ps = sem("s_ps")
        self.m1 = sem("m1")
        self.m2 = sem("m2")
        self.m3 = sem("m3")
        self.m4 = sem("m4")
        self.top = sem("top")
        self.shift = sem("shift")
        self.ex = sem("ex")
        self.tot = sem("tot")
        self.rec = sem("rec")
        self.probs = sem("probs")
        self.pt_ps = sem("pt_ps")
        self.pt_sb = sem("pt_sb")
        self.o_ps = sem("o_ps")
        self.o_sb = sem("o_sb")
        self.mask = sem("mask")
        self.l_ps = sem("l_ps")
        self.lg = sem("lg")
        self.gate_step = sem("gate_step")
        self.cnt_ps = sem("cnt_ps")
        self.gb = sem("gb")
        self.gt_ps = sem("gt_ps")
        self.gt_sb = sem("gt_sb")
        self.bb_ps = sem("bb_ps")
        self.bb = sem("bb")
        self.w0 = sem("w0")
        self.w1 = sem("w1")
        self.up_ps = sem("up_ps")
        self.act = sem("act")
        self.h = sem("h")
        self.zeroed = self.t_ps
        self.counts = self.t_sb
        self.in0, self.in1 = self.q_sb, self.k_ps
        self.in_ps, self.in_sb = self.k_sb, self.v_ps
        self.ht_ps, self.ht_sb = self.v_sb, self.pt_ps
        self.y_sb = self.pt_sb
        self.out0, self.out1 = self.sq, self.ss
        self.first_added = self.qt_sb
        self.bn2, self.mv2, self.ve2, self.rstd2, self.xn2 = self.l_ps, self.lg, self.gt_ps, self.gt_sb, self.bb_ps
        self.y_ps = sem("y_ps")
        self.added = sem("added")
        self.x = sem("x")


class Loads:

    def __init__(self, sem):
        self.x = sem("x")
        self.attn0 = sem("attn0")
        self.attn1 = sem("attn1")
        self.l2 = sem("l2")
        self.ffn0 = sem("ffn0")
        self.ffn1 = sem("ffn1")
        self.ffn2 = sem("ffn2")
        self.ffn3 = sem("ffn3")
        self.l3 = sem("l3")
        self.ctxn = sem("ctxn")
        self.out = sem("out")
        self.scattered = sem("scattered")
        self.gathered = [sem(f"gathered{q}") for q in range(4)]


class Constants:

    def __init__(self, sem):
        self.zero = sem("zero")
        self.order = sem("order")
        self.ready = sem("ready")
        self.bias = sem("bias")
        self.cleared = sem("cleared")
        self.slots = sem("slots")


def build(nc, t, out):
    with ExitStack() as ctx:
        def sb(name, shape, dt=F32):
            return ctx.enter_context(nc.sbuf_tensor("sb_" + name, shape, dt))

        X = sb("X", [P, NB, D])
        ctxT = sb("ctxT", [DC, NB * S2])
        ident = sb("ident", [P, P])
        raw = sb("raw", [P, 10752])
        work = sb("work", [P, 5600])
        score = sb("score", [P, 2, 16 * S2])
        fold = sb("fold", [P, 16 * P + 16 * D])
        foldT = fold[0:DC, 0:16 * P]
        foldV = fold[0:DC, 16 * P:]
        ctx_b = sb("ctx_b", [DC, 2, G * S2])
        xn = sb("xn", [P, G, D])
        xnT = sb("xnT", [P, 2, G * P])
        bnst = sb("bnst", [P, 2, G, 6])
        mv = sb("mv", [P, 2, G, 2])
        ve = sb("ve", [P, 2, G])
        rstd = sb("rstd", [P, 2, G])
        mhalf = sb("mhalf", [P, NB])
        epss = sb("epss", [P, G])
        top = sb("top", [P, 16])
        tot = sb("tot", [P, 16])
        rec = sb("rec", [P, 16])
        obias = sb("obias", [P, 3, D])
        xall = sb("xall", [P, NB * P])
        hid = sb("hid", [P, 2, 4, BANK])
        w1 = sb("w1", [P, 2, 1024])
        w2 = sb("w2", [P, 2, 4, D])
        b1 = sb("b1", [P, 2, 4])
        silu = sb("silu", [P, 2, BANK])
        b2 = sb("b2", [NE, 2, D])
        gates = sb("gates", [P, NB, NE])
        gb = sb("gb", [P, G * NE])
        gT = sb("gT", [NE, G * P])
        wr = sb("wr", [P, 3, NE])
        rb = sb("rb", [P, NE])
        lg = sb("lg", [P, NB, NE])
        ga = sb("ga", [P, NB, NE])
        gc = sb("gc", [P, NB, NE])
        pick = sb("pick", [P, NE, 2, NB])
        pref = sb("pref", [P, NE * 2 * NB])
        first = sb("first", [P, NE * 2 * NB])
        gtop = sb("gtop", [P, 2, NB])
        gtmp = sb("gtmp", [P, NB])
        order = sb("order", [P, NE])
        upper = sb("upper", [P, P])
        ones = sb("ones", [P, P])
        l2w = sb("l2w", [P, 3, D])
        l2b = sb("l2b", [P, 2])
        qkn = sb("qkn", [P, 2, G * P])
        l3g = sb("l3g", [P, 8])
        l3w = sb("l3w", [P, 384 + 256 + 128])
        sq = sb("sq", [P, 512])
        ss = sb("ss", [P, 8])
        sr = sb("sr", [P, 8])
        sr2 = sb("sr2", [P, 8])
        mask8 = sb("mask8", [P, NB * S2], U8)

        bank = [ctx.enter_context(nc.psum_tensor(f"bank{i}", [P, BANK], F32)) for i in range(8)]

        def sems(kind, prefix):
            return kind(lambda n: ctx.enter_context(nc.semaphore(f"{prefix}_{n}")))

        stage = [sems(Stage, "even"), sems(Stage, "odd")]
        passed = ctx.enter_context(nc.semaphore("passed"))
        phase_done = ctx.enter_context(nc.semaphore("phase_done"))
        loads = sems(Loads, "load")
        const = sems(Constants, "const")

        def phase_start(eng, k):
            if k > 0:
                eng.wait_ge(phase_done, ENGINES * k)

        def clear_last_phase(pool, k):
            if k > 0:
                old = stage[(k - 1) % 2]
                pool.sem_clear(range(old.bn.num, old.x.num + 1))

        def phase_end(eng):
            eng.drain().then_inc(phase_done, 1)

        slots_x = nc.dram_tensor("slots_x", (SPARE + 2 * NB * P, D), F32, kind="Internal").ap()
        slots_y = nc.dram_tensor("slots_y", (SPARE, D), F32, kind="Internal").ap()

        def tile(n):
            return X[:, ds(n, 1), :].rearrange("p a d -> p (a d)")


        def hold(dve, sem, value):
            dve.wait_ge(sem, value)
            dve.sem_inc(passed, 1)

        def ln_stats(dve, s, n, u, g):
            for i in range(g):
                dve.bn_stats(bnst[:, u, i, :], tile(n * g + i)).then_inc(s.bn, 1)
            hold(dve, s.bn, (n + 1) * g)
            for i in range(g):
                dve.bn_aggr(mv[:, u, i, :], bnst[:, u, i, :]).then_inc(s.mv, 1)

        def ln_rstd(pool, s, n, u, g):
            pool.wait_ge(s.mv, (n + 1) * g)
            pool.tensor_tensor(ve[:, u, 0:g], mv[:, u, 0:g, 1], epss[:, 0:g], ALU.add).then_inc(s.ve, 1)
            pool.wait_ge(s.ve, n + 1)
            pool.tensor_tensor(rstd[:, u, 0:g], ve[:, u, 0:g], mhalf[:, 0:g], ALU.pow).then_inc(s.rstd, 1)

        def ln_apply(dve, s, n, u, g, transposed):
            dve.wait_ge(s.rstd, n + 1)
            at_least(dve, transposed, n)
            for i in range(g):
                ins = dve.tensor_scalar(xn[:, i, :], tile(n * g + i), mv[:, u, i, 0:1],
                                        rstd[:, u, i:i + 1], ALU.subtract, ALU.mult)
            ins.then_inc(s.xn, 1)

        class Attention:
            def __init__(self, layer, phase, heads):
                self.layer, self.phase, self.heads = layer, phase, heads
                self.chunks = heads // 4
                self.load = (loads.attn0, loads.attn1)[layer]
                o = 0 if layer else 7168
                self.wqT = raw[0:HD, o:o + heads * D].rearrange("p (h d) -> p h d", h=heads)
                self.woh = raw[HD:P, o:o + heads * D].rearrange("p (h d) -> p h d", h=heads)
                o += heads * D
                self.wkT = raw[0:HD, o:o + heads * DC].rearrange("p (h d) -> p h d", h=heads)
                self.wvT = raw[HD:P, o:o + heads * DC].rearrange("p (h d) -> p h d", h=heads)
                self.bias = obias[:, layer, :]
                self.s = stage[phase % 2]

        keys = work[:, 0:1232]
        vals = work[0:S2, 1232:3280]
        probsT = work[0:S2, 3280:5328]
        RING = (4, 5, 6)

        def ring(a, kind, c):
            return bank[RING[(kind * a.chunks + c) % 3]]

        def ring_free(pe, a, n, kind, c):
            s, k = a.s, kind * a.chunks + c - 3
            back = 0
            if k < 0:
                k, back = k + 3 * a.chunks, 1
            was, c0 = k // a.chunks, k % a.chunks
            if was == 0 and not within(n, 0, NB):
                return at_least(pe, s.pt_sb, (n - 1) * a.chunks)
            done = (s.t_sb, s.v_sb, s.pt_sb)[was]
            at_least(pe, done, (n - back - (1 if was else 0)) * a.chunks + c0 + 1)

        def attn_fold_pe(pe, a):
            s = a.s
            pe.wait_ge(a.load, 16 * 4)
            pe.wait_ge(const.ready, 3)
            for j in range(2 * a.chunks):
                if j >= 3:
                    pe.wait_ge(s.fold_sb, j - 2)
                for i in range(4):
                    h = 4 * (j % a.chunks) + i
                    lhs, rhs = (a.wkT, a.wqT) if j < a.chunks else (a.wvT, a.woh)
                    ins = pe.matmul(bank[RING[j % 3]][0:DC, i * D:(i + 1) * D], lhs[:, h, :], rhs[:, h, :],
                                    start=True, stop=True)
                ins.then_inc(s.fold_ps, 1)
            pe.wait_ge(s.fold_sb, 2 * a.chunks)

        def attn_fold_act(act, a):
            for j in range(2 * a.chunks):
                act.wait_ge(a.s.fold_ps, j + 1)
                c = j % a.chunks
                dst = foldT if j < a.chunks else foldV
                nc.scalar.copy(dst[:, c * BANK:(c + 1) * BANK], bank[RING[j % 3]][0:DC, :]).then_inc(a.s.fold_sb, 1)

        def attn_pe(pe, a):
            s, C, W = a.s, a.chunks, 4 * S2
            phase_start(pe, a.phase)
            attn_fold_pe(pe, a)

            def step(n, u):
                if within(n, 0, NB):
                    pe.wait_ge(s.xn, n + 1)
                    at_least(pe, s.shift, (n - 1) * C + 1)
                    pe.transpose(bank[0][:, 384:512], xn[:, 0, :], ident[:, :]).then_inc(s.xt_ps, 1)
                    pe.wait_ge(s.ctx, n + 1)
                    for c in range(C):
                        ring_free(pe, a, n, 0, c)
                        for i in range(4):
                            h = 4 * c + i
                            ins = pe.matmul(ring(a, 0, c)[:, i * S2:(i + 1) * S2], foldT[:, h * P:(h + 1) * P],
                                            ctx_b[:, u, 0:S2], start=True, stop=True)
                        ins.then_inc(s.t_ps, 1)
                if within(n, 1, NB + 1):
                    for c in range(C):
                        ring_free(pe, a, n, 1, c)
                        pe.matmul(ring(a, 1, c)[0:S2, :], ctx_b[:, 1 - u, 0:S2], foldV[:, c * BANK:(c + 1) * BANK],
                                  start=True, stop=True).then_inc(s.v_ps, 1)
                    pe.wait_ge(s.probs, n)
                    for c in range(C):
                        ring_free(pe, a, n, 2, c)
                        for i in range(4):
                            h = 4 * c + i
                            ins = pe.transpose(ring(a, 2, c)[0:S2, i * P:(i + 1) * P],
                                               score[:, 1 - u, h * S2:(h + 1) * S2], ident[:, :])
                        ins.then_inc(s.pt_ps, 1)
                if within(n, 0, NB):
                    pe.wait_ge(s.xt_sb, n + 1)
                    for c in range(C):
                        pe.wait_ge(s.t_sb, n * C + c + 1)
                        at_least(pe, s.shift, (n - 1) * C + c + 1)
                        pe.matmul(bank[c][:, 0:W], xnT[:, 0, 0:P], keys[:, c * W:(c + 1) * W],
                                  start=True, stop=True).then_inc(s.s_ps, 1)
                if within(n, 1, NB + 1):
                    pe.wait_ge(s.v_sb, n * C)
                    pe.wait_ge(s.pt_sb, n * C)
                    at_least(pe, s.added, n - 1)
                    for h in range(a.heads):
                        ins = pe.matmul(bank[7][:, 0:D], probsT[:, h * P:(h + 1) * P], vals[:, h * D:(h + 1) * D],
                                        start=(h == 0), stop=(h == a.heads - 1))
                    ins.then_inc(s.y_ps, 1)

            steps(pe, step, NB + 1, 2, 3)
            phase_end(pe)

        def attn_act(act, a):
            s, C, W = a.s, a.chunks, 4 * S2
            phase_start(act, a.phase)
            attn_fold_act(act, a)

            def step(n, u):
                if within(n, 0, NB):
                    act.wait_ge(s.xt_ps, n + 1)
                    at_least(act, s.s_ps, n * C)
                    nc.scalar.copy(xnT[:, 0, 0:P], bank[0][:, 384:512]).then_inc(s.xt_sb, 1)
                    for c in range(C):
                        act.wait_ge(s.t_ps, n * C + c + 1)
                        nc.scalar.copy(keys[:, c * W:(c + 1) * W], ring(a, 0, c)[:, 0:W]).then_inc(s.t_sb, 1)
                if within(n, 1, NB + 1):
                    at_least(act, s.y_ps, n - 1)
                    for c in range(C):
                        act.wait_ge(s.pt_ps, (n - 1) * C + c + 1)
                        nc.scalar.copy(probsT[:, c * BANK:(c + 1) * BANK], ring(a, 2, c)[0:S2, :]).then_inc(s.pt_sb, 1)
                if within(n, 0, NB):
                    for c in range(C):
                        act.wait_ge(s.shift, n * C + c + 1)
                        e = score[:, u, c * W:(c + 1) * W]
                        nc.scalar.activation(e, e, ACT.Exp, scale=HD ** -0.5).then_inc(s.ex, 1)

            steps(act, step, NB + 1, 2, 3)
            phase_end(act)

        def attn_pool(pool, a):
            s, C = a.s, a.chunks
            phase_start(pool, a.phase)
            clear_last_phase(pool, a.phase)

            def fetch(n, u):
                at_least(pool, s.v_ps, (n - 1) * C)
                pool.tensor_copy(ctx_b[:, u, 0:S2], ctxT[:, ds(n * S2, S2)]).then_inc(s.ctx, 1)

            pool.wait_ge(loads.x, 32)
            fetch(0, 0)
            ln_rstd(pool, s, 0, 0, 1)

            def step(n, u):
                if within(n, 0, NB - 1):
                    ln_rstd(pool, s, n + 1, 1 - u, 1)
                    fetch(n + 1, 1 - u)

            steps(pool, step, NB + 1, 2, 3)
            phase_end(pool)

        def attn_dve(dve, a):
            s, C, H, W = a.s, a.chunks, a.heads, 4 * S2
            phase_start(dve, a.phase)
            dve.wait_ge(loads.x, 32)
            ln_stats(dve, s, 0, 0, 1)
            ln_apply(dve, s, 0, 0, 1, s.xt_ps)

            def heads_of(ap):
                return ap.rearrange("p (h j) -> p h j", j=S2)

            def step(n, u):
                if within(n, 1, NB + 1):
                    at_least(dve, s.y_ps, n - 1)
                    for c in range(C):
                        dve.wait_ge(s.v_ps, (n - 1) * C + c + 1)
                        dve.tensor_copy(vals[:, c * BANK:(c + 1) * BANK], ring(a, 1, c)[0:S2, :]).then_inc(s.v_sb, 1)
                if within(n, 0, NB - 1):
                    ln_stats(dve, s, n + 1, 1 - u, 1)
                if within(n, 0, NB):
                    at_least(dve, s.pt_ps, (n - 1) * C)
                    for c in range(C):
                        dve.wait_ge(s.s_ps, n * C + c + 1)
                        dve.reduce_max(top[:, 4 * c:4 * c + 4], heads_of(bank[c][:, 0:W]), AX.X).then_inc(s.top, 1)
                        dve.wait_ge(s.top, n * C + c + 1)
                        dve.tensor_tensor(heads_of(score[:, u, c * W:(c + 1) * W]), heads_of(bank[c][:, 0:W]),
                                          top[:, 4 * c:4 * c + 4].unsqueeze(2).to_broadcast([P, 4, S2]),
                                          ALU.subtract).then_inc(s.shift, 1)
                if within(n, 0, NB - 1):
                    ln_apply(dve, s, n + 1, 1 - u, 1, s.xt_ps)
                if within(n, 0, NB):
                    for c in range(C):
                        e = heads_of(score[:, u, c * W:(c + 1) * W])
                        dve.wait_ge(s.ex, n * C + c + 1)
                        dve.reduce_sum(tot[:, 4 * c:4 * c + 4], e, AX.X).then_inc(s.tot, 1)
                    dve.wait_ge(s.tot, (n + 1) * C)
                    dve.reciprocal(rec[:, 0:H], tot[:, 0:H]).then_inc(s.rec, 1)
                    dve.wait_ge(s.rec, n + 1)
                    e = heads_of(score[:, u, 0:H * S2])
                    dve.tensor_tensor(e, e, rec[:, 0:H].unsqueeze(2).to_broadcast([P, H, S2]),
                                      ALU.mult).then_inc(s.probs, 1)
                if within(n, 1, NB + 1):
                    dve.wait_ge(s.y_ps, n)
                    x = tile(n - 1)
                    dve.tensor_tensor(x, bank[7][:, 0:D], x, ALU.add).then_inc(s.added, 1)
                    dve.wait_ge(s.added, n)
                    dve.tensor_tensor(x, x, a.bias, ALU.add).then_inc(s.x, 1)

            steps(dve, step, NB + 1, 2, 3)
            phase_end(dve)

        s2 = stage[4 % 2]
        PH2 = 4
        q2, k2 = qkn[:, 0, :], work[:, 0:G * S2]
        v2, pT2 = work[0:S2, 512:1024], work[0:S2, 1024:1536]

        def attn2_pe(pe):
            s = s2
            phase_start(pe, PH2)
            pe.wait_ge(loads.l2, 16 * 5)

            def step(n, u):
                if within(n, 0, NG):
                    pe.wait_ge(s.xn, n + 1)
                    at_least(pe, s.xt_sb, n)
                    for i in range(G):
                        ins = pe.transpose(bank[0][:, i * P:(i + 1) * P], xn[:, i, :], ident[:, :])
                    ins.then_inc(s.xt_ps, 1)
                    pe.wait_ge(s.ctx, n + 1)
                    at_least(pe, s.k_sb, n)
                    pe.matmul(bank[2][:, 0:G * S2], l2w[0:DC, 1, :], ctx_b[:, u, :], start=True, stop=True)\
                      .then_inc(s.k_ps, 1)
                    pe.wait_ge(s.xt_sb, n + 1)
                    at_least(pe, s.q_sb, n)
                    pe.matmul(bank[1][:, :], l2w[:, 0, :], xnT[:, 0, :], start=True, stop=True).then_inc(s.q_ps, 1)
                if within(n, 1, NG + 1):
                    at_least(pe, s.v_sb, n - 1)
                    for i in range(G):
                        ins = pe.matmul(bank[3][0:S2, i * D:(i + 1) * D], ctx_b[:, 1 - u, i * S2:(i + 1) * S2],
                                        l2w[0:DC, 2, :], start=True, stop=True)
                    ins.then_inc(s.v_ps, 1)
                    pe.wait_ge(s.probs, n)
                    at_least(pe, s.pt_sb, n - 1)
                    for i in range(G):
                        ins = pe.transpose(bank[5][0:S2, i * P:(i + 1) * P], score[:, 1 - u, i * S2:(i + 1) * S2],
                                           ident[:, :])
                    ins.then_inc(s.pt_ps, 1)
                if within(n, 0, NG):
                    pe.wait_ge(s.q_sb, n + 1)
                    pe.wait_ge(s.k_sb, n + 1)
                    at_least(pe, s.shift, n)
                    for i in range(G):
                        ins = pe.matmul(bank[4][:, i * S2:(i + 1) * S2], q2[:, i * P:(i + 1) * P],
                                        k2[:, i * S2:(i + 1) * S2], start=True, stop=True)
                    ins.then_inc(s.s_ps, 1)
                if within(n, 1, NG + 1):
                    pe.wait_ge(s.v_sb, n)
                    pe.wait_ge(s.pt_sb, n)
                    at_least(pe, s.added, n - 1)
                    for i in range(G):
                        ins = pe.matmul(bank[6][:, i * D:(i + 1) * D], pT2[:, i * P:(i + 1) * P],
                                        v2[:, i * D:(i + 1) * D], start=True, stop=True)
                    ins.then_inc(s.y_ps, 1)

            steps(pe, step, NG + 1, 2, 3)
            phase_end(pe)

        def attn2_act(act):
            s = s2
            phase_start(act, PH2)
            act.wait_ge(loads.l2, 16 * 5)

            def step(n, u):
                if within(n, 0, NG):
                    act.wait_ge(s.xt_ps, n + 1)
                    at_least(act, s.q_ps, n)
                    nc.scalar.copy(xnT[:, 0, :], bank[0][:, :]).then_inc(s.xt_sb, 1)
                    act.wait_ge(s.k_ps, n + 1)
                    at_least(act, s.s_ps, n)
                    nc.scalar.activation(k2, bank[2][:, 0:G * S2], ACT.Identity, bias=l2b[:, 1:2]).then_inc(s.k_sb, 1)
                    act.wait_ge(s.q_ps, n + 1)
                    nc.scalar.activation(q2, bank[1][:, :], ACT.Identity, bias=l2b[:, 0:1]).then_inc(s.q_sb, 1)
                if within(n, 1, NG + 1):
                    act.wait_ge(s.v_ps, n)
                    at_least(act, s.y_ps, n - 1)
                    nc.scalar.copy(v2, bank[3][0:S2, :]).then_inc(s.v_sb, 1)
                    act.wait_ge(s.pt_ps, n)
                    nc.scalar.copy(pT2, bank[5][0:S2, :]).then_inc(s.pt_sb, 1)
                if within(n, 0, NG):
                    act.wait_ge(s.shift, n + 1)
                    e = score[:, u, 0:G * S2]
                    nc.scalar.activation(e, e, ACT.Exp, scale=D ** -0.5).then_inc(s.ex, 1)

            steps(act, step, NG + 1, 2, 3)
            phase_end(act)

        def attn2_pool(pool):
            s = s2
            phase_start(pool, PH2)
            clear_last_phase(pool, PH2)

            def fetch(n, u):
                at_least(pool, s.v_ps, n - 1)
                pool.tensor_copy(ctx_b[:, u, :], ctxT[:, ds(n * G * S2, G * S2)]).then_inc(s.ctx, 1)

            fetch(0, 0)
            ln_rstd(pool, s, 0, 0, G)

            def step(n, u):
                if within(n, 0, NG - 1):
                    ln_rstd(pool, s, n + 1, 1 - u, G)
                    fetch(n + 1, 1 - u)

            steps(pool, step, NG + 1, 2, 3)
            phase_end(pool)

        def attn2_dve(dve):
            s = s2
            phase_start(dve, PH2)
            dve.wait_ge(loads.l2, 16 * 5)
            ln_stats(dve, s, 0, 0, G)
            ln_apply(dve, s, 0, 0, G, s.xt_ps)

            def step(n, u):
                if within(n, 0, NG - 1):
                    ln_stats(dve, s, n + 1, 1 - u, G)
                e = score[:, u, 0:G * S2].rearrange("p (h j) -> p h j", j=S2)
                if within(n, 0, NG):
                    at_least(dve, s.pt_ps, n - 1)
                    sc = bank[4][:, 0:G * S2].rearrange("p (h j) -> p h j", j=S2)
                    dve.wait_ge(s.s_ps, n + 1)
                    dve.reduce_max(top[:, 0:G], sc, AX.X).then_inc(s.top, 1)
                    dve.wait_ge(s.top, n + 1)
                    dve.tensor_tensor(e, sc, top[:, 0:G].unsqueeze(2).to_broadcast([P, G, S2]),
                                      ALU.subtract).then_inc(s.shift, 1)
                if within(n, 0, NG - 1):
                    ln_apply(dve, s, n + 1, 1 - u, G, s.xt_ps)
                if within(n, 0, NG):
                    dve.wait_ge(s.ex, n + 1)
                    dve.reduce_sum(tot[:, 0:G], e, AX.X).then_inc(s.tot, 1)
                    dve.wait_ge(s.tot, n + 1)
                    dve.reciprocal(rec[:, 0:G], tot[:, 0:G]).then_inc(s.rec, 1)
                    dve.wait_ge(s.rec, n + 1)
                    dve.tensor_tensor(e, e, rec[:, 0:G].unsqueeze(2).to_broadcast([P, G, S2]),
                                      ALU.mult).then_inc(s.probs, 1)
                if within(n, 1, NG + 1):
                    dve.wait_ge(s.y_ps, n)
                    x = X[:, ds((n - 1) * G, G), :]
                    dve.tensor_tensor(x, bank[6][:, :].rearrange("p (g d) -> p g d", g=G), x, ALU.add)\
                       .then_inc(s.added, 1)
                    dve.wait_ge(s.added, n)
                    dve.tensor_tensor(x, x, obias[:, 2, :].unsqueeze(1).to_broadcast([P, G, D]), ALU.add)\
                       .then_inc(s.x, 1)

            steps(dve, step, NG + 1, 2, 3)
            phase_end(dve)

        PH3C, PH3X = 6, 7
        kc = raw[:, 0:NB * S2]
        vc = raw[0:S2, 2560:2560 + NB * D].rearrange("p (b d) -> p b d", d=D)
        ctxn = work[0:S2, 0:NB * DC].rearrange("p (b c) -> p b c", c=DC)
        maskb = raw[:, 6656:6656 + NB * S2]
        wkv, wl, wo3 = l3w[0:DC, 384:640], l3w[:, 0:384], l3w[:, 640:768]
        s3c = stage[6 % 2]
        bnc = hid[0:S2, 0, 0, 0:NB * 6].rearrange("p (b k) -> p b k", k=6)
        mvc = hid[0:S2, 0, 1, 0:NB * 2].rearrange("p (b k) -> p b k", k=2)
        vec, rsc = hid[0:S2, 0, 2, 0:NB], hid[0:S2, 0, 3, 0:NB]
        xnc = score[0:S2, :, 0:G * DC].rearrange("p u (g c) -> p u g c", g=G)

        def kv_view(lo, hi, i):
            return bank[i][0:S2, :].rearrange("p (b c) -> p b c", b=2)[:, :, lo:hi]

        def ctx3_pe(pe):
            s = s3c
            phase_start(pe, PH3C)
            pe.wait_ge(loads.l3, 16 * 9)

            def step(n, u):
                if within(n, 0, NG):
                    pe.wait_ge(s.xn, n + 1)
                    at_least(pe, s.xt_sb, n)
                    for i in range(G):
                        ins = pe.transpose(bank[0][0:DC, i * S2:(i + 1) * S2], xnc[:, u, i, :], ident[0:S2, 0:S2])
                    ins.then_inc(s.xt_ps, 1)
                if within(n, 2, NG + 2):
                    pe.wait_ge(s.qk, n - 1)
                    pe.wait_ge(s.kt_sb, n - 1)
                    for i in range(G):
                        ins = pe.transpose(bank[5][:, i * S2:(i + 1) * S2], qkn[0:S2, u, i * P:(i + 1) * P],
                                           ident[0:S2, 0:S2])
                    ins.then_inc(s.kt_ps, 1)
                if within(n, 0, NG):
                    pe.wait_ge(s.xt_sb, n + 1)
                    at_least(pe, s.qk, n - 1)
                    at_least(pe, s.v_sb, 2 * (n - 1))
                    for i in range(G):
                        ins = pe.matmul(bank[1 + 2 * u + i // 2][0:S2, (i % 2) * 256:(i % 2) * 256 + 256],
                                        xnT[0:DC, u, i * S2:(i + 1) * S2], wkv, start=True, stop=True)
                    ins.then_inc(s.qkv_ps, 1)

            steps(pe, step, NG + 2, 2, 4)
            phase_end(pe)

        def ctx3_act(act):
            s = s3c
            phase_start(act, PH3C)
            act.wait_ge(loads.l3, 16 * 9)
            act.sem_inc(s.kt_sb, 1)

            def step(n, u):
                if within(n, 0, NG):
                    act.wait_ge(s.xt_ps, n + 1)
                    at_least(act, s.qkv_ps, n - 1)
                    nc.scalar.activation(xnT[0:DC, u, 0:G * S2], bank[0][0:DC, 0:G * S2], ACT.Identity,
                                         bias=l3g[0:DC, 1:2], scale=l3g[0:DC, 0:1]).then_inc(s.xt_sb, 1)
                if within(n, 2, NG + 2):
                    act.wait_ge(s.kt_ps, n - 1)
                    nc.scalar.copy(kc[:, ds((n - 2) * G * S2, G * S2)], bank[5][:, 0:G * S2]).then_inc(s.kt_sb, 1)
                if within(n, 0, NG):
                    act.wait_ge(s.qkv_ps, n + 1)
                    at_least(act, s.ss, n)
                    for i in range(2):
                        nc.scalar.activation(sq[0:S2, i * 256:(i + 1) * 256].rearrange("p (b c) -> p b c", b=2),
                                             kv_view(0, 128, 1 + 2 * u + i), ACT.Square).then_inc(s.sq, 1)
                    for i in range(2):
                        nc.scalar.copy(vc[:, ds(n * G + 2 * i, 2), :], kv_view(128, 256, 1 + 2 * u + i))\
                            .then_inc(s.v_sb, 1)

            steps(act, step, NG + 2, 2, 4)
            phase_end(act)

        def ctx3_pool(pool):
            s = s3c
            phase_start(pool, PH3C)
            clear_last_phase(pool, PH3C)
            pool.wait_ge(s.mv, NB)
            pool.tensor_scalar(vec, mvc[:, :, 1], EPS, None, ALU.add).then_inc(s.ve, 1)
            pool.wait_ge(s.ve, 1)
            pool.tensor_tensor(rsc, vec, mhalf[0:S2, 0:NB], ALU.pow).then_inc(s.rstd, 1)
            for n in range(NG):
                gather(pool, ffn[2], n)
                pool.wait_ge(s.sr, n + 1)
                pool.tensor_tensor(sr2[0:S2, :], sr[0:S2, :], mhalf[0:S2, 0:8], ALU.pow).then_inc(s.sr2, 1)
            phase_end(pool)

        def ctx3_dve(dve):
            s = s3c
            phase_start(dve, PH3C)
            dve.wait_ge(loads.l3, 16 * 9)
            dve.wait_ge(loads.ctxn, 32)
            with dve.Fori(0, NG) as n:
                for i in range(G):
                    dve.bn_stats(bnc[:, ds(n * G + i, 1), :].rearrange("p a k -> p (a k)"),
                                 ctxn[:, ds(n * G + i, 1), :].rearrange("p a c -> p (a c)")).then_inc(s.bn, 1)
            dve.wait_ge(s.bn, NB)
            for b in range(NB):
                dve.bn_aggr(mvc[:, b, :], bnc[:, b, :]).then_inc(s.mv, 1)
            dve.tensor_scalar(maskb, mask8[:, :], -1.0, FLT_MAX, ALU.add, ALU.mult)
            dve.tensor_tensor(l3g[:, 5:6], l3g[:, 4:5], l3g[:, 6:7], ALU.mult)
            dve.wait_ge(s.rstd, 1)

            def apply(n, u):
                at_least(dve, s.xt_ps, n - 1)
                for i in range(G):
                    if isinstance(n, int):
                        b = n * G + i
                        mean, dev = mvc[:, b, 0:1], rsc[:, b:b + 1]
                    else:
                        b = n * G + i
                        mean, dev = mvc[:, ds(b, 1), 0], rsc[:, ds(b, 1)]
                    ins = dve.tensor_scalar(xnc[:, u, i, :], ctxn[:, ds(b, 1), :].rearrange("p a c -> p (a c)"),
                                            mean, dev, ALU.subtract, ALU.mult)
                ins.then_inc(s.xn, 1)

            apply(0, 0)

            def step(n, u):
                if within(n, 1, NG + 1):
                    dve.wait_ge(s.sr2, n)
                    dve.wait_ge(s.v_sb, 2 * n)
                    for i in range(2):
                        ins = dve.tensor_tensor(
                            qkn[0:S2, 1 - u, i * 256:(i + 1) * 256].rearrange("p (b h d) -> p b h d", b=2, h=2),
                            kv_view(0, 128, 3 - 2 * u + i).rearrange("p b (h d) -> p b h d", h=2),
                            sr2[0:S2, 4 * i:4 * i + 4].rearrange("p (b h) -> p b h", b=2).unsqueeze(3)
                            .to_broadcast([S2, 2, 2, HD]), ALU.mult)
                    ins.then_inc(s.qk, 1)
                if within(n, 0, NG - 1):
                    apply(n + 1, 1 - u)
                if within(n, 0, NG):
                    dve.wait_ge(s.sq, 2 * n + 2)
                    dve.reduce_sum(ss[0:S2, :], sq[0:S2, :].rearrange("p (h d) -> p h d", d=HD), AX.X)\
                       .then_inc(s.ss, 1)
                    dve.wait_ge(s.ss, n + 1)
                    dve.tensor_scalar(sr[0:S2, :], ss[0:S2, :], 1.0 / HD, RMS_EPS ** 2, ALU.mult, ALU.max)\
                       .then_inc(s.sr, 1)

            steps(dve, step, NG + 2, 2, 4)
            sorted_back_dve(dve, ffn[2])
            phase_end(dve)

        s3 = stage[7 % 2]
        g3, N3 = 2, NB // 2
        KL = S2 + P
        qT3, kT3 = xall[:, 0:2 * P], xall[:, 256:512]
        pT3 = xall[:, 512:1536]
        oT3 = xall[:, 1536:1536 + 2 * P]
        sc3 = xall[:, 2048:2048 + 2 * 2 * 2 * KL].rearrange("p (u t h j) -> p u t h j", u=2, t=2, h=2)

        def v3(j, i):
            return hid[:, j // 2, j % 2, i * P:(i + 1) * P]


        def sbank(h):
            return bank[4 + h][:, 0:2 * KL].rearrange("p (t j) -> p t j", t=2)

        def attn3_pe(pe):
            s = s3
            phase_start(pe, PH3X)

            def step(n, q):
                u = q % 2
                if within(n, 1, N3 + 1):
                    pe.wait_ge(s.qk, n)
                    at_least(pe, s.kt_sb, n - 1)
                    for i in range(g3):
                        for j in range(2):
                            ins = pe.transpose(bank[3][:, (2 * j + i) * P:(2 * j + i + 1) * P],
                                               qkn[:, 1 - u, (2 * i + j) * P:(2 * i + j + 1) * P], ident[:, :])
                    ins.then_inc(s.qkt_ps, 1)
                if within(n, 0, N3):
                    pe.wait_ge(s.xn, n + 1)
                    at_least(pe, s.xt_sb, n)
                    for i in range(g3):
                        ins = pe.transpose(bank[0][:, i * P:(i + 1) * P], xn[:, i, :], ident[:, :])
                    ins.then_inc(s.xt_ps, 1)
                if within(n, 3, N3 + 3):
                    pe.wait_ge(s.o_sb, n - 2)
                    for i in range(g3):
                        ins = pe.matmul(bank[7][:, i * P:(i + 1) * P], oT3[:, i * P:(i + 1) * P], wo3,
                                        start=True, stop=True)
                    ins.then_inc(s.y_ps, 1)
                if within(n, 1, N3 + 1):
                    pe.wait_ge(s.kt_sb, n)
                    pe.wait_ge(s.ctx, n)
                    at_least(pe, s.shift, n - 1)
                    for i in range(g3):
                        for h in range(2):
                            hp = slice(h * HD, (h + 1) * HD)
                            pe.matmul(bank[4 + h][:, i * KL:i * KL + S2], qT3[hp, i * P:(i + 1) * P],
                                      kcs[hp, 1 - u, i * S2:(i + 1) * S2], start=True, stop=True)
                            ins = pe.matmul(bank[4 + h][:, i * KL + S2:(i + 1) * KL], qT3[hp, i * P:(i + 1) * P],
                                            kT3[hp, i * P:(i + 1) * P], start=True, stop=True)
                    ins.then_inc(s.s_ps, 1)
                if within(n, 0, N3):
                    pe.wait_ge(s.xt_sb, n + 1)
                    at_least(pe, s.qk, n)
                    at_least(pe, s.v_sb, n)
                    for i in range(g3):
                        ins = pe.matmul(bank[1 + i][:, 0:384], xnT[:, u, i * P:(i + 1) * P], wl, start=True, stop=True)
                    ins.then_inc(s.qkv_ps, 1)
                if within(n, 2, N3 + 2):
                    pe.wait_ge(s.probs, n - 1)
                    for i in range(g3):
                        at_least(pe, s.pt_sb, 2 * (n - 2) + i)
                        for h in range(2):
                            pr = sc3[:, u, i, h, :]
                            pe.transpose(bank[6][0:S2, h * P:(h + 1) * P], pr[:, 0:S2], ident[:, :])
                            ins = pe.transpose(bank[6][:, (2 + h) * P:(3 + h) * P], pr[:, S2:KL], ident[:, :])
                        ins.then_inc(s.pt_ps, 1)
                    pe.wait_ge(s.xall, n - 1)
                    at_least(pe, s.added, n - 2)
                    for i in range(g3):
                        pe.wait_ge(s.pt_sb, 2 * (n - 2) + i + 1)
                        for h in range(2):
                            o = bank[7][h * HD:(h + 1) * HD, i * P:(i + 1) * P]
                            hv = slice(h * HD, (h + 1) * HD)
                            pe.matmul(o, vcs[:, u, i, hv], pT3[0:S2, (4 * i + h) * P:(4 * i + h + 1) * P],
                                      start=True, stop=False)
                            ins = pe.matmul(o, v3((q + 2) % 4, i)[:, hv], pT3[:, (4 * i + 2 + h) * P:(4 * i + 3 + h) * P],
                                            start=False, stop=True)
                    ins.then_inc(s.o_ps, 1)

            steps(pe, step, N3 + 3, 4, 7, by=4)
            phase_end(pe)

        kcs = sb("kcs", [P, 2, g3 * S2])
        vcs = sb("vcs", [S2, 2, g3, D])

        def attn3_act(act):
            s = s3
            phase_start(act, PH3X)

            def step(n, q):
                u = q % 2
                if within(n, 1, N3 + 1):
                    act.wait_ge(s.qkt_ps, n)
                    at_least(act, s.s_ps, n - 1)
                    nc.scalar.activation(qT3, bank[3][:, 0:2 * P], ACT.Copy, scale=l3g[:, 5:6])
                    nc.scalar.copy(kT3, bank[3][:, 2 * P:4 * P]).then_inc(s.kt_sb, 1)
                if within(n, 0, N3):
                    act.wait_ge(s.xt_ps, n + 1)
                    at_least(act, s.qkv_ps, n - 1)
                    nc.scalar.activation(xnT[:, u, 0:2 * P], bank[0][:, 0:256], ACT.Identity,
                                         bias=l3g[:, 3:4], scale=l3g[:, 2:3]).then_inc(s.xt_sb, 1)
                    act.wait_ge(s.qkv_ps, n + 1)
                    at_least(act, s.ss, n)
                    for i in range(g3):
                        ins = nc.scalar.activation(sq[:, i * 256:(i + 1) * 256], bank[1 + i][:, 0:256], ACT.Square)
                    ins.then_inc(s.sq, 1)
                    at_least(act, s.o_ps, n - 3)
                    for i in range(g3):
                        ins = nc.scalar.copy(v3(q, i), bank[1 + i][:, 256:384])
                    ins.then_inc(s.v_sb, 1)
                if within(n, 2, N3 + 2):
                    at_least(act, s.o_ps, n - 2)
                    for i in range(g3):
                        act.wait_ge(s.pt_ps, 2 * (n - 2) + i + 1)
                        nc.scalar.copy(pT3[0:S2, 4 * i * P:(4 * i + 2) * P], bank[6][0:S2, 0:2 * P])
                        nc.scalar.copy(pT3[:, (4 * i + 2) * P:(4 * i + 4) * P], bank[6][:, 2 * P:4 * P])\
                            .then_inc(s.pt_sb, 1)
                if within(n, 1, N3 + 1):
                    act.wait_ge(s.shift, n)
                    e = sc3[:, 1 - u, :, :, :].rearrange("p t h j -> p (t h j)")
                    nc.scalar.activation(e, e, ACT.Exp, scale=HD ** -0.5).then_inc(s.ex, 1)
                if within(n, 2, N3 + 2):
                    act.wait_ge(s.o_ps, n - 1)
                    at_least(act, s.y_ps, n - 2)
                    nc.scalar.copy(oT3, bank[7][:, 0:2 * P]).then_inc(s.o_sb, 1)

            steps(act, step, N3 + 2, 4, 6, by=4)
            phase_end(act)

        def attn3_pool(pool):
            s = s3
            phase_start(pool, PH3X)
            clear_last_phase(pool, PH3X)

            def rstds(n, u):
                pool.wait_ge(s.ve, n + 1)
                pool.tensor_tensor(rstd[:, u, 0:g3], ve[:, u, 0:g3], mhalf[:, 0:g3], ALU.pow).then_inc(s.rstd, 1)

            rstds(0, 0)

            def step(n, u):
                if within(n, 0, N3):
                    pool.wait_ge(s.sr, n + 1)
                    pool.tensor_tensor(sr2[:, :], sr[:, :], mhalf[:, 0:8], ALU.pow).then_inc(s.sr2, 1)
                if within(n, 0, N3 - 1):
                    rstds(n + 1, 1 - u)
                if within(n, 0, N3):
                    at_least(pool, s.s_ps, n - 1)
                    pool.tensor_copy(kcs[:, u, :], kc[:, ds(n * g3 * S2, g3 * S2)]).then_inc(s.ctx, 1)
                if within(n, 1, N3 + 1):
                    at_least(pool, s.o_ps, n - 2)
                    pool.tensor_copy(vcs[:, 1 - u, :, :], vc[:, ds((n - 1) * g3, g3), :]).then_inc(s.xall, 1)

            steps(pool, step, N3 + 1, 4, 3)
            phase_end(pool)

        def attn3_dve(dve):
            s = s3
            phase_start(dve, PH3X)

            def stats(n, u):
                ln_stats(dve, s, n, u, g3)
                dve.wait_ge(s.mv, (n + 1) * g3)
                dve.tensor_scalar(ve[:, u, 0:g3], mv[:, u, 0:g3, 1], 1.0 + EPS, EPS * EPS, ALU.mult, ALU.add)\
                   .then_inc(s.ve, 1)

            stats(0, 0)
            ln_apply(dve, s, 0, 0, g3, s.xt_ps)

            def step(n, u):
                if within(n, 1, N3 + 1):
                    mb = maskb[:, ds((n - 1) * g3 * S2, g3 * S2)].rearrange("p (t j) -> p t j", t=2)
                    e = sc3[:, 1 - u, :, :, :]
                    dve.wait_ge(s.s_ps, n)
                    at_least(dve, s.pt_ps, 2 * (n - 2))
                    ctop, ltop, mx = (top[:, 4 * k:4 * k + 4].rearrange("p (t h) -> p t h", t=2) for k in range(3))
                    for h in range(2):
                        dve.tensor_tensor(e[:, :, h, 0:S2], sbank(h)[:, :, 0:S2], mb, ALU.add).then_inc(s.m2, 1)
                        dve.reduce_max(ltop[:, :, h], sbank(h)[:, :, S2:KL], AX.X).then_inc(s.m3, 1)
                    dve.wait_ge(s.m2, n * 2)
                    dve.reduce_max(ctop, e[:, :, :, 0:S2], AX.X).then_inc(s.m3, 1)
                    dve.wait_ge(s.m3, n * 3)
                    dve.tensor_tensor(mx, ctop, ltop, ALU.max).then_inc(s.m4, 1)
                    dve.wait_ge(s.m4, n)
                    dve.tensor_tensor(e[:, :, :, 0:S2], e[:, :, :, 0:S2],
                                      mx.unsqueeze(3).to_broadcast([P, 2, 2, S2]), ALU.subtract)
                    for h in range(2):
                        ins = dve.tensor_tensor(e[:, :, h, S2:KL], sbank(h)[:, :, S2:KL],
                                                mx[:, :, h].unsqueeze(2).to_broadcast([P, 2, P]), ALU.subtract)
                    ins.then_inc(s.shift, 1)
                if within(n, 0, N3):
                    dve.wait_ge(s.sq, n + 1)
                    dve.reduce_sum(ss[:, :], sq[:, :].rearrange("p (h d) -> p h d", d=HD), AX.X).then_inc(s.ss, 1)
                    dve.wait_ge(s.ss, n + 1)
                    dve.tensor_scalar(sr[:, :], ss[:, :], 1.0 / HD, RMS_EPS ** 2, ALU.mult, ALU.max).then_inc(s.sr, 1)
                if within(n, 0, N3 - 1):
                    stats(n + 1, 1 - u)
                if within(n, 3, N3 + 3):
                    dve.wait_ge(s.y_ps, n - 2)
                    x = X[:, ds((n - 3) * g3, g3), :]
                    dve.tensor_tensor(x, bank[7][:, 0:256].rearrange("p (t d) -> p t d", t=2), x, ALU.add)\
                       .then_inc(s.added, 1)
                    dve.wait_ge(s.added, n - 2)
                    dve.tensor_tensor(x, x, l3bo[:, :].unsqueeze(1).to_broadcast([P, g3, D]), ALU.add)\
                       .then_inc(s.x, 1)
                if within(n, 0, N3):
                    dve.wait_ge(s.sr2, n + 1)
                    dve.wait_ge(s.v_sb, n + 1)
                    at_least(dve, s.qkt_ps, n - 1)
                    for i in range(g3):
                        ins = dve.tensor_tensor(
                            qkn[:, u, i * 256:(i + 1) * 256].rearrange("p (h d) -> p h d", d=HD),
                            bank[1 + i][:, 0:256].rearrange("p (h d) -> p h d", d=HD),
                            sr2[:, 4 * i:4 * i + 4].unsqueeze(2).to_broadcast([P, 4, HD]), ALU.mult)
                    ins.then_inc(s.qk, 1)
                if within(n, 1, N3 + 1):
                    dve.wait_ge(s.ex, n)
                    et = e.rearrange("p t h j -> p (t h) j")
                    dve.reduce_sum(tot[:, 0:4], et, AX.X).then_inc(s.tot, 1)
                    dve.wait_ge(s.tot, n)
                    dve.reciprocal(rec[:, 0:4], tot[:, 0:4]).then_inc(s.rec, 1)
                    dve.wait_ge(s.rec, n)
                    dve.tensor_tensor(et, et, rec[:, 0:4].unsqueeze(2).to_broadcast([P, 4, KL]),
                                      ALU.mult).then_inc(s.probs, 1)
                if within(n, 0, N3 - 1):
                    ln_apply(dve, s, n + 1, 1 - u, g3, s.xt_ps)

            steps(dve, step, N3 + 3, 4, 5)
            phase_end(dve)

        l3bo = sb("l3bo", [P, D])

        class Ffn:
            def __init__(self, layer, phase, experts, chunks, func, gated, ranks, router, biased):
                self.layer, self.phase, self.experts, self.chunks = layer, phase, experts, chunks
                self.func, self.gated, self.ranks, self.router, self.biased = func, gated, ranks, router, biased
                self.slots = {(4, False): 4, (1, False): 2, (4, True): 2, (3, True): 3}[chunks, gated]
                self.load = (loads.ffn0, loads.ffn1, loads.ffn2, loads.ffn3)[layer]
                self.s = stage[phase % 2]
                self.sorted = layer in (0, 2)
                self.scatters = {0: 2 * NB, 2: 3 * NB}.get(layer)
                self.loads = {0: 3, 1: 2, 2: 4, 3: 2}[layer]

        def chunk_at(f, g, c):
            return (g * f.chunks + c) % f.slots

        def up_bank(f, slot, half=0):
            return bank[2 * slot + half] if f.gated else bank[slot]

        def over_experts(eng, f, body):
            if f.experts == 1:
                body(0, 0, 0)
                return
            with eng.Fori(0, f.experts // 2) as i:
                for p in (0, 1):
                    body(i * 2 + p, p, i)

        def ffn_sp(sp, f, w1_of, w2_of, b1_of):
            s = f.s
            phase_start(sp, f.phase)

            def load(e, p, wait):
                if wait is not None:
                    sp.wait_ge(s.y_ps, wait)
                n = f.chunks * P * (2 if f.gated else 1)
                sp.dma_start(w1[:, p, 0:n], w1_of(e)).then_inc((s.w0, s.w1)[p], 16)
                sp.dma_start(w2[:, p, 0:f.chunks, :], w2_of(e)).then_inc((s.w0, s.w1)[p], 16)
                sp.dma_start(b1[:, p, 0:f.chunks], b1_of(e)).then_inc((s.w0, s.w1)[p], 16)

            load(0, 0, None)
            load(1, 1, None)
            with sp.Fori(1, f.experts // 2) as i:
                for p in (0, 1):
                    load(i * 2 + p, p, (i * 2 + p - 1) * NG + 2)

        def ffn_pe(pe, f):
            s, C, R = f.s, f.chunks, f.slots
            phase_start(pe, f.phase)
            pe.wait_ge(f.load, 16 * 2)

            def front(n, u):
                pe.wait_ge(s.xn, n + 1)
                at_least(pe, s.xt_sb, n)
                for i in range(G):
                    ins = pe.transpose(bank[0][:, i * P:(i + 1) * P], xn[:, i, :], ident[:, :])
                ins.then_inc(s.xt_ps, 1)
                if f.ranks:
                    pe.wait_ge(s.xt_sb, n + 1)
                    at_least(pe, s.lg, n - 1)
                    for i in range(G):
                        ins = pe.matmul(bank[1 + u][:, i * NE:(i + 1) * NE], xnT[:, u, i * P:(i + 1) * P],
                                        wr[:, f.layer, :], start=True, stop=True)
                    ins.then_inc(s.l_ps, 1)

            steps(pe, front, NG, 2, 2)
            if f.biased:
                def bias(n, u):
                    pe.wait_ge(s.gb, n + 1)
                    at_least(pe, s.gt_sb, n)
                    for i in range(G):
                        ins = pe.transpose(bank[5][0:NE, i * P:(i + 1) * P], gb[:, i * NE:(i + 1) * NE], ident[:, :])
                    ins.then_inc(s.gt_ps, 1)
                    pe.wait_ge(s.gt_sb, n + 1)
                    at_least(pe, s.bb, n)
                    for i in range(G):
                        ins = pe.matmul(bank[6][:, i * D:(i + 1) * D], gT[:, i * P:(i + 1) * P], b2[:, f.layer, :],
                                        start=True, stop=True)
                    ins.then_inc(s.bb_ps, 1)

                steps(pe, bias, NG, 2, 2)
            if f.biased:
                pe.wait_ge(s.bb, NG)
            elif f.ranks:
                pe.wait_ge(s.lg, NG)
            pe.wait_ge(s.xall, NG)
            pe.sem_inc(s.y_ps, 2)

            def expert(e, p, i):
                if f.experts == 1:
                    pe.wait_ge(s.w0, 1)
                else:
                    pe.wait_ge((s.w0, s.w1)[p], i * 48 + 48)

                def step(g, u):
                    it = e * NG + g
                    if within(g, 0, NG):
                        for c in range(C):
                            slot = chunk_at(f, u, c)
                            pe.wait_ge(s.h, it * C + c + 1)
                            for half in range(2 if f.gated else 1):
                                o = (half * C + c) * P
                                ins = pe.matmul(up_bank(f, slot, half)[:, :], w1[:, p, o:o + P],
                                                xall[:, ds(g * G * P, G * P)], start=True, stop=True)
                            ins.then_inc(s.up_ps, 1)
                    if within(g, 1, NG + 1):
                        pe.wait_ge(s.h, it * C + R)
                        pe.wait_ge(s.x, it)
                        for i in range(G):
                            for c in range(C):
                                ins = pe.matmul(bank[6 + (1 - u)][:, i * D:(i + 1) * D],
                                                hid[:, 1 - u, c, i * P:(i + 1) * P], w2[:, p, c, :],
                                                start=(c == 0), stop=(c == C - 1))
                        ins.then_inc(s.y_ps, 1)

                steps(pe, step, NG + 1, 2, 1)

            over_experts(pe, f, expert)
            phase_end(pe)

        def ffn_act(act, f):
            s, C, R = f.s, f.chunks, f.slots
            phase_start(act, f.phase)

            def front(n, u):
                act.wait_ge(s.xt_ps, n + 1)
                at_least(act, s.xall, n - 1)
                if f.ranks:
                    at_least(act, s.l_ps, n - 1)
                nc.scalar.copy(xnT[:, u, :], bank[0][:, :]).then_inc(s.xt_sb, 1)

            steps(act, front, NG, 2, 2)
            if f.ranks:
                act.wait_ge(s.gate_step, 2)
                nc.scalar.activation(ga[:, :, :], gc[:, :, :], ACT.Exp).then_inc(s.ex, 1)
            if f.biased:
                def bias(n, u):
                    act.wait_ge(s.gt_ps, n + 1)
                    at_least(act, s.bb_ps, n)
                    nc.scalar.copy(gT[:, :], bank[5][0:NE, :]).then_inc(s.gt_sb, 1)

                steps(act, bias, NG, 2, 2)
            if not f.gated:
                act.sem_inc(s.h, R)

            def expert(e, p, i):
                if f.experts > 1:
                    act.wait_ge((s.w0, s.w1)[p], i * 48 + 48)

                def step(g, u):
                    it = e * NG + g
                    act.wait_ge(s.y_ps, it + 1)
                    for c in range(C):
                        src = up_bank(f, chunk_at(f, u, c))[:, :]
                        act.wait_ge(s.up_ps, it * C + c + 1)
                        if f.gated:
                            act.wait_ge(s.h, it * C + c - 1 + R)
                            nc.scalar.activation(silu[:, c % 2 if C % 2 == 0 else (u + c) % 2, :], src,
                                                 ACT.Silu).then_inc(s.act, 1)
                        elif f.biased:
                            nc.scalar.activation(hid[:, u, c, :], src, f.func, bias=b1[:, p, c:c + 1])\
                                .then_inc(s.h, 1)

                steps(act, step, NG, 2, 2)

            over_experts(act, f, expert)
            phase_end(act)

        def ffn_pool(pool, f):
            s = f.s
            phase_start(pool, f.phase)
            clear_last_phase(pool, f.phase)
            ln_rstd(pool, s, 0, 0, G)

            def front(n, u):
                if within(n, 0, NG - 1):
                    ln_rstd(pool, s, n + 1, 1 - u, G)
                pool.wait_ge(s.xt_sb, n + 1)
                pool.tensor_copy(xall[:, ds(n * G * P, G * P)], xnT[:, u, :]).then_inc(s.xall, 1)

            steps(pool, front, NG, 2, 2)
            phase_end(pool)

        def softmax_and_choice(dve, f):
            s = f.s
            done = [0]

            def link(ins):
                done[0] += 1
                ins.then_inc(s.gate_step, 1)
                dve.wait_ge(s.gate_step, done[0])

            def per_expert(ap):
                return ap.unsqueeze(2).to_broadcast([P, NB, NE])

            if f.layer == 2:
                dve.memset(pick[:, :, 1, :], 0.0).then_inc(s.zeroed, 1)
            src = lg[:, :, :]
            dve.wait_ge(s.lg, NG)
            link(dve.reduce_max(gtmp[:, :], src, AX.X))
            link(dve.tensor_tensor(gc[:, :, :], src, per_expert(gtmp[:, :]), ALU.subtract))
            dve.wait_ge(s.ex, 1)
            link(dve.reduce_sum(gtmp[:, :], ga[:, :, :], AX.X))
            link(dve.reciprocal(gtmp[:, :], gtmp[:, :]))
            link(dve.tensor_tensor(ga[:, :, :], ga[:, :, :], per_expert(gtmp[:, :]), ALU.mult))
            for r in range(f.ranks):
                link(dve.reduce_max(gtop[:, r, :], ga[:, :, :], AX.X))
                link(dve.tensor_tensor(gc[:, :, :], ga[:, :, :], per_expert(gtop[:, r, :]), ALU.is_equal))
                link(dve.tensor_tensor(gc[:, :, :], gc[:, :, :],
                                       order[:, :].unsqueeze(1).to_broadcast([P, NB, NE]), ALU.mult))
                link(dve.reduce_max(gtmp[:, :], gc[:, :, :], AX.X))
                chosen = pick[:, :, r, :].rearrange("p e b -> p b e")
                link(dve.tensor_tensor(chosen, gc[:, :, :], per_expert(gtmp[:, :]), ALU.is_equal))
                if r + 1 < f.ranks:
                    link(dve.scalar_tensor_tensor(out=ga[:, :, :], in0=chosen, scalar=-2.0, in1=ga[:, :, :],
                                                  op0=ALU.mult, op1=ALU.add))
            if f.sorted:
                assert done[0] == CHOSEN[f.ranks]
                return link, done
            out_view = gates[:, :, :]
            for r in range(f.ranks):
                link(dve.tensor_tensor(pick[:, :, r, :], pick[:, :, r, :],
                                       gtop[:, r, :].unsqueeze(1).to_broadcast([P, NE, NB]), ALU.mult))
            if f.ranks == 2:
                link(dve.tensor_tensor(out_view, pick[:, :, 0, :].rearrange("p e b -> p b e"),
                                       pick[:, :, 1, :].rearrange("p e b -> p b e"), ALU.add))
            else:
                link(dve.tensor_copy(out_view, pick[:, :, 0, :].rearrange("p e b -> p b e")))

        gate_of = gates[:, :, :].rearrange("p b e -> p (b e)")

        CHOSEN = {1: 10, 2: 16}


        sort_ = work[:, 4928:5600]
        tile_start = sort_[:, 0:NT]
        spare = sort_[:, 40:40 + 2 * NB]
        cap_start = sort_[:, 104:104 + NE]
        tiles_of = sort_[:, 112:112 + NE]
        base = sort_[:, 120:120 + NE]
        slot_f = sort_[:, 128:192]
        keep = sort_[:, 192:256]
        slot_out = sort_[:, 256:320].bitcast(U32)
        slot_in = sort_[:, 320:384].bitcast(U32)
        expert_f = sort_[:, 384:384 + NT]
        expert_of = sort_[:, 424:424 + NT].bitcast(I32)
        iota_i = sort_[:, 464:464 + 112].bitcast(I32)
        slot_g = sort_[:, 576:640]
        flat = pick[:, :, :, :].rearrange("p e k b -> p (e k b)")
        w1all = raw[:, 0:NE * 1024]
        b2all = work[:, 0:NE * D]
        xin = score[:, :, 0:BANK]
        yout = silu
        second = hid[:, :, :, :].rearrange("p a b c -> p (a b c)")
        tokens = xall[:, :].rearrange("p (b d) -> p b d", d=D)

        def sorted_front_pe(pe, f):
            s = f.s
            phase_start(pe, f.phase)
            pe.wait_ge(f.load, 16 * f.loads)

            def front(n, u):
                pe.wait_ge(s.xn, n + 1)
                at_least(pe, s.xt_sb, n)
                for i in range(G):
                    ins = pe.transpose(bank[0][:, i * P:(i + 1) * P], xn[:, i, :], ident[:, :])
                ins.then_inc(s.xt_ps, 1)
                pe.wait_ge(s.xt_sb, n + 1)
                at_least(pe, s.lg, n - 1)
                for i in range(G):
                    ins = pe.matmul(bank[1 + u][:, i * NE:(i + 1) * NE], xnT[:, u, i * P:(i + 1) * P],
                                    wr[:, f.layer, :], start=True, stop=True)
                ins.then_inc(s.l_ps, 1)

            steps(pe, front, NG, 2, 2)
            pe.wait_ge(s.gate_step, CHOSEN[f.ranks])
            if f.ranks == 1:
                pe.wait_ge(s.zeroed, 1)
            pe.wait_ge(const.ready, 3)
            pe.matmul(bank[3][:, :], upper[:, :], flat, start=True, stop=True)
            pe.matmul(bank[4][:, :], ones[:, :], flat, start=True, stop=True).then_inc(s.cnt_ps, 1)

        def sorted_front_act(act, f):
            s = f.s
            phase_start(act, f.phase)

            def front(n, u):
                act.wait_ge(s.xt_ps, n + 1)
                at_least(act, s.l_ps, n - 1)
                nc.scalar.copy(xnT[:, u, :], bank[0][:, :]).then_inc(s.xt_sb, 1)

            steps(act, front, NG, 2, 2)
            act.wait_ge(s.gate_step, 2)
            nc.scalar.activation(ga[:, :, :], gc[:, :, :], ACT.Exp).then_inc(s.ex, 1)

        def sorted_front_pool(pool, f):
            s = f.s
            phase_start(pool, f.phase)
            clear_last_phase(pool, f.phase)
            ln_rstd(pool, s, 0, 0, G)

            def front(n, u):
                if within(n, 0, NG - 1):
                    ln_rstd(pool, s, n + 1, 1 - u, G)
                pool.wait_ge(s.xn, n + 1)
                pool.tensor_copy(tokens[:, ds(n * G, G), :], xn[:, :, :]).then_inc(s.xall, 1)

            steps(pool, front, NG, 2, 2)
            pool.iota(iota_i[:, 0:NT], [[P, NT]], base=0, channel_multiplier=0).then_inc(s.counts, 1)
            if f.layer == 0:
                pool.iota(iota_i[:, 40:104], [[P, 2 * NB]], base=SPARE, channel_multiplier=1).then_inc(s.counts, 1)
                pool.iota(iota_i[:, 104:112], [[CAP, NE]], base=0, channel_multiplier=0).then_inc(s.counts, 1)
            pool.wait_ge(s.gate_step, SLOTTED[f.layer])
            pool.wait_ge(s.xall, NG)
            pool.wait_ge(const.slots, 16 * (SPARE // (NB * P)))
            for k in range(f.ranks):
                for b in range(NB):
                    c = k * NB + b
                    pool.indirect_dma_start(slots_x, bass.IndirectOffsetOnAxis(ap=slot_in[:, c:c + 1], axis=0),
                                            tokens[:, b, :], None).then_inc(loads.scattered, 16)

        def all_stored(pool, f, out0, out1):
            s = f.s
            pool.wait_ge(loads.scattered, 16 * f.scatters)
            pool.wait_ge(s.out0, 16 * out0)
            pool.wait_ge(s.out1, 16 * out1)

        def gather(pool, f, g):
            for b in range(g * G, (g + 1) * G):
                for k in range(f.ranks):
                    dst = (tokens[:, b, :], second[:, b * D:(b + 1) * D])[k]
                    c = k * NB + b
                    pool.indirect_dma_start(dst, None, slots_y,
                                            bass.IndirectOffsetOnAxis(ap=slot_out[:, c:c + 1], axis=0))\
                        .then_inc(loads.gathered[b // 8], 16)

        def sorted_front_dve(dve, f):
            s = f.s
            phase_start(dve, f.phase)
            dve.wait_ge(f.load, 16 * f.loads)

            def normalise(n, u):
                ln_stats(dve, s, n, u, G)
                at_least(dve, s.xall, n)
                ln_apply(dve, s, n, u, G, s.xt_ps)

            normalise(0, 0)

            def front(n, u):
                if within(n, 0, NG - 1):
                    normalise(n + 1, 1 - u)
                dve.wait_ge(s.l_ps, n + 1)
                dst = lg[:, ds(n * G, G), :]
                src = bank[1 + u][:, 0:G * NE].rearrange("p (g e) -> p g e", g=G)
                if f.layer == 2:
                    dve.tensor_tensor(dst, src, rb[:, :].unsqueeze(1).to_broadcast([P, G, NE]), ALU.add)\
                       .then_inc(s.lg, 1)
                else:
                    dve.tensor_copy(dst, src).then_inc(s.lg, 1)

            steps(dve, front, NG, 2, 2)
            link, done = softmax_and_choice(dve, f)
            per_e = pref[:, :].rearrange("p (e n) -> p e n", e=NE)

            def places():
                dve.wait_ge(s.cnt_ps, 1)
                link(dve.tensor_tensor_scan(pref[:, :], first[:, :], bank[4][:, :], 0.0, ALU.mult, ALU.add))
                if f.layer == 2:
                    dve.wait_ge(s.counts, 1)
                    link(dve.tensor_copy(tile_start, iota_i[:, 0:NT]))
                    cmp = lg[:, :, :].rearrange("p b e -> p (b e)")
                    link(dve.tensor_copy(slot_g[:, 0:NE], per_e[:, :, 2 * NB - 1]))
                    c3 = compare.rearrange("p (e t) -> p e t", e=NE)
                    link(dve.tensor_tensor(c3, slot_g[:, 0:NE].unsqueeze(2).to_broadcast([P, NE, NT]),
                                           tile_start.unsqueeze(1).to_broadcast([P, NE, NT]), ALU.is_gt))
                    link(dve.reduce_sum(base, c3, AX.X))
                    link(dve.tensor_scalar(base, base, float(P), None, ALU.mult))
                    link(dve.tensor_tensor_scan(tiles_of, ones[:, 0:NE], base, 0.0, ALU.mult, ALU.add))
                    link(dve.tensor_tensor(base, tiles_of, base, ALU.subtract))
                    c3 = compare.rearrange("p (t e) -> p t e", e=NE)
                    link(dve.tensor_tensor(c3, tile_start.unsqueeze(2).to_broadcast([P, NT, NE]),
                                           tiles_of.unsqueeze(1).to_broadcast([P, NT, NE]), ALU.is_ge))
                    link(dve.reduce_sum(expert_f, c3, AX.X))
                    link(dve.tensor_scalar(expert_f, expert_f, float(NE - 1), None, ALU.min))
                    link(dve.tensor_copy(expert_of, expert_f))
                else:
                    dve.wait_ge(s.counts, 3)
                    link(dve.tensor_copy(spare, iota_i[:, 40:104]))
                    link(dve.tensor_copy(base, iota_i[:, 104:112]))
                link(dve.tensor_tensor(pref[:, :], pref[:, :], bank[4][:, :], ALU.subtract))
                link(dve.tensor_tensor(pref[:, :], pref[:, :], bank[3][:, :], ALU.add))

            by_choice = flat.rearrange("p (e n) -> p n e", e=NE)
            places()
            if f.layer == 0:
                link(dve.tensor_tensor(gtmp[:, :], gtop[:, 0, :], gtop[:, 1, :], ALU.add))
                link(dve.reciprocal(gtmp[:, :], gtmp[:, :]))
                link(dve.tensor_tensor(gtop[:, :, :], gtop[:, :, :],
                                       gtmp[:, :].unsqueeze(1).to_broadcast([P, 2, NB]), ALU.mult))
                kept = lg[:, :, :].rearrange("p b e -> p (b e)")
                link(dve.tensor_tensor(slot_all, pref[:, :], flat, ALU.mult))
                link(dve.reduce_sum(slot_f, slot_all.rearrange("p (e n) -> p n e", e=NE), AX.X))
                link(dve.tensor_scalar(keep, slot_f, float(CAP), None, ALU.is_le))
                link(dve.tensor_tensor(gtop[:, :, :].rearrange("p k b -> p (k b)"),
                                       gtop[:, :, :].rearrange("p k b -> p (k b)"), keep, ALU.mult))
            link(dve.tensor_tensor(per_e, per_e, base.unsqueeze(2).to_broadcast([P, NE, 2 * NB]), ALU.add))
            link(dve.tensor_tensor(flat, flat, pref[:, :], ALU.mult))
            link(dve.reduce_sum(slot_f, by_choice, AX.X))
            link(dve.tensor_scalar(slot_f, slot_f, 1.0, None, ALU.subtract))
            if f.layer == 0:
                link(dve.tensor_tensor(slot_f, slot_f, keep, ALU.mult))
                link(dve.tensor_tensor(slot_g, spare, keep, ALU.mult))
                link(dve.tensor_tensor(slot_g, spare, slot_g, ALU.subtract))
                link(dve.tensor_tensor(slot_g, slot_f, slot_g, ALU.add))
                link(dve.tensor_copy(slot_out, slot_f))
                link(dve.tensor_copy(slot_in, slot_g))
            else:
                link(dve.tensor_copy(slot_out[:, 0:NB], slot_f[:, 0:NB]))
                link(dve.tensor_copy(slot_in[:, 0:NB], slot_f[:, 0:NB]))
            assert done[0] == SLOTTED[f.layer], done[0]

        SLOTTED = {0: 38, 2: 30}
        compare = xin_free = score[:, 1, 512:512 + NE * NT]
        slot_all = score[:, 1, 512:1024]

        def sorted_back_dve(dve, f):
            s = f.s
            for q in range(4):
                dve.wait_ge(loads.gathered[q], 16 * f.scatters // 4)
                for k in range(f.ranks):
                    if k:
                        dve.wait_ge(s.first_added, q + 1)
                    src = (xall, second)[k]
                    with dve.Fori(q * 8, q * 8 + 8) as b:
                        x = tile(b)
                        dve.scalar_tensor_tensor(out=x, in0=src[:, ds(b * D, D)], scalar=gtop[:, k, ds(b, 1)],
                                                 in1=x, op0=ALU.mult, op1=ALU.add)
                    if k + 1 < f.ranks:
                        dve.drain().then_inc(s.first_added, 1)

        N0 = SPARE // BANK

        def parity_in(s, j):
            return (s.in0, s.in1)[j % 2]

        def parity_out(s, j):
            return (s.out0, s.out1)[j % 2]

        def sorted0_sp(sp, f):
            s = f.s
            phase_start(sp, f.phase)
            sp.dma_start(b2all.rearrange("p (e d) -> p e d", e=NE), t["L0_b2"].partition_broadcast(P)).then_inc(f.load, 16)

            def weights(e, p):
                w = (s.w0, s.w1)[p]
                sp.dma_start(w1[:, p, 0:4 * P], row(t["L0_w1"], e)).then_inc(w, 16)
                sp.dma_start(w2[:, p, :, :], expert_w2(t["L0_w2"], e)).then_inc(w, 16)
                sp.dma_start(b1[:, p, :], row(t["L0_b1"], e)).then_inc(w, 16)

            def load(m, j):
                sp.dma_start(xin[:, j % 2, :].rearrange("p (t d) -> p t d", d=D),
                             slots_x[ds(m * BANK, BANK), :].rearrange("(t p) d -> p t d", p=P))\
                  .then_inc(parity_in(s, j), 16)

            weights(0, 0)
            weights(1, 1)
            sp.wait_ge(loads.scattered, 16 * f.scatters)
            load(0, 0)
            load(1, 1)

            def step(m, j):
                if within(m, 0, N0 - 2):
                    sp.wait_ge(s.in_ps, m + 1)
                    load(m + 2, j)
                if within(m, 2, N0 + 2):
                    sp.wait_ge(s.y_sb, m - 1)
                    sp.dma_start(slots_y[ds((m - 2) * BANK, BANK), :].rearrange("(t p) d -> p t d", p=P),
                                 yout[:, j % 2, :].rearrange("p (t d) -> p t d", d=D)).then_inc(parity_out(s, j), 16)
                if j % 2 == 1 and within(m, 3, N0 - 2):
                    weights((m + 1) // 2 if isinstance(m, int) else (m - j) // 2 + (j + 1) // 2,
                            ((j + 1) // 2) % 2)

            steps(sp, step, N0 + 2, 4, 6, by=4)

        def sorted0_pe(pe, f):
            s = f.s
            sorted_front_pe(pe, f)

            def turn(m, j):
                pe.wait_ge(parity_in(s, j), 8 * m + 16 - 8 * (j % 2))
                at_least(pe, s.in_sb, m)
                for i in range(4):
                    ins = pe.transpose(bank[0][:, i * P:(i + 1) * P], xin[:, j % 2, i * P:(i + 1) * P], ident[:, :])
                ins.then_inc(s.in_ps, 1)

            turn(0, 0)

            def step(n, j):
                u = j % 2
                if within(n, 0, N0):
                    p = j // 2
                    pe.wait_ge((s.w0, s.w1)[p], 12 * (n - j) + 48)
                    pe.wait_ge(s.in_sb, n + 1)
                    for c in range(4):
                        at_least(pe, s.h, 4 * (n - 1) + c + 1)
                        pe.matmul(bank[1 + c][:, :], w1[:, p, c * P:(c + 1) * P], xnT[:, u, :], start=True, stop=True)\
                          .then_inc(s.up_ps, 1)
                if within(n, 0, N0 - 1):
                    turn(n + 1, j + 1)
                if within(n, 1, N0 + 1):
                    p = ((j - 1) % 4) // 2
                    pe.wait_ge(s.h, 4 * n)
                    at_least(pe, s.y_sb, n - 2)
                    for i in range(4):
                        for c in range(4):
                            ins = pe.matmul(bank[6 - u][:, i * D:(i + 1) * D], hid[:, 1 - u, c, i * P:(i + 1) * P],
                                            w2[:, p, c, :], start=(c == 0), stop=(c == 3))
                    ins.then_inc(s.y_ps, 1)

            def stepped(n, j):
                step(n, j)

            steps(pe, stepped, N0 + 1, 4, 5, by=4)
            phase_end(pe)

        def sorted0_act(act, f):
            s = f.s
            sorted_front_act(act, f)

            def turn(m, j):
                act.wait_ge(s.in_ps, m + 1)
                at_least(act, s.up_ps, 4 * (m - 1))
                nc.scalar.copy(xnT[:, j % 2, :], bank[0][:, :]).then_inc(s.in_sb, 1)

            turn(0, 0)

            def step(n, j):
                act.wait_ge((s.w0, s.w1)[j // 2], 12 * (n - j) + 48)
                at_least(act, s.y_ps, n - 1)
                for c in range(4):
                    act.wait_ge(s.up_ps, 4 * n + c + 1)
                    nc.scalar.activation(hid[:, j % 2, c, :], bank[1 + c][:, :], ACT.Relu,
                                         bias=b1[:, j // 2, c:c + 1]).then_inc(s.h, 1)
                if within(n, 0, N0 - 1):
                    turn(n + 1, j + 1)

            steps(act, step, N0, 4, 4, by=4)
            phase_end(act)

        def sorted0_pool(pool, f):
            sorted_front_pool(pool, f)
            all_stored(pool, f, N0 // 2, N0 // 2)
            for g in range(NG):
                gather(pool, f, g)
            phase_end(pool)

        def sorted0_dve(dve, f):
            s = f.s
            sorted_front_dve(dve, f)

            def step(m, j):
                dve.wait_ge(s.y_ps, m + 1)
                at_least(dve, parity_out(s, j), 8 * (m - j % 2))
                e = m // 2 if isinstance(m, int) else (m - j) // 2 + j // 2
                dve.tensor_tensor(yout[:, j % 2, :].rearrange("p (t d) -> p t d", d=D),
                                  bank[5 + j % 2][:, :].rearrange("p (t d) -> p t d", d=D),
                                  b2all[:, ds(e * D, D)].unsqueeze(1).to_broadcast([P, 4, D]), ALU.add)\
                   .then_inc(s.y_sb, 1)

            steps(dve, step, N0, 4, 4, by=4)
            sorted_back_dve(dve, f)
            phase_end(dve)

        def sorted2_sp(sp, f):
            s = f.s
            phase_start(sp, f.phase)
            sp.wait_ge(loads.scattered, 16 * f.scatters)

            def load(m, u):
                sp.dma_start(xin[:, u, 0:D], slots_x[ds(m * P, P), :]).then_inc(parity_in(s, u), 16)

            load(0, 0)
            load(1, 1)

            def step(m, u):
                if within(m, 0, NT - 2):
                    sp.wait_ge(s.in_ps, m + 1)
                    load(m + 2, u)
                if within(m, 2, NT + 2):
                    sp.wait_ge(s.y_sb, m - 1)
                    sp.dma_start(slots_y[ds((m - 2) * P, P), :], yout[:, u, 0:D]).then_inc(parity_out(s, u), 16)

            steps(sp, step, NT + 2, 2, 5)

        def sorted2_pe(pe, f):
            s = f.s
            sorted_front_pe(pe, f)
            up_w = w1all.rearrange("p (h n) -> p h n", n=BANK)
            down_w = fold[:, :].rearrange("p (q d) -> p q d", d=D)

            def turn(m, u):
                pe.wait_ge(parity_in(s, u), 8 * m + 16 - 8 * u)
                pe.transpose(bank[0][:, u * P:(u + 1) * P], xin[:, u, 0:D], ident[:, :]).then_inc(s.in_ps, 1)

            def expert(m):
                return pe.value_load(expert_of[0:1, ds(m, 1)], min_val=0, max_val=NE - 1)

            turn(0, 0)

            def step(n, u):
                if within(n, 0, NT):
                    e = expert(n)
                    pe.wait_ge(s.in_sb, n + 1)
                    at_least(pe, s.h, n - 1)
                    for half in (0, 1):
                        ins = pe.matmul(bank[1 + 2 * u + half][:, :], xnT[:, u, 0:P],
                                        up_w[:, ds(e * 2 + half, 1), :].rearrange("p a n -> p (a n)"),
                                        start=True, stop=True)
                    ins.then_inc(s.up_ps, 1)
                if within(n, 0, NT - 1):
                    turn(n + 1, 1 - u)
                if within(n, 1, NT + 1):
                    pe.wait_ge(s.h, n)
                    at_least(pe, s.ht_sb, n - 1)
                    for c in range(4):
                        ins = pe.transpose(bank[5][:, c * P:(c + 1) * P], hid[:, 1 - u, 0, c * P:(c + 1) * P],
                                           ident[:, :])
                    ins.then_inc(s.ht_ps, 1)
                if within(n, 2, NT + 2):
                    e = expert(n - 2)
                    pe.wait_ge(s.ht_sb, n - 1)
                    at_least(pe, s.y_sb, n - 3)
                    for c in range(4):
                        ins = pe.matmul(bank[6 + u][:, 0:D], hid[:, u, 1, c * P:(c + 1) * P],
                                        down_w[:, ds(e * 4 + c, 1), :].rearrange("p a n -> p (a n)"),
                                        start=(c == 0), stop=(c == 3))
                    ins.then_inc(s.y_ps, 1)

            steps(pe, step, NT + 2, 4, 3)
            phase_end(pe)

        def sorted2_act(act, f):
            s = f.s
            sorted_front_act(act, f)

            def turn(m, u):
                act.wait_ge(s.in_ps, m + 1)
                at_least(act, s.up_ps, m - 1)
                nc.scalar.copy(xnT[:, u, 0:P], bank[0][:, u * P:(u + 1) * P]).then_inc(s.in_sb, 1)

            turn(0, 0)

            def step(n, u):
                if within(n, 0, NT):
                    act.wait_ge(s.up_ps, n + 1)
                    at_least(act, s.h, n - 1)
                    nc.scalar.activation(hid[:, u, 2, :], bank[1 + 2 * u][:, :], ACT.Silu).then_inc(s.act, 1)
                if within(n, 0, NT - 1):
                    turn(n + 1, 1 - u)
                if within(n, 1, NT + 1):
                    act.wait_ge(s.ht_ps, n)
                    at_least(act, s.y_ps, n - 2)
                    nc.scalar.copy(hid[:, 1 - u, 1, :], bank[5][:, :]).then_inc(s.ht_sb, 1)

            steps(act, step, NT + 1, 4, 4)
            phase_end(act)

        def sorted2_pool(pool, f):
            sorted_front_pool(pool, f)
            all_stored(pool, f, (NT + 1) // 2, NT // 2)
            phase_end(pool)

        def sorted2_dve(dve, f):
            s = f.s
            sorted_front_dve(dve, f)

            def step(n, u):
                if within(n, 0, NT):
                    dve.wait_ge(s.act, n + 1)
                    at_least(dve, s.ht_ps, n - 1)
                    dve.tensor_tensor(hid[:, u, 0, :], bank[2 + 2 * u][:, :], hid[:, u, 2, :], ALU.mult)\
                       .then_inc(s.h, 1)
                if within(n, 2, NT + 2):
                    dve.wait_ge(s.y_ps, n - 1)
                    at_least(dve, parity_out(s, u), 8 * (n - 2 - u))
                    dve.tensor_copy(yout[:, u, 0:D], bank[6 + u][:, 0:D]).then_inc(s.y_sb, 1)

            steps(dve, step, NT + 2, 4, 3)
            phase_end(dve)

        def ffn_dve(dve, f):
            s, C, R = f.s, f.chunks, f.slots
            phase_start(dve, f.phase)
            dve.wait_ge(f.load, 16 * 2)
            ln_stats(dve, s, 0, 0, G)
            ln_apply(dve, s, 0, 0, G, s.xt_ps)
            if f.layer == 3:
                w1i, w2i = lay3.w1i, lay3.w2i
                dve.tensor_scalar(w1[:, 0, 0:768], w1i, 1.0 / 127.0, None, ALU.mult)
                dve.tensor_scalar(w2[:, 0, 0:3, :], w2i, 1.0 / 127.0, None, ALU.mult).then_inc(s.w0, 1)

            def front(n, u):
                if within(n, 0, NG - 1):
                    ln_stats(dve, s, n + 1, 1 - u, G)
                    ln_apply(dve, s, n + 1, 1 - u, G, s.xt_ps)
                if f.ranks:
                    dve.wait_ge(s.l_ps, n + 1)
                    dst = lg[:, ds(n * G, G), :]
                    src = bank[1 + u][:, 0:G * NE].rearrange("p (g e) -> p g e", g=G)
                    if f.layer == 2:
                        dve.tensor_tensor(dst, src, rb[:, :].unsqueeze(1).to_broadcast([P, G, NE]), ALU.add)\
                           .then_inc(s.lg, 1)
                    else:
                        dve.tensor_copy(dst, src).then_inc(s.lg, 1)

            steps(dve, front, NG, 2, 2)
            if f.ranks:
                softmax_and_choice(dve, f)
            if f.biased:
                def bias(n, u):
                    at_least(dve, s.gt_ps, n)
                    dve.tensor_copy(gb[:, :], gates[:, ds(n * G, G), :].rearrange("p g e -> p (g e)"))\
                       .then_inc(s.gb, 1)
                    dve.wait_ge(s.bb_ps, n + 1)
                    x = X[:, ds(n * G, G), :]
                    dve.tensor_tensor(x, bank[6][:, :].rearrange("p (g d) -> p g d", g=G), x, ALU.add)\
                       .then_inc(s.bb, 1)

                steps(dve, bias, NG, 2, 2)
                dve.wait_ge(s.bb, NG)
            dve.sem_inc(s.x, 2)
            if f.gated:
                dve.sem_inc(s.h, R)

            def expert(e, p, i):
                def step(g, u):
                    it = e * NG + g
                    if f.gated and within(g, 0, NG):
                        dve.wait_ge(s.y_ps, it + 1)
                        for c in range(C):
                            dve.wait_ge(s.act, it * C + c + 1)
                            dve.tensor_tensor(hid[:, u, c, :], up_bank(f, chunk_at(f, u, c), 1)[:, :],
                                              silu[:, c % 2 if C % 2 == 0 else (u + c) % 2, :], ALU.mult)\
                               .then_inc(s.h, 1)
                    if within(g, 1, NG + 1):
                        y = bank[6 + (1 - u)][:, :].rearrange("p (g d) -> p g d", g=G)
                        dve.wait_ge(s.y_ps, it + 2)
                        dve.wait_ge(s.x, it + 1)
                        if f.ranks:
                            for i in range(G):
                                x = tile((g - 1) * G + i)
                                gate = gate_of[:, ds(((g - 1) * G + i) * NE + e, 1)]
                                ins = dve.scalar_tensor_tensor(out=x, in0=y[:, i, :], scalar=gate, in1=x, op0=ALU.mult, op1=ALU.add)
                        else:
                            x = X[:, ds((g - 1) * G, G), :]
                            ins = dve.tensor_tensor(x, y, x, ALU.add)
                        ins.then_inc(s.x, 1)

                steps(dve, step, NG + 1, 2, 1)

            over_experts(dve, f, expert)
            phase_end(dve)

        attn = [Attention(0, 0, 8), Attention(1, 2, 16)]
        ffn = [Ffn(0, 1, NE, 4, ACT.Relu, False, 2, True, True),
               Ffn(1, 3, NE, 1, ACT.Gelu_apprx_tanh, False, 2, True, True),
               Ffn(2, 5, NE, 4, ACT.Silu, True, 1, True, False),
               Ffn(3, 8, 1, 3, ACT.Silu, True, 0, False, False)]

        class lay3:
            w1i = raw[:, 9216:9984].bitcast(I32)
            w2i = raw[:, 9984:10368].bitcast(I32).rearrange("p (c d) -> p c d", c=3)

        def row(ap, e):
            return ap[ds(e, 1)].rearrange("a p n -> (a p) n")

        def expert_w2(ap, e):
            return ap[ds(e, 1)].rearrange("a p c d -> (a p) c d")

        def small():
            sp = nc.sync
            for i in range(3):
                q = f"L{i}_"
                sp.dma_start(obias[:, i, :], t[q + "bo"].partition_broadcast(P)).then_inc(const.bias, 16)
            for i in range(2):
                sp.dma_start(wr[:, i, :], t[f"L{i}_wr"]).then_inc(ffn[i].load, 16)
                sp.dma_start(b2[:, i, :], t[f"L{i}_b2"]).then_inc(ffn[i].load, 16)
            sp.dma_start(wr[:, 2, :], t["L2_wr"]).then_inc(loads.ffn2, 16)
            sp.dma_start(rb[:, :], t["L2_rb"].partition_broadcast(P)).then_inc(loads.ffn2, 16)
            sp.dma_start(l2w[:, 0, :], t["L2_wq"]).then_inc(loads.l2, 16)
            sp.dma_start(l2w[0:DC, 1, :], t["L2_wk"]).then_inc(loads.l2, 16)
            sp.dma_start(l2w[0:DC, 2, :], t["L2_wv"]).then_inc(loads.l2, 16)
            sp.dma_start(l2b[:, 0:1], t["L2_bq"]).then_inc(loads.l2, 16)
            sp.dma_start(l2b[:, 1:2], t["L2_bk"]).then_inc(loads.l2, 16)
            for i, name in enumerate(("ln_x_g", "ln_x_b")):
                sp.dma_start(l3g[0:DC, i:i + 1], t["L3_" + name]).then_inc(loads.l3, 16)
            for i, name in enumerate(("ln_l_g", "ln_l_b", "qn_g")):
                sp.dma_start(l3g[:, 2 + i:3 + i], t["L3_" + name]).then_inc(loads.l3, 16)
            sp.dma_start(l3g[:, 6:7], t["L3_kn_g"]).then_inc(loads.l3, 16)
            sp.dma_start(l3w[:, 0:384], t["L3_wl"]).then_inc(loads.l3, 16)
            sp.dma_start(l3w[0:DC, 384:640], t["L3_wkv"]).then_inc(loads.l3, 16)
            sp.dma_start(l3w[:, 640:768], t["L3_wo"]).then_inc(loads.l3, 16)
            sp.dma_start(l3bo[:, :], t["L3_bo"].partition_broadcast(P)).then_inc(const.bias, 16)

        block = ctx.enter_context(nc.Block())

        @block.sync
        def _(sp):
            sp.dma_start(X[:, :, :], t["x"].rearrange("b s d -> s b d")).then_inc(loads.x, 16)
            sp.dma_start(ctxT[:, :], t["ctxT"]).then_inc(loads.x, 16)
            for a in attn:
                q = f"L{a.layer}_"
                sp.dma_start(a.wqT, t[q + "wqT"]).then_inc(a.load, 16)
                sp.dma_start(a.wkT, t[q + "wkT"]).then_inc(a.load, 16)
                sp.dma_start(a.wvT, t[q + "wvT"]).then_inc(a.load, 16)
                sp.dma_start(a.woh, t[q + "wo"]).then_inc(a.load, 16)
                if a.layer == 0:
                    small()
            sp.wait_ge(const.cleared, 1)
            for i in range(SPARE // (NB * P)):
                sp.dma_start(slots_x[i * NB * P:(i + 1) * NB * P, :].rearrange("(p r) d -> p (r d)", p=P), xall[:, :])\
                  .then_inc(const.slots, 16)
            sorted0_sp(sp, ffn[0])
            phase_start(sp, ffn[1].phase)
            sp.dma_start(w1all.rearrange("p (e n) -> p e n", e=NE), t["L2_w1"].rearrange("e p n -> p e n"))\
              .then_inc(loads.ffn2, 16)
            sp.dma_start(fold[:, :].rearrange("p (e c d) -> p e c d", e=NE, c=4), t["L2_w2"].rearrange("e p c d -> p e c d"))\
              .then_inc(loads.ffn2, 16)
            ffn_sp(sp, ffn[1], lambda e: row(t["L1_w1"], e), lambda e: expert_w2(t["L1_w2"], e),
                   lambda e: row(t["L1_b1"], e))
            phase_start(sp, ffn[2].phase)
            sp.dma_start(ctxn, t["ctx"].rearrange("b s c -> s b c")).then_inc(loads.ctxn, 16)
            sp.dma_start(mask8[:, :], t["mask"].partition_broadcast(P)).then_inc(loads.ctxn, 16)
            sp.dma_start(lay3.w1i, t["L3_w1"]).then_inc(loads.ffn3, 16)
            sp.dma_start(lay3.w2i, t["L3_w2"]).then_inc(loads.ffn3, 16)
            sorted2_sp(sp, ffn[2])
            phase_start(sp, 9)
            sp.dma_start(out.rearrange("b s d -> s b d"), X[:, :, :]).then_inc(loads.out, 16)
            sp.wait_ge(loads.out, 16)

        @block.gpsimd
        def _(pool):
            pool.memset(xall[:, :], 0.0).then_inc(const.cleared, 1)
            pool.memset(mhalf[:, :], -0.5).then_inc(const.zero, 1)
            pool.memset(ones[:, :], 1.0).then_inc(const.zero, 1)
            pool.memset(epss[:, :], EPS).then_inc(const.zero, 1)
            pool.memset(first[:, :], 1.0).then_inc(const.zero, 1)
            pool.memset(ident[:, :], 0.0).then_inc(const.zero, 1)
            pool.wait_ge(const.zero, 5)
            pool.affine_select(out=ident[:, :], in_=ident[:, :], compare_op=ALU.not_equal, fill=1.0, base=0,
                               pattern=[[-1, P]], channel_multiplier=1).then_inc(const.ready, 1)
            pool.affine_select(out=upper[:, :], in_=ones[:, :], compare_op=ALU.is_ge, fill=0.0, base=0,
                               pattern=[[1, P]], channel_multiplier=-1).then_inc(const.ready, 1)
            pool.memset(first[:, :].rearrange("p (e n) -> p e n", e=NE)[:, :, 0:1], 0.0).then_inc(const.ready, 1)
            for e in range(NE):
                pool.memset(order[:, e:e + 1], float(NE - e)).then_inc(const.order, 1)
            attn_pool(pool, attn[0])
            sorted0_pool(pool, ffn[0])
            attn_pool(pool, attn[1])
            ffn_pool(pool, ffn[1])
            attn2_pool(pool)
            sorted2_pool(pool, ffn[2])
            ctx3_pool(pool)
            attn3_pool(pool)
            ffn_pool(pool, ffn[3])

        @block.scalar
        def _(act):
            attn_act(act, attn[0])
            sorted0_act(act, ffn[0])
            attn_act(act, attn[1])
            ffn_act(act, ffn[1])
            attn2_act(act)
            sorted2_act(act, ffn[2])
            ctx3_act(act)
            attn3_act(act)
            ffn_act(act, ffn[3])

        @block.vector
        def _(dve):
            dve.wait_ge(const.bias, 16 * 4)
            dve.wait_ge(const.ready, 3)
            dve.wait_ge(const.order, NE)
            attn_dve(dve, attn[0])
            sorted0_dve(dve, ffn[0])
            attn_dve(dve, attn[1])
            ffn_dve(dve, ffn[1])
            attn2_dve(dve)
            sorted2_dve(dve, ffn[2])
            ctx3_dve(dve)
            attn3_dve(dve)
            ffn_dve(dve, ffn[3])

        @block.tensor
        def _(pe):
            attn_pe(pe, attn[0])
            sorted0_pe(pe, ffn[0])
            attn_pe(pe, attn[1])
            ffn_pe(pe, ffn[1])
            attn2_pe(pe)
            sorted2_pe(pe, ffn[2])
            ctx3_pe(pe)
            attn3_pe(pe)
            ffn_pe(pe, ffn[3])


_OUT = (NB, P, D)


def kernel(**inputs):
    import numpy as np
    import concourse.bacc as bacc
    from concourse.bass_utils import run_bass_kernel_spmd as run

    a = {k: np.asarray(v) for k, v in inputs.items()}

    def heads(w):
        return w.reshape(w.shape[0], -1, HD).transpose(2, 1, 0)

    def second(w):
        return w.reshape(w.shape[0], -1, P, D).transpose(0, 2, 1, 3)

    def hidden_bias(b):
        return b.reshape(b.shape[0], -1, P).transpose(0, 2, 1)

    arrays = {
        "x": a["x"], "ctx": a["ctx_768"],
        "ctxT": a["ctx_768"].transpose(2, 0, 1).reshape(DC, NB * S2),
        "mask": a["mask_BxS2_bk0"].reshape(NB * S2),
        "L0_w1": a["L0_ffn_w1"], "L0_w2": second(a["L0_ffn_w2"]), "L0_b1": hidden_bias(a["L0_ffn_b1"]),
        "L0_b2": a["L0_ffn_b2"], "L0_wr": a["L0_ffn_wg"],
        "L1_w1": a["L1_ffn_w_in"], "L1_w2": second(a["L1_ffn_w_out"]), "L1_b1": hidden_bias(a["L1_ffn_b_in"]),
        "L1_b2": a["L1_ffn_b_out"], "L1_wr": a["L1_ffn_router_w"],
        "L2_w1": a["L2_ffn_w1"], "L2_w2": second(a["L2_ffn_w2"]), "L2_wr": a["L2_ffn_router_w"],
        "L2_rb": a["L2_ffn_router_b"],
        "L2_wq": a["L2_xattn_Wq"], "L2_wk": a["L2_xattn_Wk"], "L2_wv": a["L2_xattn_Wv"],
        "L2_bq": a["L2_xattn_bq"].reshape(D, 1), "L2_bk": a["L2_xattn_bk"].reshape(D, 1),
        "L2_bo": a["L2_xattn_bv"],
        "L3_ln_x_g": a["L3_xattn_ln_x_g"].reshape(DC, 1), "L3_ln_x_b": a["L3_xattn_ln_x_b"].reshape(DC, 1),
        "L3_ln_l_g": a["L3_xattn_ln_l_g"].reshape(D, 1), "L3_ln_l_b": a["L3_xattn_ln_l_b"].reshape(D, 1),
        "L3_qn_g": np.tile(a["L3_xattn_qn_g"], 2).reshape(D, 1),
        "L3_kn_g": np.tile(a["L3_xattn_kn_g"], 2).reshape(D, 1),
        "L3_wl": np.concatenate([a["L3_xattn_Wq"], a["L3_xattn_Wlkv"]], 0).T,
        "L3_wkv": a["L3_xattn_Wkv"].T, "L3_wo": a["L3_xattn_Wo"].T, "L3_bo": a["L3_xattn_bo"],
        "L3_w1": np.concatenate([a["L3_ffn_w_gate"], a["L3_ffn_w_up"]], 0).T,
        "L3_w2": a["L3_ffn_w_down"].T.reshape(3, P, D).transpose(1, 0, 2),
    }
    for i in (0, 1):
        q = f"L{i}_xattn_"
        arrays |= {f"L{i}_wqT": heads(a[q + "Wq"]), f"L{i}_wkT": heads(a[q + "Wk"]), f"L{i}_wvT": heads(a[q + "Wv"]),
                   f"L{i}_wo": a[q + "Wo"].reshape(-1, HD, D).transpose(1, 0, 2), f"L{i}_bo": a[q + "bo"]}
    arrays = {k: np.ascontiguousarray(v) for k, v in arrays.items()}

    nc = bacc.Bacc("TRN2", target_bir_lowering=False, num_devices=1)
    t = {k: nc.dram_tensor("in_" + k, v.shape, mybir.dt.from_np(v.dtype), kind="ExternalInput").ap()
         for k, v in arrays.items()}
    out = nc.dram_tensor("out_dram", _OUT, F32, kind="ExternalOutput").ap()
    build(nc, t, out)
    return run(nc, [{"in_" + k: v for k, v in arrays.items()}], core_ids=[0]).results[0]["out_dram"]
```

```python
from contextlib import ExitStack

import concourse.bass as bass
from concourse import mybir

F32 = mybir.dt.float32
I32 = mybir.dt.int32
U8 = mybir.dt.uint8
U32 = mybir.dt.uint32
ALU = mybir.AluOpType
ACT = mybir.ActivationFunctionType
AX = mybir.AxisListType
ds = bass.ds

P = 128
NB = 32
D = 128
S2 = 77
DC = 96
HD = 64
NE = 8
G = 4
NG = NB // G
CAP = 2 * NB * P // NE
NT = NB + NE - 1
SPARE = NE * CAP
FILLS = SPARE // (16 * P)
FIRST = 2
EPS = 1e-5
RMS_EPS = 1e-8
FLT_MAX = 3.4028234663852886e38
BANK = 512
ENGINES = 4


def at_least(eng, sem, value):
    if isinstance(value, int) and value <= 0:
        return
    eng.wait_ge(sem, value)


def within(n, low, high):
    return not isinstance(n, int) or low <= n < high


def steps(eng, step, total, head, tail, by=2):
    for n in range(head):
        step(n, n % by)
    with eng.Fori(head // by, (total - tail) // by) as i:
        for u in range(by):
            step(i * by + u, u)
    for n in range(total - tail, total):
        step(n, n % by)


class Stage:

    def __init__(self, sem):
        self.bn = sem("bn")
        self.mv = sem("mv")
        self.ve = sem("ve")
        self.rstd = sem("rstd")
        self.xn = sem("xn")
        self.xt_ps = sem("xt_ps")
        self.xt_sb = sem("xt_sb")
        self.xall = sem("xall")
        self.ctx = sem("ctx")
        self.fold_ps = sem("fold_ps")
        self.fold_sb = sem("fold_sb")
        self.q_ps = sem("q_ps")
        self.q_sb = sem("q_sb")
        self.k_ps = sem("k_ps")
        self.k_sb = sem("k_sb")
        self.v_ps = sem("v_ps")
        self.v_sb = sem("v_sb")
        self.t_ps = sem("t_ps")
        self.t_sb = sem("t_sb")
        self.qkv_ps = sem("qkv_ps")
        self.sq = sem("sq")
        self.ss = sem("ss")
        self.sr = sem("sr")
        self.sr2 = sem("sr2")
        self.qk = sem("qk")
        self.qkt_ps = sem("qkt_ps")
        self.qt_sb = sem("qt_sb")
        self.kt_ps = sem("kt_ps")
        self.kt_sb = sem("kt_sb")
        self.s_ps = sem("s_ps")
        self.m1 = sem("m1")
        self.m2 = sem("m2")
        self.m3 = sem("m3")
        self.m4 = sem("m4")
        self.top = sem("top")
        self.shift = sem("shift")
        self.ex = sem("ex")
        self.tot = sem("tot")
        self.rec = sem("rec")
        self.probs = sem("probs")
        self.pt_ps = sem("pt_ps")
        self.pt_sb = sem("pt_sb")
        self.o_ps = sem("o_ps")
        self.o_sb = sem("o_sb")
        self.mask = sem("mask")
        self.l_ps = sem("l_ps")
        self.lg = sem("lg")
        self.gate_step = sem("gate_step")
        self.cnt_ps = sem("cnt_ps")
        self.gb = sem("gb")
        self.gt_ps = sem("gt_ps")
        self.gt_sb = sem("gt_sb")
        self.bb_ps = sem("bb_ps")
        self.bb = sem("bb")
        self.w0 = sem("w0")
        self.w1 = sem("w1")
        self.up_ps = sem("up_ps")
        self.act = sem("act")
        self.h = sem("h")
        self.zeroed = self.t_ps
        self.counts = self.t_sb
        self.in0, self.in1 = self.q_sb, self.k_ps
        self.in_ps, self.in_sb = self.k_sb, self.v_ps
        self.ht_ps, self.ht_sb = self.v_sb, self.pt_ps
        self.y_sb = self.pt_sb
        self.out0, self.out1 = self.sq, self.ss
        self.c_bn, self.c_mv, self.c_ve = self.m1, self.m2, self.m3
        self.slots_now = self.q_sb
        self.first_added = self.qt_sb
        self.second_added = self.kt_sb
        self.bn2, self.mv2, self.ve2, self.rstd2, self.xn2 = self.l_ps, self.lg, self.gt_ps, self.gt_sb, self.bb_ps
        self.y_ps = sem("y_ps")
        self.added = sem("added")
        self.x = sem("x")


class Loads:

    def __init__(self, sem):
        self.first = sem("first")
        self.ctx = sem("ctx")
        self.x = sem("x")
        self.attn0 = sem("attn0")
        self.attn1 = sem("attn1")
        self.l2 = sem("l2")
        self.ffn0 = sem("ffn0")
        self.ffn1 = sem("ffn1")
        self.ffn2 = sem("ffn2")
        self.ffn3 = sem("ffn3")
        self.l3 = sem("l3")
        self.ctxn = sem("ctxn")
        self.out = sem("out")
        self.scattered = sem("scattered")
        self.gathered = [sem(f"gathered{q}") for q in range(4)]


class Constants:

    def __init__(self, sem):
        self.zero = sem("zero")
        self.order = sem("order")
        self.ready = sem("ready")
        self.bias = sem("bias")
        self.cleared = sem("cleared")
        self.slots = sem("slots")


def build(nc, t, out):
    with ExitStack() as ctx:
        def sb(name, shape, dt=F32):
            return ctx.enter_context(nc.sbuf_tensor("sb_" + name, shape, dt))

        X = sb("X", [P, NB, D])
        ctxT = sb("ctxT", [DC, NB * S2])
        ident = sb("ident", [P, P])
        raw = sb("raw", [P, 10752])
        work = sb("work", [P, 5600])
        score = sb("score", [P, 2, 16 * S2])
        fold = sb("fold", [P, 16 * P + 16 * D])
        foldT = fold[0:DC, 0:16 * P]
        foldV = fold[0:DC, 16 * P:]
        ctx_b = sb("ctx_b", [DC, 2, G * S2])
        xn = sb("xn", [P, G, D])
        xnT = sb("xnT", [P, 2, G * P])
        bnst = sb("bnst", [P, 2, G, 6])
        mv = sb("mv", [P, 2, G, 2])
        ve = sb("ve", [P, 2, G])
        rstd = sb("rstd", [P, 2, G])
        mhalf = sb("mhalf", [P, NB])
        epss = sb("epss", [P, G])
        top = sb("top", [P, 16])
        tot = sb("tot", [P, 16])
        rec = sb("rec", [P, 16])
        obias = sb("obias", [P, 3, D])
        xall = sb("xall", [P, NB * P])
        hid = sb("hid", [P, 2, 4, BANK])
        w1 = sb("w1", [P, 2, 1024])
        w2 = sb("w2", [P, 2, 4, D])
        b1 = sb("b1", [P, 2, 4])
        silu = sb("silu", [P, 2, BANK])
        b2 = sb("b2", [NE, 2, D])
        gates = sb("gates", [P, NB, NE])
        gb = sb("gb", [P, 2, G * NE])
        gT = xnT[0:NE, :, :]
        wr = sb("wr", [P, 3, NE])
        rb = sb("rb", [P, NE])
        lg = sb("lg", [P, NB, NE])
        ga = sb("ga", [P, NB, NE])
        gc = sb("gc", [P, NB, NE])
        pick = sb("pick", [P, NE, 2, NB])
        pref = sb("pref", [P, NE * 2 * NB])
        first = sb("first", [P, NE * 2 * NB])
        gtop = sb("gtop", [P, 2, NB])
        gtmp = sb("gtmp", [P, NB])
        order = sb("order", [P, NE])
        upper = sb("upper", [P, P])
        ones = sb("ones", [P, P])
        l2w = sb("l2w", [P, 3, D])
        l2b = sb("l2b", [P, 2])
        qkn = sb("qkn", [P, 2, G * P])
        l3g = sb("l3g", [P, 8])
        l3w = sb("l3w", [P, 384 + 256 + 128])
        sq = sb("sq", [P, 512])
        ss = sb("ss", [P, 8])
        sr = sb("sr", [P, 8])
        sr2 = sb("sr2", [P, 8])
        mask8 = sb("mask8", [P, NB * S2], U8)

        bank = [ctx.enter_context(nc.psum_tensor(f"bank{i}", [P, BANK], F32)) for i in range(8)]

        def sems(kind, prefix):
            return kind(lambda n: ctx.enter_context(nc.semaphore(f"{prefix}_{n}")))

        stage = [sems(Stage, "even"), sems(Stage, "odd")]
        passed = ctx.enter_context(nc.semaphore("passed"))
        phase_done = ctx.enter_context(nc.semaphore("phase_done"))
        loads = sems(Loads, "load")
        const = sems(Constants, "const")

        def phase_start(eng, k):
            if k > 0:
                eng.wait_ge(phase_done, ENGINES * k)

        def clear_last_phase(pool, k):
            if k > 0:
                old = stage[(k - 1) % 2]
                pool.sem_clear(range(old.bn.num, old.x.num + 1))

        def phase_end(eng):
            eng.drain().then_inc(phase_done, 1)

        gates_flat = ga[:, :, :].rearrange("p b e -> p (b e)")
        slot_out = gates_flat[:, 0:2 * NB].bitcast(U32)
        slot_now = gates_flat[:, 2 * NB:2 * NB + 4].bitcast(U32).rearrange("p (u k) -> p u k", u=2)
        arrived = xall[:, 0:4 * D].rearrange("p (u k d) -> p u k d", u=2, k=2)
        slots_x = nc.dram_tensor("slots_x", (SPARE + 2 * NB * P, D), F32, kind="Internal").ap()
        slots_y = nc.dram_tensor("slots_y", (SPARE, D), F32, kind="Internal").ap()

        def tile(n):
            return X[:, ds(n, 1), :].rearrange("p a d -> p (a d)")


        def hold(eng, sem, value):
            eng.wait_ge(sem, value)
            eng.sem_inc(passed, 1)

        def ln_stats(dve, s, n, u, g):
            for i in range(g):
                dve.bn_stats(bnst[:, u, i, :], tile(n * g + i)).then_inc(s.bn, 1)
            hold(dve, s.bn, (n + 1) * g)
            for i in range(g):
                dve.bn_aggr(mv[:, u, i, :], bnst[:, u, i, :]).then_inc(s.mv, 1)

        def ln_rstd(pool, s, n, u, g):
            pool.wait_ge(s.mv, (n + 1) * g)
            pool.tensor_tensor(ve[:, u, 0:g], mv[:, u, 0:g, 1], epss[:, 0:g], ALU.add).then_inc(s.ve, 1)
            pool.wait_ge(s.ve, n + 1)
            pool.tensor_tensor(rstd[:, u, 0:g], ve[:, u, 0:g], mhalf[:, 0:g], ALU.pow).then_inc(s.rstd, 1)

        def ln_apply(dve, s, n, u, g, transposed):
            dve.wait_ge(s.rstd, n + 1)
            at_least(dve, transposed, n)
            for i in range(g):
                ins = dve.tensor_scalar(xn[:, i, :], tile(n * g + i), mv[:, u, i, 0:1],
                                        rstd[:, u, i:i + 1], ALU.subtract, ALU.mult)
            ins.then_inc(s.xn, 1)

        class Attention:
            def __init__(self, layer, phase, heads):
                self.layer, self.phase, self.heads = layer, phase, heads
                self.chunks = heads // 4
                self.load = (loads.attn0, loads.attn1)[layer]
                o = 0 if layer else 7168
                self.wqT = raw[0:HD, o:o + heads * D].rearrange("p (h d) -> p h d", h=heads)
                self.woh = raw[HD:P, o:o + heads * D].rearrange("p (h d) -> p h d", h=heads)
                o += heads * D
                self.wkT = raw[0:HD, o:o + heads * DC].rearrange("p (h d) -> p h d", h=heads)
                self.wvT = raw[HD:P, o:o + heads * DC].rearrange("p (h d) -> p h d", h=heads)
                self.bias = obias[:, layer, :]
                self.fold_s = stage[(0, 1)[layer]]
                self.s = stage[phase % 2]

        FOLD = ((4, 5, 6), (5, 6, 7))
        hidden = hid[:, :, :, :].rearrange("p a b c -> p (a b c)")
        key_pairs = (hidden[:, 0:2 * 16 * S2], xall[:, 1024:1024 + 2 * 16 * S2])

        def keys(a, q):
            return key_pairs[q][:, 0:2 * a.heads * S2].rearrange("p (t h j) -> p t h j", t=2, h=a.heads)

        def key_products(pe, a, first_seq, dst, h):
            for i in range(2):
                ins = pe.matmul(dst[:, 2 * i * S2:2 * (i + 1) * S2], foldT[:, (h + i) * P:(h + i + 1) * P],
                                ctxT[:, ds(first_seq * S2, 2 * S2)], start=True, stop=True)
            ins.then_inc(a.s.t_ps, 1)

        def copy_keys(act, a, q, src, h):
            nc.scalar.copy(keys(a, q)[:, :, h:h + 2, :].rearrange("p t h j -> p h t j"),
                           src[:, 0:4 * S2].rearrange("p (h t j) -> p h t j", h=2, t=2)).then_inc(a.s.t_sb, 1)

        vals = work[0:S2, 1232:3280]
        probsT = work[0:S2, 3280:5328]
        RING = (4, 5, 6)

        def ring(a, kind, c):
            return bank[RING[(kind * a.chunks + c) % 3]]

        def ring_free(pe, a, n, kind, c):
            s, k = a.s, kind * a.chunks + c - 3
            back = 0
            if k < 0:
                k, back = k + 3 * a.chunks, 1
            was, c0 = k // a.chunks, k % a.chunks
            if was == 0 and not within(n, 0, NB - 2):
                return at_least(pe, s.pt_sb, (n - 1) * a.chunks)
            done = (s.t_sb, s.v_sb, s.pt_sb)[was]
            at_least(pe, done, (n - back + (-1 if was else 2)) * a.chunks + c0 + 1)

        def attn_fold_pe(pe, a):
            s = a.fold_s
            pe.wait_ge(a.load, 16 * 4)
            pe.wait_ge(const.ready, 3)
            for j in range(2 * a.chunks):
                if j >= 3:
                    pe.wait_ge(s.fold_sb, j - 2)
                for i in range(4):
                    h = 4 * (j % a.chunks) + i
                    lhs, rhs = (a.wkT, a.wqT) if j < a.chunks else (a.wvT, a.woh)
                    ins = pe.matmul(bank[FOLD[a.layer][j % 3]][0:DC, i * D:(i + 1) * D], lhs[:, h, :], rhs[:, h, :],
                                    start=True, stop=True)
                ins.then_inc(s.fold_ps, 1)
            pe.wait_ge(s.fold_sb, 2 * a.chunks)

        def attn_fold_act(act, a):
            for j in range(2 * a.chunks):
                act.wait_ge(a.fold_s.fold_ps, j + 1)
                c = j % a.chunks
                dst = foldT if j < a.chunks else foldV
                nc.scalar.copy(dst[:, c * BANK:(c + 1) * BANK], bank[FOLD[a.layer][j % 3]][0:DC, :])\
                    .then_inc(a.fold_s.fold_sb, 1)

        def attn_pe(pe, a):
            s, C, W = a.s, a.chunks, 4 * S2
            phase_start(pe, a.phase)
            if a.layer == 0:
                attn_fold_pe(pe, a)

            pe.wait_ge(loads.ctx, 16)
            for c in range(2 * C):
                at_least(pe, s.t_sb, c - 2)
                key_products(pe, a, 0, bank[RING[c % 3]], 2 * c)
            pe.wait_ge(s.t_sb, 2 * C)

            def step(n, j):
                u, q = j % 2, j // 2
                if within(n, 0, NB):
                    pe.wait_ge(s.xn, n + 1)
                    at_least(pe, s.shift, (n - 1) * C + 1)
                    pe.transpose(bank[0][:, 384:512], xn[:, 0, :], ident[:, :]).then_inc(s.xt_ps, 1)
                if within(n, 0, NB - 2):
                    if isinstance(n, int) and n == 1:
                        pe.wait_ge(s.t_sb, 3 * C)
                    for c in range(C):
                        ring_free(pe, a, n, 0, c)
                        key_products(pe, a, n + 2 - u, ring(a, 0, c), u * a.heads // 2 + 2 * c)
                if within(n, 1, NB + 1):
                    pe.wait_ge(s.ctx, n)
                    for c in range(C):
                        ring_free(pe, a, n, 1, c)
                        pe.matmul(ring(a, 1, c)[0:S2, :], ctx_b[:, 1 - u, 0:S2], foldV[:, c * BANK:(c + 1) * BANK],
                                  start=True, stop=True).then_inc(s.v_ps, 1)
                    pe.wait_ge(s.probs, n)
                    for c in range(C):
                        ring_free(pe, a, n, 2, c)
                        for i in range(4):
                            h = 4 * c + i
                            ins = pe.transpose(ring(a, 2, c)[0:S2, i * P:(i + 1) * P],
                                               score[:, 1 - u, h * S2:(h + 1) * S2], ident[:, :])
                        ins.then_inc(s.pt_ps, 1)
                if within(n, 0, NB):
                    pe.wait_ge(s.xt_sb, n + 1)
                    pe.wait_ge(s.t_sb, (n - u + 2) * C)
                    for c in range(C):
                        at_least(pe, s.shift, (n - 1) * C + c + 1)
                        pe.matmul(bank[c][:, 0:W], xnT[:, 0, 0:P],
                                  keys(a, q)[:, u, 4 * c:4 * c + 4, :].rearrange("p h j -> p (h j)"),
                                  start=True, stop=True).then_inc(s.s_ps, 1)
                if within(n, 1, NB + 1):
                    pe.wait_ge(s.v_sb, n * C)
                    pe.wait_ge(s.pt_sb, n * C)
                    at_least(pe, s.added, n - 1)
                    for h in range(a.heads):
                        ins = pe.matmul(bank[7][:, 0:D], probsT[:, h * P:(h + 1) * P], vals[:, h * D:(h + 1) * D],
                                        start=(h == 0), stop=(h == a.heads - 1))
                    ins.then_inc(s.y_ps, 1)

            steps(pe, step, NB + 1, 4, 5, by=4)
            phase_end(pe)

        def attn_act(act, a):
            s, C, W = a.s, a.chunks, 4 * S2
            phase_start(act, a.phase)
            if a.layer == 0:
                attn_fold_act(act, a)

            for c in range(2 * C):
                act.wait_ge(s.t_ps, c + 1)
                copy_keys(act, a, 0, bank[RING[c % 3]], 2 * c)

            def step(n, j):
                u, q = j % 2, j // 2
                if within(n, 0, NB):
                    act.wait_ge(s.xt_ps, n + 1)
                    at_least(act, s.s_ps, n * C)
                    nc.scalar.copy(xnT[:, 0, 0:P], bank[0][:, 384:512]).then_inc(s.xt_sb, 1)
                if within(n, 0, NB - 2):
                    for c in range(C):
                        act.wait_ge(s.t_ps, (n + 2) * C + c + 1)
                        copy_keys(act, a, 1 - q, ring(a, 0, c), u * a.heads // 2 + 2 * c)
                if within(n, 1, NB + 1):
                    at_least(act, s.y_ps, n - 1)
                    for c in range(C):
                        act.wait_ge(s.pt_ps, (n - 1) * C + c + 1)
                        nc.scalar.copy(probsT[:, c * BANK:(c + 1) * BANK], ring(a, 2, c)[0:S2, :]).then_inc(s.pt_sb, 1)
                if within(n, 0, NB):
                    for c in range(C):
                        act.wait_ge(s.shift, n * C + c + 1)
                        e = score[:, u, c * W:(c + 1) * W]
                        nc.scalar.activation(e, e, ACT.Exp, scale=HD ** -0.5).then_inc(s.ex, 1)

            steps(act, step, NB + 1, 4, 5, by=4)
            phase_end(act)

        def attn_pool(pool, a):
            s, C, W = a.s, a.chunks, 4 * S2
            phase_start(pool, a.phase)
            clear_last_phase(pool, a.phase)

            def fetch(n, u):
                at_least(pool, s.v_ps, (n - 1) * C)
                pool.tensor_copy(ctx_b[:, u, 0:S2], ctxT[:, ds(n * S2, S2)]).then_inc(s.ctx, 1)

            def gather(m, u):
                at_least(pool, s.second_added, m - 1)
                pool.tensor_copy(slot_now[:, u, :], slot_out[:, :].rearrange("p (k b) -> p k b", k=2)[:, :, ds(m, 1)]
                                 .rearrange("p k b -> p (k b)")).then_inc(s.slots_now, 1)
                hold(pool, s.slots_now, m + 1)
                for k in range(2):
                    pool.indirect_dma_start(arrived[:, u, k, :], None, slots_y,
                                            bass.IndirectOffsetOnAxis(ap=slot_now[:, u, k:k + 1], axis=0))\
                        .then_inc(loads.gathered[u], 16)

            pool.wait_ge(loads.ctx, 16)
            if a.layer:
                gather(0, 0)
                gather(1, 1)
            fetch(0, 0)
            ln_rstd(pool, s, 0, 0, 1)
            if a.layer:
                gather(2, 0)

            def step(n, u):
                if within(n, 0, NB - 1):
                    ln_rstd(pool, s, n + 1, 1 - u, 1)
                    fetch(n + 1, 1 - u)
                if a.layer and within(n, 0, NB - 3):
                    gather(n + 3, 1 - u)

            steps(pool, step, NB + 1, 2, 5)
            phase_end(pool)

        def attn_dve(dve, a):
            s, C, H, W = a.s, a.chunks, a.heads, 4 * S2
            phase_start(dve, a.phase)
            dve.wait_ge(loads.first, 16)

            def arrive(m, u):
                if a.layer == 0:
                    return
                dve.wait_ge(loads.gathered[u], 16 * (m - u) + 32)
                for k, added in enumerate((s.first_added, s.second_added)):
                    dve.scalar_tensor_tensor(out=tile(m), in0=arrived[:, u, k, :], scalar=gtop[:, k, ds(m, 1)],
                                             in1=tile(m), op0=ALU.mult, op1=ALU.add).then_inc(added, 1)
                    hold(dve, added, m + 1)

            arrive(0, 0)
            ln_stats(dve, s, 0, 0, 1)
            ln_apply(dve, s, 0, 0, 1, s.xt_ps)

            def heads_of(ap):
                return ap.rearrange("p (h j) -> p h j", j=S2)

            def step(n, u):
                if within(n, 1, NB + 1):
                    at_least(dve, s.y_ps, n - 1)
                    for c in range(C):
                        dve.wait_ge(s.v_ps, (n - 1) * C + c + 1)
                        dve.tensor_copy(vals[:, c * BANK:(c + 1) * BANK], ring(a, 1, c)[0:S2, :]).then_inc(s.v_sb, 1)
                if a.layer == 0 and isinstance(n, int) and n == FIRST - 1:
                    dve.wait_ge(loads.x, 16)
                if within(n, 0, NB - 1):
                    arrive(n + 1, 1 - u)
                    ln_stats(dve, s, n + 1, 1 - u, 1)
                if within(n, 0, NB):
                    at_least(dve, s.pt_ps, (n - 1) * C)
                    for c in range(C):
                        dve.wait_ge(s.s_ps, n * C + c + 1)
                        dve.reduce_max(top[:, 4 * c:4 * c + 4], heads_of(bank[c][:, 0:W]), AX.X).then_inc(s.top, 1)
                        dve.wait_ge(s.top, n * C + c + 1)
                        dve.tensor_tensor(heads_of(score[:, u, c * W:(c + 1) * W]), heads_of(bank[c][:, 0:W]),
                                          top[:, 4 * c:4 * c + 4].unsqueeze(2).to_broadcast([P, 4, S2]),
                                          ALU.subtract).then_inc(s.shift, 1)
                if within(n, 0, NB - 1):
                    ln_apply(dve, s, n + 1, 1 - u, 1, s.xt_ps)
                if within(n, 0, NB):
                    for c in range(C):
                        e = heads_of(score[:, u, c * W:(c + 1) * W])
                        dve.wait_ge(s.ex, n * C + c + 1)
                        dve.reduce_sum(tot[:, 4 * c:4 * c + 4], e, AX.X).then_inc(s.tot, 1)
                    dve.wait_ge(s.tot, (n + 1) * C)
                    dve.reciprocal(rec[:, 0:H], tot[:, 0:H]).then_inc(s.rec, 1)
                    dve.wait_ge(s.rec, n + 1)
                    e = heads_of(score[:, u, 0:H * S2])
                    dve.tensor_tensor(e, e, rec[:, 0:H].unsqueeze(2).to_broadcast([P, H, S2]),
                                      ALU.mult).then_inc(s.probs, 1)
                if a.layer == 0 and isinstance(n, int) and n == 1:
                    dve.wait_ge(const.bias, 16 * 4)
                if within(n, 1, NB + 1):
                    dve.wait_ge(s.y_ps, n)
                    x = tile(n - 1)
                    dve.tensor_tensor(x, bank[7][:, 0:D], x, ALU.add).then_inc(s.added, 1)
                    dve.wait_ge(s.added, n)
                    dve.tensor_tensor(x, x, a.bias, ALU.add).then_inc(s.x, 1)

            steps(dve, step, NB + 1, 2, 3)
            phase_end(dve)

        s2 = stage[4 % 2]
        PH2 = 4
        q2, k2 = qkn[:, 0, :], work[:, 0:G * S2]
        v2, pT2 = work[0:S2, 512:1024], work[0:S2, 1024:1536]

        def attn2_pe(pe):
            s = s2
            phase_start(pe, PH2)
            pe.wait_ge(loads.l2, 16 * 5)

            def step(n, u):
                if within(n, 0, NG):
                    pe.wait_ge(s.xn, n + 1)
                    at_least(pe, s.xt_sb, n)
                    for i in range(G):
                        ins = pe.transpose(bank[0][:, i * P:(i + 1) * P], xn[:, i, :], ident[:, :])
                    ins.then_inc(s.xt_ps, 1)
                    pe.wait_ge(s.ctx, n + 1)
                    at_least(pe, s.k_sb, n)
                    pe.matmul(bank[2][:, 0:G * S2], l2w[0:DC, 1, :], ctx_b[:, u, :], start=True, stop=True)\
                      .then_inc(s.k_ps, 1)
                    pe.wait_ge(s.xt_sb, n + 1)
                    at_least(pe, s.q_sb, n)
                    pe.matmul(bank[1][:, :], l2w[:, 0, :], xnT[:, 0, :], start=True, stop=True).then_inc(s.q_ps, 1)
                if within(n, 1, NG + 1):
                    at_least(pe, s.v_sb, n - 1)
                    for i in range(G):
                        ins = pe.matmul(bank[3][0:S2, i * D:(i + 1) * D], ctx_b[:, 1 - u, i * S2:(i + 1) * S2],
                                        l2w[0:DC, 2, :], start=True, stop=True)
                    ins.then_inc(s.v_ps, 1)
                    pe.wait_ge(s.probs, n)
                    at_least(pe, s.pt_sb, n - 1)
                    for i in range(G):
                        ins = pe.transpose(bank[5][0:S2, i * P:(i + 1) * P], score[:, 1 - u, i * S2:(i + 1) * S2],
                                           ident[:, :])
                    ins.then_inc(s.pt_ps, 1)
                if within(n, 0, NG):
                    pe.wait_ge(s.q_sb, n + 1)
                    pe.wait_ge(s.k_sb, n + 1)
                    at_least(pe, s.shift, n)
                    for i in range(G):
                        ins = pe.matmul(bank[4][:, i * S2:(i + 1) * S2], q2[:, i * P:(i + 1) * P],
                                        k2[:, i * S2:(i + 1) * S2], start=True, stop=True)
                    ins.then_inc(s.s_ps, 1)
                if within(n, 1, NG + 1):
                    pe.wait_ge(s.v_sb, n)
                    pe.wait_ge(s.pt_sb, n)
                    at_least(pe, s.added, n - 1)
                    for i in range(G):
                        ins = pe.matmul(bank[6][:, i * D:(i + 1) * D], pT2[:, i * P:(i + 1) * P],
                                        v2[:, i * D:(i + 1) * D], start=True, stop=True)
                    ins.then_inc(s.y_ps, 1)

            steps(pe, step, NG + 1, 2, 3)
            phase_end(pe)

        def attn2_act(act):
            s = s2
            phase_start(act, PH2)
            act.wait_ge(loads.l2, 16 * 5)

            def step(n, u):
                if within(n, 0, NG):
                    act.wait_ge(s.xt_ps, n + 1)
                    at_least(act, s.q_ps, n)
                    nc.scalar.copy(xnT[:, 0, :], bank[0][:, :]).then_inc(s.xt_sb, 1)
                    act.wait_ge(s.k_ps, n + 1)
                    at_least(act, s.s_ps, n)
                    nc.scalar.activation(k2, bank[2][:, 0:G * S2], ACT.Identity, bias=l2b[:, 1:2]).then_inc(s.k_sb, 1)
                    act.wait_ge(s.q_ps, n + 1)
                    nc.scalar.activation(q2, bank[1][:, :], ACT.Identity, bias=l2b[:, 0:1]).then_inc(s.q_sb, 1)
                if within(n, 1, NG + 1):
                    act.wait_ge(s.v_ps, n)
                    at_least(act, s.y_ps, n - 1)
                    nc.scalar.copy(v2, bank[3][0:S2, :]).then_inc(s.v_sb, 1)
                    act.wait_ge(s.pt_ps, n)
                    nc.scalar.copy(pT2, bank[5][0:S2, :]).then_inc(s.pt_sb, 1)
                if within(n, 0, NG):
                    act.wait_ge(s.shift, n + 1)
                    e = score[:, u, 0:G * S2]
                    nc.scalar.activation(e, e, ACT.Exp, scale=D ** -0.5).then_inc(s.ex, 1)

            steps(act, step, NG + 1, 2, 3)
            phase_end(act)

        def attn2_pool(pool):
            s = s2
            phase_start(pool, PH2)
            clear_last_phase(pool, PH2)

            def fetch(n, u):
                at_least(pool, s.v_ps, n - 1)
                pool.tensor_copy(ctx_b[:, u, :], ctxT[:, ds(n * G * S2, G * S2)]).then_inc(s.ctx, 1)

            fetch(0, 0)
            ln_rstd(pool, s, 0, 0, G)

            def step(n, u):
                if within(n, 0, NG - 1):
                    ln_rstd(pool, s, n + 1, 1 - u, G)
                    fetch(n + 1, 1 - u)

            steps(pool, step, NG + 1, 2, 3)
            phase_end(pool)

        def attn2_dve(dve):
            s = s2
            phase_start(dve, PH2)
            dve.wait_ge(loads.l2, 16 * 5)
            ln_stats(dve, s, 0, 0, G)
            ln_apply(dve, s, 0, 0, G, s.xt_ps)

            def step(n, u):
                if within(n, 0, NG - 1):
                    ln_stats(dve, s, n + 1, 1 - u, G)
                e = score[:, u, 0:G * S2].rearrange("p (h j) -> p h j", j=S2)
                if within(n, 0, NG):
                    at_least(dve, s.pt_ps, n - 1)
                    sc = bank[4][:, 0:G * S2].rearrange("p (h j) -> p h j", j=S2)
                    dve.wait_ge(s.s_ps, n + 1)
                    dve.reduce_max(top[:, 0:G], sc, AX.X).then_inc(s.top, 1)
                    dve.wait_ge(s.top, n + 1)
                    dve.tensor_tensor(e, sc, top[:, 0:G].unsqueeze(2).to_broadcast([P, G, S2]),
                                      ALU.subtract).then_inc(s.shift, 1)
                if within(n, 0, NG - 1):
                    ln_apply(dve, s, n + 1, 1 - u, G, s.xt_ps)
                if within(n, 0, NG):
                    dve.wait_ge(s.ex, n + 1)
                    dve.reduce_sum(tot[:, 0:G], e, AX.X).then_inc(s.tot, 1)
                    dve.wait_ge(s.tot, n + 1)
                    dve.reciprocal(rec[:, 0:G], tot[:, 0:G]).then_inc(s.rec, 1)
                    dve.wait_ge(s.rec, n + 1)
                    dve.tensor_tensor(e, e, rec[:, 0:G].unsqueeze(2).to_broadcast([P, G, S2]),
                                      ALU.mult).then_inc(s.probs, 1)
                if within(n, 1, NG + 1):
                    dve.wait_ge(s.y_ps, n)
                    x = X[:, ds((n - 1) * G, G), :]
                    dve.tensor_tensor(x, bank[6][:, :].rearrange("p (g d) -> p g d", g=G), x, ALU.add)\
                       .then_inc(s.added, 1)
                    dve.wait_ge(s.added, n)
                    dve.tensor_tensor(x, x, obias[:, 2, :].unsqueeze(1).to_broadcast([P, G, D]), ALU.add)\
                       .then_inc(s.x, 1)

            steps(dve, step, NG + 1, 2, 3)
            phase_end(dve)

        PH3C, PH3X = 6, 7
        kc = raw[:, 0:NB * S2]
        vc = raw[0:S2, 2560:2560 + NB * D].rearrange("p (b d) -> p b d", d=D)
        ctxn = work[0:S2, 0:NB * DC].rearrange("p (b c) -> p b c", c=DC)
        maskb = raw[:, 6656:6656 + NB * S2]
        wkv, wl, wo3 = l3w[0:DC, 384:640], l3w[:, 0:384], l3w[:, 640:768]
        s3c = stage[6 % 2]
        stats_c = w2[0:S2, :, :, :].rearrange("p a c d -> p (a c d)")
        bnc = stats_c[:, 0:NB * 6].rearrange("p (b k) -> p b k", k=6)
        mvc = stats_c[:, 256:256 + NB * 2].rearrange("p (b k) -> p b k", k=2)
        vec, rsc = stats_c[:, 384:384 + NB], stats_c[:, 512:512 + NB]

        def context_stats_dve(dve, s):
            dve.wait_ge(loads.ctxn, 32)
            with dve.Fori(0, NG) as n:
                for i in range(G):
                    dve.bn_stats(bnc[:, ds(n * G + i, 1), :].rearrange("p a k -> p (a k)"),
                                 ctxn[:, ds(n * G + i, 1), :].rearrange("p a c -> p (a c)")).then_inc(s.c_bn, 1)
            dve.wait_ge(s.c_bn, NB)
            for b in range(NB):
                dve.bn_aggr(mvc[:, b, :], bnc[:, b, :]).then_inc(s.c_mv, 1)

        def context_stats_pool(pool, s):
            pool.wait_ge(s.c_mv, NB)
            pool.tensor_scalar(vec, mvc[:, :, 1], EPS, None, ALU.add).then_inc(s.c_ve, 1)
            pool.wait_ge(s.c_ve, 1)
            pool.tensor_tensor(rsc, vec, mhalf[0:S2, 0:NB], ALU.pow)

        xnc = score[0:S2, :, 0:G * DC].rearrange("p u (g c) -> p u g c", g=G)

        def kv_view(lo, hi, i):
            return bank[i][0:S2, :].rearrange("p (b c) -> p b c", b=2)[:, :, lo:hi]

        def ctx3_pe(pe):
            s = s3c
            phase_start(pe, PH3C)
            pe.wait_ge(loads.l3, 16 * 9)

            def step(n, u):
                if within(n, 0, NG):
                    pe.wait_ge(s.xn, n + 1)
                    at_least(pe, s.xt_sb, n)
                    for i in range(G):
                        ins = pe.transpose(bank[0][0:DC, i * S2:(i + 1) * S2], xnc[:, u, i, :], ident[0:S2, 0:S2])
                    ins.then_inc(s.xt_ps, 1)
                if within(n, 2, NG + 2):
                    pe.wait_ge(s.qk, n - 1)
                    pe.wait_ge(s.kt_sb, n - 1)
                    for i in range(G):
                        ins = pe.transpose(bank[5][:, i * S2:(i + 1) * S2], qkn[0:S2, u, i * P:(i + 1) * P],
                                           ident[0:S2, 0:S2])
                    ins.then_inc(s.kt_ps, 1)
                if within(n, 0, NG):
                    pe.wait_ge(s.xt_sb, n + 1)
                    at_least(pe, s.qk, n - 1)
                    at_least(pe, s.v_sb, 2 * (n - 1))
                    for i in range(G):
                        ins = pe.matmul(bank[1 + 2 * u + i // 2][0:S2, (i % 2) * 256:(i % 2) * 256 + 256],
                                        xnT[0:DC, u, i * S2:(i + 1) * S2], wkv, start=True, stop=True)
                    ins.then_inc(s.qkv_ps, 1)

            steps(pe, step, NG + 2, 2, 4)
            phase_end(pe)

        def ctx3_act(act):
            s = s3c
            phase_start(act, PH3C)
            act.wait_ge(loads.l3, 16 * 9)
            act.sem_inc(s.kt_sb, 1)

            def step(n, u):
                if within(n, 0, NG):
                    act.wait_ge(s.xt_ps, n + 1)
                    at_least(act, s.qkv_ps, n - 1)
                    nc.scalar.activation(xnT[0:DC, u, 0:G * S2], bank[0][0:DC, 0:G * S2], ACT.Identity,
                                         bias=l3g[0:DC, 1:2], scale=l3g[0:DC, 0:1]).then_inc(s.xt_sb, 1)
                if within(n, 2, NG + 2):
                    act.wait_ge(s.kt_ps, n - 1)
                    nc.scalar.copy(kc[:, ds((n - 2) * G * S2, G * S2)], bank[5][:, 0:G * S2]).then_inc(s.kt_sb, 1)
                if within(n, 0, NG):
                    act.wait_ge(s.qkv_ps, n + 1)
                    at_least(act, s.ss, n)
                    for i in range(2):
                        nc.scalar.activation(sq[0:S2, i * 256:(i + 1) * 256].rearrange("p (b c) -> p b c", b=2),
                                             kv_view(0, 128, 1 + 2 * u + i), ACT.Square).then_inc(s.sq, 1)
                    for i in range(2):
                        nc.scalar.copy(vc[:, ds(n * G + 2 * i, 2), :], kv_view(128, 256, 1 + 2 * u + i))\
                            .then_inc(s.v_sb, 1)

            steps(act, step, NG + 2, 2, 4)
            phase_end(act)

        def ctx3_pool(pool):
            s = s3c
            phase_start(pool, PH3C)
            clear_last_phase(pool, PH3C)
            for n in range(NG):
                gather2(pool, n)
                pool.wait_ge(s.sr, n + 1)
                pool.tensor_tensor(sr2[0:S2, :], sr[0:S2, :], mhalf[0:S2, 0:8], ALU.pow).then_inc(s.sr2, 1)
            phase_end(pool)

        def ctx3_dve(dve):
            s = s3c
            phase_start(dve, PH3C)
            dve.wait_ge(loads.l3, 16 * 9)
            dve.tensor_tensor(l3g[:, 5:6], l3g[:, 4:5], l3g[:, 6:7], ALU.mult)

            def apply(n, u):
                at_least(dve, s.xt_ps, n - 1)
                for i in range(G):
                    if isinstance(n, int):
                        b = n * G + i
                        mean, dev = mvc[:, b, 0:1], rsc[:, b:b + 1]
                    else:
                        b = n * G + i
                        mean, dev = mvc[:, ds(b, 1), 0], rsc[:, ds(b, 1)]
                    ins = dve.tensor_scalar(xnc[:, u, i, :], ctxn[:, ds(b, 1), :].rearrange("p a c -> p (a c)"),
                                            mean, dev, ALU.subtract, ALU.mult)
                ins.then_inc(s.xn, 1)

            apply(0, 0)

            def step(n, u):
                if within(n, 1, NG + 1):
                    dve.wait_ge(s.sr2, n)
                    dve.wait_ge(s.v_sb, 2 * n)
                    for i in range(2):
                        ins = dve.tensor_tensor(
                            qkn[0:S2, 1 - u, i * 256:(i + 1) * 256].rearrange("p (b h d) -> p b h d", b=2, h=2),
                            kv_view(0, 128, 3 - 2 * u + i).rearrange("p b (h d) -> p b h d", h=2),
                            sr2[0:S2, 4 * i:4 * i + 4].rearrange("p (b h) -> p b h", b=2).unsqueeze(3)
                            .to_broadcast([S2, 2, 2, HD]), ALU.mult)
                    ins.then_inc(s.qk, 1)
                if within(n, 0, NG - 1):
                    apply(n + 1, 1 - u)
                if within(n, 0, NG):
                    dve.wait_ge(s.sq, 2 * n + 2)
                    dve.reduce_sum(ss[0:S2, :], sq[0:S2, :].rearrange("p (h d) -> p h d", d=HD), AX.X)\
                       .then_inc(s.ss, 1)
                    dve.wait_ge(s.ss, n + 1)
                    dve.tensor_scalar(sr[0:S2, :], ss[0:S2, :], 1.0 / HD, RMS_EPS ** 2, ALU.mult, ALU.max)\
                       .then_inc(s.sr, 1)

            steps(dve, step, NG + 2, 2, 4)
            dve.tensor_scalar(maskb, mask8[:, :], -1.0, FLT_MAX, ALU.add, ALU.mult)
            back2_dve(dve)
            phase_end(dve)

        s3 = stage[7 % 2]
        g3, N3 = 2, NB // 2
        KL = S2 + P
        qT3 = [hid[:, h, 3, 0:2 * P] for h in range(2)]
        k3 = hid[:, :, 2, 0:2 * KL].rearrange("p u (t j) -> p u t j", t=2)
        pT3 = xall[:, 512:1536]
        oT3 = xall[:, 1536:1536 + 2 * P]
        sc3 = xall[:, 2048:2048 + 2 * 2 * 2 * KL].rearrange("p (u t h j) -> p u t h j", u=2, t=2, h=2)

        def v3(j, i):
            return hid[:, j // 2, j % 2, i * P:(i + 1) * P]


        def sbank(h):
            return bank[4 + h][:, 0:2 * KL].rearrange("p (t j) -> p t j", t=2)

        def attn3_pe(pe):
            s = s3
            phase_start(pe, PH3X)
            pe.wait_ge(s.zeroed, 2)

            def step(n, q):
                u = q % 2
                if within(n, 1, N3 + 1):
                    pe.wait_ge(s.qk, n)
                    at_least(pe, s.kt_sb, n - 1)
                    for i in range(g3):
                        for j in range(2):
                            ins = pe.transpose(bank[3][:, (2 * j + i) * P:(2 * j + i + 1) * P],
                                               qkn[:, 1 - u, (2 * i + j) * P:(2 * i + j + 1) * P], ident[:, :])
                    ins.then_inc(s.qkt_ps, 1)
                if within(n, 0, N3):
                    pe.wait_ge(s.xn, n + 1)
                    at_least(pe, s.xt_sb, n)
                    for i in range(g3):
                        ins = pe.transpose(bank[0][:, i * P:(i + 1) * P], xn[:, i, :], ident[:, :])
                    ins.then_inc(s.xt_ps, 1)
                if within(n, 3, N3 + 3):
                    pe.wait_ge(s.o_sb, n - 2)
                    for i in range(g3):
                        ins = pe.matmul(bank[7][:, i * P:(i + 1) * P], oT3[:, i * P:(i + 1) * P], wo3,
                                        start=True, stop=True)
                    ins.then_inc(s.y_ps, 1)
                if within(n, 1, N3 + 1):
                    pe.wait_ge(s.kt_sb, n)
                    pe.wait_ge(s.ctx, n)
                    at_least(pe, s.shift, n - 1)
                    for i in range(g3):
                        for h in range(2):
                            ins = pe.matmul(bank[4 + h][:, i * KL:(i + 1) * KL], qT3[h][:, i * P:(i + 1) * P],
                                            k3[:, 1 - u, i, :], start=True, stop=True)
                    ins.then_inc(s.s_ps, 1)
                if within(n, 0, N3):
                    pe.wait_ge(s.xt_sb, n + 1)
                    at_least(pe, s.qk, n)
                    at_least(pe, s.v_sb, n)
                    for i in range(g3):
                        ins = pe.matmul(bank[1 + i][:, 0:384], xnT[:, u, i * P:(i + 1) * P], wl, start=True, stop=True)
                    ins.then_inc(s.qkv_ps, 1)
                if within(n, 2, N3 + 2):
                    pe.wait_ge(s.probs, n - 1)
                    for i in range(g3):
                        at_least(pe, s.pt_sb, 2 * (n - 2) + i)
                        for h in range(2):
                            pr = sc3[:, u, i, h, :]
                            pe.transpose(bank[6][0:S2, h * P:(h + 1) * P], pr[:, 0:S2], ident[:, :])
                            ins = pe.transpose(bank[6][:, (2 + h) * P:(3 + h) * P], pr[:, S2:KL], ident[:, :])
                        ins.then_inc(s.pt_ps, 1)
                    pe.wait_ge(s.xall, n - 1)
                    at_least(pe, s.added, n - 2)
                    for i in range(g3):
                        pe.wait_ge(s.pt_sb, 2 * (n - 2) + i + 1)
                        for h in range(2):
                            o = bank[7][h * HD:(h + 1) * HD, i * P:(i + 1) * P]
                            hv = slice(h * HD, (h + 1) * HD)
                            pe.matmul(o, vcs[:, u, i, hv], pT3[0:S2, (4 * i + h) * P:(4 * i + h + 1) * P],
                                      start=True, stop=False)
                            ins = pe.matmul(o, v3((q + 2) % 4, i)[:, hv], pT3[:, (4 * i + 2 + h) * P:(4 * i + 3 + h) * P],
                                            start=False, stop=True)
                    ins.then_inc(s.o_ps, 1)

            steps(pe, step, N3 + 3, 4, 7, by=4)
            phase_end(pe)

        vcs = sb("vcs", [S2, 2, g3, D])

        def attn3_act(act):
            s = s3
            phase_start(act, PH3X)

            def step(n, q):
                u = q % 2
                if within(n, 1, N3 + 1):
                    act.wait_ge(s.qkt_ps, n)
                    at_least(act, s.s_ps, n - 1)
                    for h in range(2):
                        hp = slice(h * HD, (h + 1) * HD)
                        nc.scalar.activation(qT3[h][hp, :], bank[3][hp, 0:2 * P], ACT.Copy, scale=l3g[hp, 5:6])
                    nc.scalar.copy(k3[:, 1 - u, :, S2:KL], bank[3][:, 2 * P:4 * P].rearrange("p (t j) -> p t j", t=2))\
                        .then_inc(s.kt_sb, 1)
                if within(n, 0, N3):
                    act.wait_ge(s.xt_ps, n + 1)
                    at_least(act, s.qkv_ps, n - 1)
                    nc.scalar.activation(xnT[:, u, 0:2 * P], bank[0][:, 0:256], ACT.Identity,
                                         bias=l3g[:, 3:4], scale=l3g[:, 2:3]).then_inc(s.xt_sb, 1)
                    act.wait_ge(s.qkv_ps, n + 1)
                    at_least(act, s.ss, n)
                    for i in range(g3):
                        ins = nc.scalar.activation(sq[:, i * 256:(i + 1) * 256], bank[1 + i][:, 0:256], ACT.Square)
                    ins.then_inc(s.sq, 1)
                    at_least(act, s.o_ps, n - 3)
                    for i in range(g3):
                        ins = nc.scalar.copy(v3(q, i), bank[1 + i][:, 256:384])
                    ins.then_inc(s.v_sb, 1)
                if within(n, 2, N3 + 2):
                    at_least(act, s.o_ps, n - 2)
                    for i in range(g3):
                        act.wait_ge(s.pt_ps, 2 * (n - 2) + i + 1)
                        nc.scalar.copy(pT3[0:S2, 4 * i * P:(4 * i + 2) * P], bank[6][0:S2, 0:2 * P])
                        nc.scalar.copy(pT3[:, (4 * i + 2) * P:(4 * i + 4) * P], bank[6][:, 2 * P:4 * P])\
                            .then_inc(s.pt_sb, 1)
                if within(n, 1, N3 + 1):
                    act.wait_ge(s.shift, n)
                    e = sc3[:, 1 - u, :, :, :].rearrange("p t h j -> p (t h j)")
                    nc.scalar.activation(e, e, ACT.Exp, scale=HD ** -0.5).then_inc(s.ex, 1)
                if within(n, 2, N3 + 2):
                    act.wait_ge(s.o_ps, n - 1)
                    at_least(act, s.y_ps, n - 2)
                    nc.scalar.copy(oT3, bank[7][:, 0:2 * P]).then_inc(s.o_sb, 1)

            steps(act, step, N3 + 2, 4, 6, by=4)
            phase_end(act)

        def attn3_pool(pool):
            s = s3
            phase_start(pool, PH3X)
            clear_last_phase(pool, PH3X)

            def rstds(n, u):
                pool.wait_ge(s.ve, n + 1)
                pool.tensor_tensor(rstd[:, u, 0:g3], ve[:, u, 0:g3], mhalf[:, 0:g3], ALU.pow).then_inc(s.rstd, 1)

            for h in range(2):
                other = slice((1 - h) * HD, (2 - h) * HD)
                pool.memset(qT3[h][other, :], 0.0).then_inc(s.zeroed, 1)
                pool.wait_ge(s.zeroed, h + 1)
            rstds(0, 0)

            def step(n, u):
                if within(n, 0, N3):
                    pool.wait_ge(s.sr, n + 1)
                    pool.tensor_tensor(sr2[:, :], sr[:, :], mhalf[:, 0:8], ALU.pow).then_inc(s.sr2, 1)
                if within(n, 0, N3 - 1):
                    rstds(n + 1, 1 - u)
                if within(n, 0, N3):
                    at_least(pool, s.s_ps, n - 1)
                    pool.tensor_copy(k3[:, u, :, 0:S2], kc[:, ds(n * g3 * S2, g3 * S2)]
                                     .rearrange("p (t j) -> p t j", t=2)).then_inc(s.ctx, 1)
                if within(n, 1, N3 + 1):
                    at_least(pool, s.o_ps, n - 2)
                    pool.tensor_copy(vcs[:, 1 - u, :, :], vc[:, ds((n - 1) * g3, g3), :]).then_inc(s.xall, 1)

            steps(pool, step, N3 + 1, 4, 3)
            phase_end(pool)

        def attn3_dve(dve):
            s = s3
            phase_start(dve, PH3X)

            def stats(n, u):
                ln_stats(dve, s, n, u, g3)
                dve.wait_ge(s.mv, (n + 1) * g3)
                dve.tensor_scalar(ve[:, u, 0:g3], mv[:, u, 0:g3, 1], 1.0 + EPS, EPS * EPS, ALU.mult, ALU.add)\
                   .then_inc(s.ve, 1)

            stats(0, 0)
            ln_apply(dve, s, 0, 0, g3, s.xt_ps)

            def step(n, u):
                if within(n, 3, N3 + 3):
                    dve.wait_ge(s.y_ps, n - 2)
                    x = X[:, ds((n - 3) * g3, g3), :]
                    dve.tensor_tensor(x, bank[7][:, 0:256].rearrange("p (t d) -> p t d", t=2), x, ALU.add)\
                       .then_inc(s.added, 1)
                    dve.wait_ge(s.added, n - 2)
                    dve.tensor_tensor(x, x, l3bo[:, :].unsqueeze(1).to_broadcast([P, g3, D]), ALU.add)\
                       .then_inc(s.x, 1)
                if within(n, 1, N3 + 1):
                    mb = maskb[:, ds((n - 1) * g3 * S2, g3 * S2)].rearrange("p (t j) -> p t j", t=2)
                    e = sc3[:, 1 - u, :, :, :]
                    dve.wait_ge(s.s_ps, n)
                    at_least(dve, s.pt_ps, 2 * (n - 2))
                    ctop, ltop, mx = (top[:, 4 * k:4 * k + 4].rearrange("p (t h) -> p t h", t=2) for k in range(3))
                    for h in range(2):
                        dve.tensor_tensor(e[:, :, h, 0:S2], sbank(h)[:, :, 0:S2], mb, ALU.add).then_inc(s.m2, 1)
                        dve.reduce_max(ltop[:, :, h], sbank(h)[:, :, S2:KL], AX.X).then_inc(s.m3, 1)
                    dve.wait_ge(s.m2, n * 2)
                    dve.reduce_max(ctop, e[:, :, :, 0:S2], AX.X).then_inc(s.m3, 1)
                    dve.wait_ge(s.m3, n * 3)
                    dve.tensor_tensor(mx, ctop, ltop, ALU.max).then_inc(s.m4, 1)
                    dve.wait_ge(s.m4, n)
                    dve.tensor_tensor(e[:, :, :, 0:S2], e[:, :, :, 0:S2],
                                      mx.unsqueeze(3).to_broadcast([P, 2, 2, S2]), ALU.subtract)
                    for h in range(2):
                        ins = dve.tensor_tensor(e[:, :, h, S2:KL], sbank(h)[:, :, S2:KL],
                                                mx[:, :, h].unsqueeze(2).to_broadcast([P, 2, P]), ALU.subtract)
                    ins.then_inc(s.shift, 1)
                if within(n, 0, N3):
                    dve.wait_ge(s.sq, n + 1)
                    dve.reduce_sum(ss[:, :], sq[:, :].rearrange("p (h d) -> p h d", d=HD), AX.X).then_inc(s.ss, 1)
                    dve.wait_ge(s.ss, n + 1)
                    dve.tensor_scalar(sr[:, :], ss[:, :], 1.0 / HD, RMS_EPS ** 2, ALU.mult, ALU.max).then_inc(s.sr, 1)
                if within(n, 0, N3 - 1):
                    stats(n + 1, 1 - u)
                if within(n, 0, N3):
                    dve.wait_ge(s.sr2, n + 1)
                    dve.wait_ge(s.v_sb, n + 1)
                    at_least(dve, s.qkt_ps, n - 1)
                    for i in range(g3):
                        ins = dve.tensor_tensor(
                            qkn[:, u, i * 256:(i + 1) * 256].rearrange("p (h d) -> p h d", d=HD),
                            bank[1 + i][:, 0:256].rearrange("p (h d) -> p h d", d=HD),
                            sr2[:, 4 * i:4 * i + 4].unsqueeze(2).to_broadcast([P, 4, HD]), ALU.mult)
                    ins.then_inc(s.qk, 1)
                if within(n, 0, N3 - 1):
                    ln_apply(dve, s, n + 1, 1 - u, g3, s.xt_ps)
                if within(n, 1, N3 + 1):
                    dve.wait_ge(s.ex, n)
                    et = e.rearrange("p t h j -> p (t h) j")
                    dve.reduce_sum(tot[:, 0:4], et, AX.X).then_inc(s.tot, 1)
                    dve.wait_ge(s.tot, n)
                    dve.reciprocal(rec[:, 0:4], tot[:, 0:4]).then_inc(s.rec, 1)
                    dve.wait_ge(s.rec, n)
                    dve.tensor_tensor(et, et, rec[:, 0:4].unsqueeze(2).to_broadcast([P, 4, KL]),
                                      ALU.mult).then_inc(s.probs, 1)

            steps(dve, step, N3 + 3, 4, 5)
            phase_end(dve)

        l3bo = sb("l3bo", [P, D])

        class Ffn:
            def __init__(self, layer, phase, experts, chunks, func, gated, ranks, router, biased):
                self.layer, self.phase, self.experts, self.chunks = layer, phase, experts, chunks
                self.func, self.gated, self.ranks, self.router, self.biased = func, gated, ranks, router, biased
                self.slots = {(4, False): 4, (1, False): 2, (4, True): 2, (3, True): 3}[chunks, gated]
                self.load = (loads.ffn0, loads.ffn1, loads.ffn2, loads.ffn3)[layer]
                self.s = stage[phase % 2]
                self.sorted = layer in (0, 2)
                self.scatters = {0: 2 * NB, 2: 3 * NB}.get(layer)
                self.loads = {0: 3, 1: 2, 2: 4, 3: 2}[layer]

        xn2 = qkn[:, :, :].rearrange("p u (g d) -> p u g d", g=G)

        def front_pe(pe, f):
            s = f.s

            def turn(n, u):
                pe.wait_ge(s.xn, n + 1)
                at_least(pe, s.xt_sb, n - 1)
                for i in range(G):
                    ins = pe.transpose(bank[7 * u][:, i * P:(i + 1) * P], xn2[:, u, i, :], ident[:, :])
                ins.then_inc(s.xt_ps, 1)

            turn(0, 0)

            def front(n, u):
                if within(n, 0, NG - 1):
                    turn(n + 1, 1 - u)
                if f.ranks:
                    pe.wait_ge(s.xt_sb, n + 1)
                    at_least(pe, s.lg, n - 1)
                    for i in range(G):
                        ins = pe.matmul(bank[1 + u][:, i * NE:(i + 1) * NE], xnT[:, u, i * P:(i + 1) * P],
                                        wr[:, f.layer, :], start=True, stop=True)
                    ins.then_inc(s.l_ps, 1)

            steps(pe, front, NG, 2, 2)

        def front_act(act, f):
            s = f.s

            def front(n, u):
                act.wait_ge(s.xt_ps, n + 1)
                if not f.sorted:
                    nc.scalar.copy(xall[:, ds(n * G * P, G * P)], bank[7 * u][:, :]).then_inc(s.xall, 1)
                if f.ranks:
                    at_least(act, s.l_ps, n - 1)
                nc.scalar.copy(xnT[:, u, :], bank[7 * u][:, :]).then_inc(s.xt_sb, 1)
                if f.sorted:
                    act.wait_ge(s.xn, n + 1)
                    nc.scalar.copy(tokens[:, ds(n * G, G), :], xn2[:, u, :, :]).then_inc(s.xall, 1)

            steps(act, front, NG, 2, 2)
            if f.ranks:
                act.wait_ge(s.gate_step, 2)
                nc.scalar.activation(ga[:, :, :], gc[:, :, :], ACT.Exp).then_inc(s.ex, 1)

        def front_pool(pool, f):
            steps(pool, lambda n, u: ln_rstd(pool, f.s, n, u, G), NG, 2, 2)

        def front_dve(dve, f):
            s = f.s

            def apply(n, u):
                dve.wait_ge(s.rstd, n + 1)
                at_least(dve, s.xt_ps, n - 1)
                if f.sorted:
                    at_least(dve, s.xall, n - 1)
                for i in range(G):
                    ins = dve.tensor_scalar(xn2[:, u, i, :], tile(n * G + i), mv[:, u, i, 0:1],
                                            rstd[:, u, i:i + 1], ALU.subtract, ALU.mult)
                ins.then_inc(s.xn, 1)

            ln_stats(dve, s, 0, 0, G)
            ln_stats(dve, s, 1, 1, G)
            apply(0, 0)

            def front(n, u):
                if within(n, 0, NG - 2):
                    ln_stats(dve, s, n + 2, u, G)
                if within(n, 0, NG - 1):
                    apply(n + 1, 1 - u)
                if f.ranks and within(n, 1, NG + 1):
                    dve.wait_ge(s.l_ps, n)
                    dst = lg[:, ds((n - 1) * G, G), :]
                    src = bank[2 - u][:, 0:G * NE].rearrange("p (g e) -> p g e", g=G)
                    if f.layer == 2:
                        dve.tensor_tensor(dst, src, rb[:, :].unsqueeze(1).to_broadcast([P, G, NE]), ALU.add)\
                           .then_inc(s.lg, 1)
                    else:
                        dve.tensor_copy(dst, src).then_inc(s.lg, 1)

            steps(dve, front, NG + 1, 2, 3)

        def chunk_at(f, g, c):
            return (g * f.chunks + c) % f.slots

        def up_bank(f, slot, half=0):
            return bank[2 * slot + half] if f.gated else bank[slot]

        def over_experts(eng, f, body):
            if f.experts == 1:
                body(0, 0, 0)
                return
            with eng.Fori(0, f.experts // 2) as i:
                for p in (0, 1):
                    body(i * 2 + p, p, i)

        def ffn_sp(sp, f, w1_of, w2_of, b1_of):
            s = f.s
            phase_start(sp, f.phase)

            def load(e, p, wait):
                if wait is not None:
                    sp.wait_ge(s.y_ps, wait)
                n = f.chunks * P * (2 if f.gated else 1)
                sp.dma_start(w1[:, p, 0:n], w1_of(e)).then_inc((s.w0, s.w1)[p], 16)
                sp.dma_start(w2[:, p, 0:f.chunks, :], w2_of(e)).then_inc((s.w0, s.w1)[p], 16)
                sp.dma_start(b1[:, p, 0:f.chunks], b1_of(e)).then_inc((s.w0, s.w1)[p], 16)

            load(0, 0, None)
            load(1, 1, None)
            with sp.Fori(1, f.experts // 2) as i:
                for p in (0, 1):
                    load(i * 2 + p, p, (i * 2 + p - 1) * NG + 2)

        def ffn_pe(pe, f):
            s, C, R = f.s, f.chunks, f.slots
            phase_start(pe, f.phase)
            pe.wait_ge(f.load, 16 * 2)

            front_pe(pe, f)
            if f.biased:
                def bias(n, u):
                    if within(n, 0, NG):
                        pe.wait_ge(s.gb, n + 1)
                        at_least(pe, s.gt_sb, n)
                        for i in range(G):
                            ins = pe.transpose(bank[5][0:NE, i * P:(i + 1) * P], gb[:, u, i * NE:(i + 1) * NE],
                                               ident[:, :])
                        ins.then_inc(s.gt_ps, 1)
                    if within(n, 1, NG + 1):
                        pe.wait_ge(s.gt_sb, n)
                        at_least(pe, s.bb, n - 1)
                        for i in range(G):
                            ins = pe.matmul(bank[6 - 3 * u][:, i * D:(i + 1) * D], gT[:, 1 - u, i * P:(i + 1) * P],
                                            b2[:, f.layer, :], start=True, stop=True)
                        ins.then_inc(s.bb_ps, 1)

                steps(pe, bias, NG + 1, 2, 3)
            if f.biased:
                pe.wait_ge(s.bb, NG)
            elif f.ranks:
                pe.wait_ge(s.lg, NG)
            pe.wait_ge(s.xall, NG)
            pe.sem_inc(s.y_ps, 2)

            def expert(e, p, i):
                if f.experts == 1:
                    pe.wait_ge(s.w0, 1)
                else:
                    pe.wait_ge((s.w0, s.w1)[p], i * 48 + 48)

                def step(g, u):
                    it = e * NG + g
                    if within(g, 0, NG):
                        for c in range(C):
                            slot = chunk_at(f, u, c)
                            pe.wait_ge(s.h, it * C + c + 1)
                            for half in range(2 if f.gated else 1):
                                o = (half * C + c) * P
                                ins = pe.matmul(up_bank(f, slot, half)[:, :], w1[:, p, o:o + P],
                                                xall[:, ds(g * G * P, G * P)], start=True, stop=True)
                            ins.then_inc(s.up_ps, 1)
                    if within(g, 1, NG + 1):
                        pe.wait_ge(s.h, it * C + R)
                        pe.wait_ge(s.x, it)
                        for i in range(G):
                            for c in range(C):
                                ins = pe.matmul(bank[6 + (1 - u)][:, i * D:(i + 1) * D],
                                                hid[:, 1 - u, c, i * P:(i + 1) * P], w2[:, p, c, :],
                                                start=(c == 0), stop=(c == C - 1))
                        ins.then_inc(s.y_ps, 1)

                steps(pe, step, NG + 1, 2, 1)

            over_experts(pe, f, expert)
            phase_end(pe)

        def ffn_act(act, f):
            s, C, R = f.s, f.chunks, f.slots
            phase_start(act, f.phase)

            front_act(act, f)
            if f.biased:
                def bias(n, u):
                    act.wait_ge(s.gt_ps, n + 1)
                    at_least(act, s.bb_ps, n - 1)
                    nc.scalar.copy(gT[:, u, :], bank[5][0:NE, :]).then_inc(s.gt_sb, 1)

                steps(act, bias, NG, 2, 2)
            if not f.gated:
                act.sem_inc(s.h, R)

            def expert(e, p, i):
                if f.experts > 1:
                    act.wait_ge((s.w0, s.w1)[p], i * 48 + 48)

                def step(g, u):
                    it = e * NG + g
                    act.wait_ge(s.y_ps, it + 1)
                    for c in range(C):
                        src = up_bank(f, chunk_at(f, u, c))[:, :]
                        act.wait_ge(s.up_ps, it * C + c + 1)
                        if f.gated:
                            act.wait_ge(s.h, it * C + c - 1 + R)
                            nc.scalar.activation(silu[:, c % 2 if C % 2 == 0 else (u + c) % 2, :], src,
                                                 ACT.Silu).then_inc(s.act, 1)
                        elif f.biased:
                            nc.scalar.activation(hid[:, u, c, :], src, f.func, bias=b1[:, p, c:c + 1])\
                                .then_inc(s.h, 1)

                steps(act, step, NG, 2, 2)

            over_experts(act, f, expert)
            phase_end(act)

        def ffn_pool(pool, f):
            s = f.s
            phase_start(pool, f.phase)
            clear_last_phase(pool, f.phase)
            front_pool(pool, f)
            phase_end(pool)

        def softmax_and_choice(dve, f):
            s = f.s
            done = [0]

            def link(ins):
                done[0] += 1
                ins.then_inc(s.gate_step, 1)
                dve.wait_ge(s.gate_step, done[0])

            def per_expert(ap):
                return ap.unsqueeze(2).to_broadcast([P, NB, NE])

            if f.layer == 2:
                dve.memset(pick[:, :, 1, :], 0.0).then_inc(s.zeroed, 1)
            src = lg[:, :, :]
            dve.wait_ge(s.lg, NG)
            link(dve.reduce_max(gtmp[:, :], src, AX.X))
            link(dve.tensor_tensor(gc[:, :, :], src, per_expert(gtmp[:, :]), ALU.subtract))
            dve.wait_ge(s.ex, 1)
            link(dve.reduce_sum(gtmp[:, :], ga[:, :, :], AX.X))
            link(dve.reciprocal(gtmp[:, :], gtmp[:, :]))
            link(dve.tensor_tensor(ga[:, :, :], ga[:, :, :], per_expert(gtmp[:, :]), ALU.mult))
            for r in range(f.ranks):
                link(dve.reduce_max(gtop[:, r, :], ga[:, :, :], AX.X))
                link(dve.tensor_tensor(gc[:, :, :], ga[:, :, :], per_expert(gtop[:, r, :]), ALU.is_equal))
                link(dve.tensor_tensor(gc[:, :, :], gc[:, :, :],
                                       order[:, :].unsqueeze(1).to_broadcast([P, NB, NE]), ALU.mult))
                link(dve.reduce_max(gtmp[:, :], gc[:, :, :], AX.X))
                chosen = pick[:, :, r, :].rearrange("p e b -> p b e")
                link(dve.tensor_tensor(chosen, gc[:, :, :], per_expert(gtmp[:, :]), ALU.is_equal))
                if r + 1 < f.ranks:
                    link(dve.scalar_tensor_tensor(out=ga[:, :, :], in0=chosen, scalar=-2.0, in1=ga[:, :, :],
                                                  op0=ALU.mult, op1=ALU.add))
            if f.sorted:
                assert done[0] == CHOSEN[f.ranks]
                return link, done
            out_view = gates[:, :, :]
            for r in range(f.ranks):
                link(dve.tensor_tensor(pick[:, :, r, :], pick[:, :, r, :],
                                       gtop[:, r, :].unsqueeze(1).to_broadcast([P, NE, NB]), ALU.mult))
            if f.ranks == 2:
                link(dve.tensor_tensor(out_view, pick[:, :, 0, :].rearrange("p e b -> p b e"),
                                       pick[:, :, 1, :].rearrange("p e b -> p b e"), ALU.add))
            else:
                link(dve.tensor_copy(out_view, pick[:, :, 0, :].rearrange("p e b -> p b e")))

        gate_of = gates[:, :, :].rearrange("p b e -> p (b e)")

        CHOSEN = {1: 10, 2: 16}


        sort_ = work[:, 4928:5600]
        tile_start = sort_[:, 0:NT]
        spare = sort_[:, 40:40 + 2 * NB]
        cap_start = sort_[:, 104:104 + NE]
        tiles_of = sort_[:, 112:112 + NE]
        base = sort_[:, 120:120 + NE]
        slot_f = sort_[:, 128:192]
        keep = sort_[:, 192:256]
        slot_in = sort_[:, 320:384].bitcast(U32)
        expert_f = sort_[:, 384:384 + NT]
        expert_of = sort_[:, 424:424 + NT].bitcast(I32)
        iota_i = sort_[:, 464:464 + 112].bitcast(I32)
        slot_g = sort_[:, 576:640]
        flat = pick[:, :, :, :].rearrange("p e k b -> p (e k b)")
        w1all = raw[:, 0:NE * 1024]
        b2all = work[:, 0:NE * D]
        xin = score[:, :, 0:BANK]
        yout = silu
        second = hid[:, :, :, :].rearrange("p a b c -> p (a b c)")
        tokens = xall[:, :].rearrange("p (b d) -> p b d", d=D)

        def sorted_front_pe(pe, f):
            s = f.s
            phase_start(pe, f.phase)
            pe.wait_ge(f.load, 16 * f.loads)

            front_pe(pe, f)
            pe.wait_ge(s.gate_step, CHOSEN[f.ranks])
            if f.ranks == 1:
                pe.wait_ge(s.zeroed, 1)
            pe.wait_ge(const.ready, 3)
            pe.matmul(bank[3][:, :], upper[:, :], flat, start=True, stop=True)
            pe.matmul(bank[4][:, :], ones[:, :], flat, start=True, stop=True).then_inc(s.cnt_ps, 1)

        def sorted_front_act(act, f):
            s = f.s
            phase_start(act, f.phase)
            front_act(act, f)

        def sorted_front_pool(pool, f):
            s = f.s
            phase_start(pool, f.phase)
            clear_last_phase(pool, f.phase)
            front_pool(pool, f)
            pool.iota(iota_i[:, 0:NT], [[P, NT]], base=0, channel_multiplier=0).then_inc(s.counts, 1)
            if f.layer == 0:
                pool.iota(iota_i[:, 40:104], [[P, 2 * NB]], base=SPARE, channel_multiplier=1).then_inc(s.counts, 1)
                pool.iota(iota_i[:, 104:112], [[CAP, NE]], base=0, channel_multiplier=0).then_inc(s.counts, 1)
            pool.wait_ge(s.gate_step, SLOTTED[f.layer])
            pool.wait_ge(s.xall, NG)
            pool.wait_ge(const.slots, 16 * FILLS)
            for k in range(f.ranks):
                for b in range(NB):
                    c = k * NB + b
                    pool.indirect_dma_start(slots_x, bass.IndirectOffsetOnAxis(ap=slot_in[:, c:c + 1], axis=0),
                                            tokens[:, b, :], None).then_inc(loads.scattered, 16)

        def all_stored(pool, f, out0, out1):
            s = f.s
            pool.wait_ge(loads.scattered, 16 * f.scatters)
            pool.wait_ge(s.out0, 16 * out0)
            pool.wait_ge(s.out1, 16 * out1)

        def gather2(pool, g):
            for b in range(g * G, (g + 1) * G):
                pool.indirect_dma_start(tokens[:, b, :], None, slots_y,
                                        bass.IndirectOffsetOnAxis(ap=slot_out[:, b:b + 1], axis=0))\
                    .then_inc(loads.gathered[b // 8], 16)

        def sorted_front_dve(dve, f):
            s = f.s
            phase_start(dve, f.phase)
            dve.wait_ge(f.load, 16 * f.loads)

            front_dve(dve, f)
            link, done = softmax_and_choice(dve, f)
            per_e = pref[:, :].rearrange("p (e n) -> p e n", e=NE)

            def places():
                dve.wait_ge(s.cnt_ps, 1)
                link(dve.tensor_tensor_scan(pref[:, :], first[:, :], bank[4][:, :], 0.0, ALU.mult, ALU.add))
                if f.layer == 2:
                    dve.wait_ge(s.counts, 1)
                    link(dve.tensor_copy(tile_start, iota_i[:, 0:NT]))
                    cmp = lg[:, :, :].rearrange("p b e -> p (b e)")
                    link(dve.tensor_copy(slot_g[:, 0:NE], per_e[:, :, 2 * NB - 1]))
                    c3 = compare.rearrange("p (e t) -> p e t", e=NE)
                    link(dve.tensor_tensor(c3, slot_g[:, 0:NE].unsqueeze(2).to_broadcast([P, NE, NT]),
                                           tile_start.unsqueeze(1).to_broadcast([P, NE, NT]), ALU.is_gt))
                    link(dve.reduce_sum(base, c3, AX.X))
                    link(dve.tensor_scalar(base, base, float(P), None, ALU.mult))
                    link(dve.tensor_tensor_scan(tiles_of, ones[:, 0:NE], base, 0.0, ALU.mult, ALU.add))
                    link(dve.tensor_tensor(base, tiles_of, base, ALU.subtract))
                    c3 = compare.rearrange("p (t e) -> p t e", e=NE)
                    link(dve.tensor_tensor(c3, tile_start.unsqueeze(2).to_broadcast([P, NT, NE]),
                                           tiles_of.unsqueeze(1).to_broadcast([P, NT, NE]), ALU.is_ge))
                    link(dve.reduce_sum(expert_f, c3, AX.X))
                    link(dve.tensor_scalar(expert_f, expert_f, float(NE - 1), None, ALU.min))
                    link(dve.tensor_copy(expert_of, expert_f))
                else:
                    dve.wait_ge(s.counts, 3)
                    link(dve.tensor_copy(spare, iota_i[:, 40:104]))
                    link(dve.tensor_copy(base, iota_i[:, 104:112]))
                link(dve.tensor_tensor(pref[:, :], pref[:, :], bank[4][:, :], ALU.subtract))
                link(dve.tensor_tensor(pref[:, :], pref[:, :], bank[3][:, :], ALU.add))

            by_choice = flat.rearrange("p (e n) -> p n e", e=NE)
            places()
            if f.layer == 0:
                link(dve.tensor_tensor(gtmp[:, :], gtop[:, 0, :], gtop[:, 1, :], ALU.add))
                link(dve.reciprocal(gtmp[:, :], gtmp[:, :]))
                link(dve.tensor_tensor(gtop[:, :, :], gtop[:, :, :],
                                       gtmp[:, :].unsqueeze(1).to_broadcast([P, 2, NB]), ALU.mult))
                kept = lg[:, :, :].rearrange("p b e -> p (b e)")
                link(dve.tensor_tensor(slot_all, pref[:, :], flat, ALU.mult))
                link(dve.reduce_sum(slot_f, slot_all.rearrange("p (e n) -> p n e", e=NE), AX.X))
                link(dve.tensor_scalar(keep, slot_f, float(CAP), None, ALU.is_le))
                link(dve.tensor_tensor(gtop[:, :, :].rearrange("p k b -> p (k b)"),
                                       gtop[:, :, :].rearrange("p k b -> p (k b)"), keep, ALU.mult))
            link(dve.tensor_tensor(per_e, per_e, base.unsqueeze(2).to_broadcast([P, NE, 2 * NB]), ALU.add))
            link(dve.tensor_tensor(flat, flat, pref[:, :], ALU.mult))
            link(dve.reduce_sum(slot_f, by_choice, AX.X))
            link(dve.tensor_scalar(slot_f, slot_f, 1.0, None, ALU.subtract))
            if f.layer == 0:
                link(dve.tensor_tensor(slot_f, slot_f, keep, ALU.mult))
                link(dve.tensor_tensor(slot_g, spare, keep, ALU.mult))
                link(dve.tensor_tensor(slot_g, spare, slot_g, ALU.subtract))
                link(dve.tensor_tensor(slot_g, slot_f, slot_g, ALU.add))
                link(dve.tensor_copy(slot_out, slot_f))
                link(dve.tensor_copy(slot_in, slot_g))
            else:
                link(dve.tensor_copy(slot_out[:, 0:NB], slot_f[:, 0:NB]))
                link(dve.tensor_copy(slot_in[:, 0:NB], slot_f[:, 0:NB]))
            assert done[0] == SLOTTED[f.layer], done[0]

        SLOTTED = {0: 38, 2: 30}
        compare = xin_free = score[:, 1, 512:512 + NE * NT]
        slot_all = score[:, 1, 512:1024]

        def back2_dve(dve):
            for q in range(4):
                before = 16 * NB if q < 2 else 0
                dve.wait_ge(loads.gathered[q], before + 16 * 8)
                for b in range(q * 8, q * 8 + 8):
                    dve.scalar_tensor_tensor(out=X[:, b, :], in0=tokens[:, b, :], scalar=gtop[:, 0, b:b + 1],
                                             in1=X[:, b, :], op0=ALU.mult, op1=ALU.add)

        N0 = SPARE // BANK

        def parity_in(s, j):
            return (s.in0, s.in1)[j % 2]

        def parity_out(s, j):
            return (s.out0, s.out1)[j % 2]

        def sorted0_sp(sp, f):
            s = f.s
            phase_start(sp, f.phase)
            sp.dma_start(b2all.rearrange("p (e d) -> p e d", e=NE), t["L0_b2"].partition_broadcast(P)).then_inc(f.load, 16)

            def weights(e, p):
                w = (s.w0, s.w1)[p]
                sp.dma_start(w1[:, p, 0:4 * P], row(t["L0_w1"], e)).then_inc(w, 16)
                sp.dma_start(w2[:, p, :, :], expert_w2(t["L0_w2"], e)).then_inc(w, 16)
                sp.dma_start(b1[:, p, :], row(t["L0_b1"], e)).then_inc(w, 16)

            def load(m, j):
                sp.dma_start(xin[:, j % 2, :].rearrange("p (t d) -> p t d", d=D),
                             slots_x[ds(m * BANK, BANK), :].rearrange("(t p) d -> p t d", p=P))\
                  .then_inc(parity_in(s, j), 16)

            sp.wait_ge(const.slots, 16 * FILLS)
            weights(0, 0)
            weights(1, 1)
            sp.wait_ge(loads.scattered, 16 * f.scatters)
            load(0, 0)
            load(1, 1)

            def step(m, j):
                if within(m, 0, N0 - 2):
                    sp.wait_ge(s.in_ps, m + 1)
                    load(m + 2, j)
                if within(m, 2, N0 + 2):
                    sp.wait_ge(s.y_sb, m - 1)
                    sp.dma_start(slots_y[ds((m - 2) * BANK, BANK), :].rearrange("(t p) d -> p t d", p=P),
                                 yout[:, j % 2, :].rearrange("p (t d) -> p t d", d=D)).then_inc(parity_out(s, j), 16)
                if j % 2 == 1 and within(m, 3, N0 - 2):
                    weights((m + 1) // 2 if isinstance(m, int) else (m - j) // 2 + (j + 1) // 2,
                            ((j + 1) // 2) % 2)

            steps(sp, step, N0 + 2, 4, 6, by=4)

        def sorted0_pe(pe, f):
            s = f.s
            sorted_front_pe(pe, f)
            attn_fold_pe(pe, attn[1])

            def turn(m, j):
                pe.wait_ge(parity_in(s, j), 8 * m + 16 - 8 * (j % 2))
                at_least(pe, s.in_sb, m)
                for i in range(4):
                    ins = pe.transpose(bank[0][:, i * P:(i + 1) * P], xin[:, j % 2, i * P:(i + 1) * P], ident[:, :])
                ins.then_inc(s.in_ps, 1)

            turn(0, 0)

            def step(n, j):
                u = j % 2
                if within(n, 0, N0):
                    p = j // 2
                    pe.wait_ge((s.w0, s.w1)[p], 12 * (n - j) + 48)
                    pe.wait_ge(s.in_sb, n + 1)
                    for c in range(4):
                        at_least(pe, s.h, 4 * (n - 1) + c + 1)
                        pe.matmul(bank[1 + c][:, :], w1[:, p, c * P:(c + 1) * P], xnT[:, u, :], start=True, stop=True)\
                          .then_inc(s.up_ps, 1)
                if within(n, 0, N0 - 1):
                    turn(n + 1, j + 1)
                if within(n, 1, N0 + 1):
                    p = ((j - 1) % 4) // 2
                    pe.wait_ge(s.h, 4 * n)
                    at_least(pe, s.y_sb, n - 2)
                    for i in range(4):
                        for c in range(4):
                            ins = pe.matmul(bank[6 - u][:, i * D:(i + 1) * D], hid[:, 1 - u, c, i * P:(i + 1) * P],
                                            w2[:, p, c, :], start=(c == 0), stop=(c == 3))
                    ins.then_inc(s.y_ps, 1)

            def stepped(n, j):
                step(n, j)

            steps(pe, stepped, N0 + 1, 4, 5, by=4)
            phase_end(pe)

        def sorted0_act(act, f):
            s = f.s
            sorted_front_act(act, f)
            attn_fold_act(act, attn[1])

            def turn(m, j):
                act.wait_ge(s.in_ps, m + 1)
                at_least(act, s.up_ps, 4 * (m - 1))
                nc.scalar.copy(xnT[:, j % 2, :], bank[0][:, :]).then_inc(s.in_sb, 1)

            turn(0, 0)

            def step(n, j):
                act.wait_ge((s.w0, s.w1)[j // 2], 12 * (n - j) + 48)
                at_least(act, s.y_ps, n - 1)
                for c in range(4):
                    act.wait_ge(s.up_ps, 4 * n + c + 1)
                    nc.scalar.activation(hid[:, j % 2, c, :], bank[1 + c][:, :], ACT.Relu,
                                         bias=b1[:, j // 2, c:c + 1]).then_inc(s.h, 1)
                if within(n, 0, N0 - 1):
                    turn(n + 1, j + 1)

            steps(act, step, N0, 4, 4, by=4)
            phase_end(act)

        def sorted0_pool(pool, f):
            sorted_front_pool(pool, f)
            all_stored(pool, f, N0 // 2, N0 // 2)
            phase_end(pool)

        def sorted0_dve(dve, f):
            s = f.s
            sorted_front_dve(dve, f)

            def step(m, j):
                dve.wait_ge(s.y_ps, m + 1)
                at_least(dve, parity_out(s, j), 8 * (m - j % 2))
                e = m // 2 if isinstance(m, int) else (m - j) // 2 + j // 2
                dve.tensor_tensor(yout[:, j % 2, :].rearrange("p (t d) -> p t d", d=D),
                                  bank[5 + j % 2][:, :].rearrange("p (t d) -> p t d", d=D),
                                  b2all[:, ds(e * D, D)].unsqueeze(1).to_broadcast([P, 4, D]), ALU.add)\
                   .then_inc(s.y_sb, 1)

            steps(dve, step, N0, 4, 4, by=4)
            phase_end(dve)

        def sorted2_sp(sp, f):
            s = f.s
            phase_start(sp, f.phase)
            sp.wait_ge(loads.scattered, 16 * f.scatters)

            def load(m, u):
                sp.dma_start(xin[:, u, 0:D], slots_x[ds(m * P, P), :]).then_inc(parity_in(s, u), 16)

            load(0, 0)
            load(1, 1)

            def step(m, u):
                if within(m, 0, NT - 2):
                    sp.wait_ge(s.in_ps, m + 1)
                    load(m + 2, u)
                if within(m, 2, NT + 2):
                    sp.wait_ge(s.y_sb, m - 1)
                    sp.dma_start(slots_y[ds((m - 2) * P, P), :], yout[:, u, 0:D]).then_inc(parity_out(s, u), 16)

            steps(sp, step, NT + 2, 2, 5)

        def sorted2_pe(pe, f):
            s = f.s
            sorted_front_pe(pe, f)
            up_w = w1all.rearrange("p (h n) -> p h n", n=BANK)
            down_w = fold[:, :].rearrange("p (q d) -> p q d", d=D)

            def turn(m, u):
                pe.wait_ge(parity_in(s, u), 8 * m + 16 - 8 * u)
                pe.transpose(bank[0][:, u * P:(u + 1) * P], xin[:, u, 0:D], ident[:, :]).then_inc(s.in_ps, 1)

            def expert(m):
                return pe.value_load(expert_of[0:1, ds(m, 1)], min_val=0, max_val=NE - 1)

            turn(0, 0)

            def step(n, u):
                if within(n, 0, NT):
                    e = expert(n)
                    pe.wait_ge(s.in_sb, n + 1)
                    at_least(pe, s.h, n - 1)
                    for half in (0, 1):
                        ins = pe.matmul(bank[1 + 2 * u + half][:, :], xnT[:, u, 0:P],
                                        up_w[:, ds(e * 2 + half, 1), :].rearrange("p a n -> p (a n)"),
                                        start=True, stop=True)
                    ins.then_inc(s.up_ps, 1)
                if within(n, 0, NT - 1):
                    turn(n + 1, 1 - u)
                if within(n, 1, NT + 1):
                    pe.wait_ge(s.h, n)
                    at_least(pe, s.ht_sb, n - 1)
                    for c in range(4):
                        ins = pe.transpose(bank[5][:, c * P:(c + 1) * P], hid[:, 1 - u, 0, c * P:(c + 1) * P],
                                           ident[:, :])
                    ins.then_inc(s.ht_ps, 1)
                if within(n, 2, NT + 2):
                    e = expert(n - 2)
                    pe.wait_ge(s.ht_sb, n - 1)
                    at_least(pe, s.y_sb, n - 3)
                    for c in range(4):
                        ins = pe.matmul(bank[6 + u][:, 0:D], hid[:, u, 1, c * P:(c + 1) * P],
                                        down_w[:, ds(e * 4 + c, 1), :].rearrange("p a n -> p (a n)"),
                                        start=(c == 0), stop=(c == 3))
                    ins.then_inc(s.y_ps, 1)

            steps(pe, step, NT + 2, 4, 3)
            phase_end(pe)

        def sorted2_act(act, f):
            s = f.s
            sorted_front_act(act, f)

            def turn(m, u):
                act.wait_ge(s.in_ps, m + 1)
                at_least(act, s.up_ps, m - 1)
                nc.scalar.copy(xnT[:, u, 0:P], bank[0][:, u * P:(u + 1) * P]).then_inc(s.in_sb, 1)

            turn(0, 0)

            def step(n, u):
                if within(n, 0, NT):
                    act.wait_ge(s.up_ps, n + 1)
                    at_least(act, s.h, n - 1)
                    nc.scalar.activation(hid[:, u, 2, :], bank[1 + 2 * u][:, :], ACT.Silu).then_inc(s.act, 1)
                if within(n, 0, NT - 1):
                    turn(n + 1, 1 - u)
                if within(n, 1, NT + 1):
                    act.wait_ge(s.ht_ps, n)
                    at_least(act, s.y_ps, n - 2)
                    nc.scalar.copy(hid[:, 1 - u, 1, :], bank[5][:, :]).then_inc(s.ht_sb, 1)

            steps(act, step, NT + 1, 4, 4)
            phase_end(act)

        def sorted2_pool(pool, f):
            sorted_front_pool(pool, f)
            context_stats_pool(pool, f.s)
            all_stored(pool, f, (NT + 1) // 2, NT // 2)
            phase_end(pool)

        def sorted2_dve(dve, f):
            s = f.s
            sorted_front_dve(dve, f)
            context_stats_dve(dve, s)

            def step(n, u):
                if within(n, 0, NT):
                    dve.wait_ge(s.act, n + 1)
                    at_least(dve, s.ht_ps, n - 1)
                    dve.tensor_tensor(hid[:, u, 0, :], bank[2 + 2 * u][:, :], hid[:, u, 2, :], ALU.mult)\
                       .then_inc(s.h, 1)
                if within(n, 2, NT + 2):
                    dve.wait_ge(s.y_ps, n - 1)
                    at_least(dve, parity_out(s, u), 8 * (n - 2 - u))
                    dve.tensor_copy(yout[:, u, 0:D], bank[6 + u][:, 0:D]).then_inc(s.y_sb, 1)

            steps(dve, step, NT + 2, 4, 3)
            phase_end(dve)

        def ffn_dve(dve, f):
            s, C, R = f.s, f.chunks, f.slots
            phase_start(dve, f.phase)
            dve.wait_ge(f.load, 16 * 2)
            if f.layer == 3:
                w1i, w2i = lay3.w1i, lay3.w2i
                dve.tensor_scalar(w1[:, 0, 0:768], w1i, 1.0 / 127.0, None, ALU.mult)
                dve.tensor_scalar(w2[:, 0, 0:3, :], w2i, 1.0 / 127.0, None, ALU.mult).then_inc(s.w0, 1)

            front_dve(dve, f)
            if f.ranks:
                softmax_and_choice(dve, f)
            if f.biased:
                def gate_group(n, u):
                    at_least(dve, s.gt_ps, n - 1)
                    dve.tensor_copy(gb[:, u, :], gates[:, ds(n * G, G), :].rearrange("p g e -> p (g e)"))\
                       .then_inc(s.gb, 1)

                gate_group(0, 0)
                gate_group(1, 1)

                def bias(n, u):
                    if within(n, 0, NG - 2):
                        gate_group(n + 2, u)
                    dve.wait_ge(s.bb_ps, n + 1)
                    x = X[:, ds(n * G, G), :]
                    dve.tensor_tensor(x, bank[3 + 3 * u][:, :].rearrange("p (g d) -> p g d", g=G), x, ALU.add)\
                       .then_inc(s.bb, 1)

                steps(dve, bias, NG, 2, 2)
                dve.wait_ge(s.bb, NG)
            dve.sem_inc(s.x, 2)
            if f.gated:
                dve.sem_inc(s.h, R)

            def expert(e, p, i):
                def step(g, u):
                    it = e * NG + g
                    if f.gated and within(g, 0, NG):
                        dve.wait_ge(s.y_ps, it + 1)
                        for c in range(C):
                            dve.wait_ge(s.act, it * C + c + 1)
                            dve.tensor_tensor(hid[:, u, c, :], up_bank(f, chunk_at(f, u, c), 1)[:, :],
                                              silu[:, c % 2 if C % 2 == 0 else (u + c) % 2, :], ALU.mult)\
                               .then_inc(s.h, 1)
                    if within(g, 1, NG + 1):
                        y = bank[6 + (1 - u)][:, :].rearrange("p (g d) -> p g d", g=G)
                        dve.wait_ge(s.y_ps, it + 2)
                        dve.wait_ge(s.x, it + 1)
                        if f.ranks:
                            for i in range(G):
                                x = tile((g - 1) * G + i)
                                gate = gate_of[:, ds(((g - 1) * G + i) * NE + e, 1)]
                                ins = dve.scalar_tensor_tensor(out=x, in0=y[:, i, :], scalar=gate, in1=x, op0=ALU.mult, op1=ALU.add)
                        else:
                            x = X[:, ds((g - 1) * G, G), :]
                            ins = dve.tensor_tensor(x, y, x, ALU.add)
                        ins.then_inc(s.x, 1)

                steps(dve, step, NG + 1, 2, 1)

            over_experts(dve, f, expert)
            phase_end(dve)

        attn = [Attention(0, 0, 8), Attention(1, 2, 16)]
        ffn = [Ffn(0, 1, NE, 4, ACT.Relu, False, 2, True, True),
               Ffn(1, 3, NE, 1, ACT.Gelu_apprx_tanh, False, 2, True, True),
               Ffn(2, 5, NE, 4, ACT.Silu, True, 1, True, False),
               Ffn(3, 8, 1, 3, ACT.Silu, True, 0, False, False)]

        class lay3:
            w1i = raw[:, 9216:9984].bitcast(I32)
            w2i = raw[:, 9984:10368].bitcast(I32).rearrange("p (c d) -> p c d", c=3)

        def row(ap, e):
            return ap[ds(e, 1)].rearrange("a p n -> (a p) n")

        def expert_w2(ap, e):
            return ap[ds(e, 1)].rearrange("a p c d -> (a p) c d")

        def small():
            sp = nc.sync
            for i in range(3):
                q = f"L{i}_"
                sp.dma_start(obias[:, i, :], t[q + "bo"].partition_broadcast(P)).then_inc(const.bias, 16)
            for i in range(2):
                sp.dma_start(wr[:, i, :], t[f"L{i}_wr"]).then_inc(ffn[i].load, 16)
                sp.dma_start(b2[:, i, :], t[f"L{i}_b2"]).then_inc(ffn[i].load, 16)
            sp.dma_start(wr[:, 2, :], t["L2_wr"]).then_inc(loads.ffn2, 16)
            sp.dma_start(rb[:, :], t["L2_rb"].partition_broadcast(P)).then_inc(loads.ffn2, 16)
            sp.dma_start(l2w[:, 0, :], t["L2_wq"]).then_inc(loads.l2, 16)
            sp.dma_start(l2w[0:DC, 1, :], t["L2_wk"]).then_inc(loads.l2, 16)
            sp.dma_start(l2w[0:DC, 2, :], t["L2_wv"]).then_inc(loads.l2, 16)
            sp.dma_start(l2b[:, 0:1], t["L2_bq"]).then_inc(loads.l2, 16)
            sp.dma_start(l2b[:, 1:2], t["L2_bk"]).then_inc(loads.l2, 16)
            for i, name in enumerate(("ln_x_g", "ln_x_b")):
                sp.dma_start(l3g[0:DC, i:i + 1], t["L3_" + name]).then_inc(loads.l3, 16)
            for i, name in enumerate(("ln_l_g", "ln_l_b", "qn_g")):
                sp.dma_start(l3g[:, 2 + i:3 + i], t["L3_" + name]).then_inc(loads.l3, 16)
            sp.dma_start(l3g[:, 6:7], t["L3_kn_g"]).then_inc(loads.l3, 16)
            sp.dma_start(l3w[:, 0:384], t["L3_wl"]).then_inc(loads.l3, 16)
            sp.dma_start(l3w[0:DC, 384:640], t["L3_wkv"]).then_inc(loads.l3, 16)
            sp.dma_start(l3w[:, 640:768], t["L3_wo"]).then_inc(loads.l3, 16)
            sp.dma_start(l3bo[:, :], t["L3_bo"].partition_broadcast(P)).then_inc(const.bias, 16)

        block = ctx.enter_context(nc.Block())

        @block.sync
        def _(sp):
            sp.dma_start(X[:, 0:FIRST, :], t["x"][0:FIRST].rearrange("b s d -> s b d")).then_inc(loads.first, 16)
            for a in attn:
                q = f"L{a.layer}_"
                sp.dma_start(a.wqT, t[q + "wqT"]).then_inc(a.load, 16)
                sp.dma_start(a.wkT, t[q + "wkT"]).then_inc(a.load, 16)
                sp.dma_start(a.wvT, t[q + "wvT"]).then_inc(a.load, 16)
                sp.dma_start(a.woh, t[q + "wo"]).then_inc(a.load, 16)
                if a.layer == 0:
                    sp.dma_start(ctxT[:, :], t["ctxT"]).then_inc(loads.ctx, 16)
                    sp.dma_start(X[:, FIRST:, :], t["x"][FIRST:].rearrange("b s d -> s b d")).then_inc(loads.x, 16)
                    small()
            sp.wait_ge(const.cleared, 1)
            for i in range(FILLS):
                sp.dma_start(slots_x[i * 16 * P:(i + 1) * 16 * P, :].rearrange("(p r) d -> p (r d)", p=P),
                             w1[:, :, :].rearrange("p a b -> p (a b)")).then_inc(const.slots, 16)
            sorted0_sp(sp, ffn[0])
            phase_start(sp, ffn[1].phase)
            sp.dma_start(w1all.rearrange("p (e n) -> p e n", e=NE), t["L2_w1"].rearrange("e p n -> p e n"))\
              .then_inc(loads.ffn2, 16)
            sp.dma_start(fold[:, :].rearrange("p (e c d) -> p e c d", e=NE, c=4), t["L2_w2"].rearrange("e p c d -> p e c d"))\
              .then_inc(loads.ffn2, 16)
            ffn_sp(sp, ffn[1], lambda e: row(t["L1_w1"], e), lambda e: expert_w2(t["L1_w2"], e),
                   lambda e: row(t["L1_b1"], e))
            phase_start(sp, ffn[2].phase)
            sp.dma_start(ctxn, t["ctx"].rearrange("b s c -> s b c")).then_inc(loads.ctxn, 16)
            sp.dma_start(mask8[:, :], t["mask"].partition_broadcast(P)).then_inc(loads.ctxn, 16)
            sp.dma_start(lay3.w1i, t["L3_w1"]).then_inc(loads.ffn3, 16)
            sp.dma_start(lay3.w2i, t["L3_w2"]).then_inc(loads.ffn3, 16)
            sorted2_sp(sp, ffn[2])
            phase_start(sp, ffn[3].phase)
            for q in range(4):
                sp.wait_ge(ffn[3].s.x, 2 + (q + 1) * NG // 4)
                seqs = slice(q * NB // 4, (q + 1) * NB // 4)
                sp.dma_start(out[seqs].rearrange("b s d -> s b d"), X[:, seqs, :]).then_inc(loads.out, 16)
            sp.wait_ge(loads.out, 16 * 4)

        @block.gpsimd
        def _(pool):
            pool.memset(w1[:, :, :], 0.0).then_inc(const.cleared, 1)
            pool.memset(mhalf[:, :], -0.5).then_inc(const.zero, 1)
            pool.memset(ones[:, :], 1.0).then_inc(const.zero, 1)
            pool.memset(epss[:, :], EPS).then_inc(const.zero, 1)
            pool.memset(first[:, :], 1.0).then_inc(const.zero, 1)
            pool.memset(ident[:, :], 0.0).then_inc(const.zero, 1)
            pool.wait_ge(const.zero, 5)
            pool.affine_select(out=ident[:, :], in_=ident[:, :], compare_op=ALU.not_equal, fill=1.0, base=0,
                               pattern=[[-1, P]], channel_multiplier=1).then_inc(const.ready, 1)
            pool.affine_select(out=upper[:, :], in_=ones[:, :], compare_op=ALU.is_ge, fill=0.0, base=0,
                               pattern=[[1, P]], channel_multiplier=-1).then_inc(const.ready, 1)
            pool.memset(first[:, :].rearrange("p (e n) -> p e n", e=NE)[:, :, 0:1], 0.0).then_inc(const.ready, 1)
            for e in range(NE):
                pool.memset(order[:, e:e + 1], float(NE - e)).then_inc(const.order, 1)
            attn_pool(pool, attn[0])
            sorted0_pool(pool, ffn[0])
            attn_pool(pool, attn[1])
            ffn_pool(pool, ffn[1])
            attn2_pool(pool)
            sorted2_pool(pool, ffn[2])
            ctx3_pool(pool)
            attn3_pool(pool)
            ffn_pool(pool, ffn[3])

        @block.scalar
        def _(act):
            attn_act(act, attn[0])
            sorted0_act(act, ffn[0])
            attn_act(act, attn[1])
            ffn_act(act, ffn[1])
            attn2_act(act)
            sorted2_act(act, ffn[2])
            ctx3_act(act)
            attn3_act(act)
            ffn_act(act, ffn[3])

        @block.vector
        def _(dve):
            dve.wait_ge(const.ready, 3)
            dve.wait_ge(const.order, NE)
            attn_dve(dve, attn[0])
            sorted0_dve(dve, ffn[0])
            attn_dve(dve, attn[1])
            ffn_dve(dve, ffn[1])
            attn2_dve(dve)
            sorted2_dve(dve, ffn[2])
            ctx3_dve(dve)
            attn3_dve(dve)
            ffn_dve(dve, ffn[3])

        @block.tensor
        def _(pe):
            attn_pe(pe, attn[0])
            sorted0_pe(pe, ffn[0])
            attn_pe(pe, attn[1])
            ffn_pe(pe, ffn[1])
            attn2_pe(pe)
            sorted2_pe(pe, ffn[2])
            ctx3_pe(pe)
            attn3_pe(pe)
            ffn_pe(pe, ffn[3])


_OUT = (NB, P, D)


def kernel(**inputs):
    import numpy as np
    import concourse.bacc as bacc
    from concourse.bass_utils import run_bass_kernel_spmd as run

    a = {k: np.asarray(v) for k, v in inputs.items()}

    def heads(w):
        return w.reshape(w.shape[0], -1, HD).transpose(2, 1, 0)

    def second(w):
        return w.reshape(w.shape[0], -1, P, D).transpose(0, 2, 1, 3)

    def hidden_bias(b):
        return b.reshape(b.shape[0], -1, P).transpose(0, 2, 1)

    arrays = {
        "x": a["x"], "ctx": a["ctx_768"],
        "ctxT": a["ctx_768"].transpose(2, 0, 1).reshape(DC, NB * S2),
        "mask": a["mask_BxS2_bk0"].reshape(NB * S2),
        "L0_w1": a["L0_ffn_w1"], "L0_w2": second(a["L0_ffn_w2"]), "L0_b1": hidden_bias(a["L0_ffn_b1"]),
        "L0_b2": a["L0_ffn_b2"], "L0_wr": a["L0_ffn_wg"],
        "L1_w1": a["L1_ffn_w_in"], "L1_w2": second(a["L1_ffn_w_out"]), "L1_b1": hidden_bias(a["L1_ffn_b_in"]),
        "L1_b2": a["L1_ffn_b_out"], "L1_wr": a["L1_ffn_router_w"],
        "L2_w1": a["L2_ffn_w1"], "L2_w2": second(a["L2_ffn_w2"]), "L2_wr": a["L2_ffn_router_w"],
        "L2_rb": a["L2_ffn_router_b"],
        "L2_wq": a["L2_xattn_Wq"], "L2_wk": a["L2_xattn_Wk"], "L2_wv": a["L2_xattn_Wv"],
        "L2_bq": a["L2_xattn_bq"].reshape(D, 1), "L2_bk": a["L2_xattn_bk"].reshape(D, 1),
        "L2_bo": a["L2_xattn_bv"],
        "L3_ln_x_g": a["L3_xattn_ln_x_g"].reshape(DC, 1), "L3_ln_x_b": a["L3_xattn_ln_x_b"].reshape(DC, 1),
        "L3_ln_l_g": a["L3_xattn_ln_l_g"].reshape(D, 1), "L3_ln_l_b": a["L3_xattn_ln_l_b"].reshape(D, 1),
        "L3_qn_g": np.tile(a["L3_xattn_qn_g"], 2).reshape(D, 1),
        "L3_kn_g": np.tile(a["L3_xattn_kn_g"], 2).reshape(D, 1),
        "L3_wl": np.concatenate([a["L3_xattn_Wq"], a["L3_xattn_Wlkv"]], 0).T,
        "L3_wkv": a["L3_xattn_Wkv"].T, "L3_wo": a["L3_xattn_Wo"].T, "L3_bo": a["L3_xattn_bo"],
        "L3_w1": np.concatenate([a["L3_ffn_w_gate"], a["L3_ffn_w_up"]], 0).T,
        "L3_w2": a["L3_ffn_w_down"].T.reshape(3, P, D).transpose(1, 0, 2),
    }
    for i in (0, 1):
        q = f"L{i}_xattn_"
        arrays |= {f"L{i}_wqT": heads(a[q + "Wq"]), f"L{i}_wkT": heads(a[q + "Wk"]), f"L{i}_wvT": heads(a[q + "Wv"]),
                   f"L{i}_wo": a[q + "Wo"].reshape(-1, HD, D).transpose(1, 0, 2), f"L{i}_bo": a[q + "bo"]}
    arrays = {k: np.ascontiguousarray(v) for k, v in arrays.items()}

    nc = bacc.Bacc("TRN2", target_bir_lowering=False, num_devices=1)
    t = {k: nc.dram_tensor("in_" + k, v.shape, mybir.dt.from_np(v.dtype), kind="ExternalInput").ap()
         for k, v in arrays.items()}
    out = nc.dram_tensor("out_dram", _OUT, F32, kind="ExternalOutput").ap()
    build(nc, t, out)
    return run(nc, [{"in_" + k: v for k, v in arrays.items()}], core_ids=[0]).results[0]["out_dram"]
```
